# Optimizing a Trainium2 kernel written in Bass

```python
import numpy as np
import jax
import jax.numpy as jnp

def _softmax(x, axis=-1):
    return jax.nn.softmax(x, axis=axis)

def _gelu(x):
    return jax.nn.gelu(x, approximate=True)

def _silu(x):
    return jax.nn.silu(x)

def _sigmoid(x):
    return jax.nn.sigmoid(x)

def _layernorm(x, axis=-1, eps=1e-05):
    m = jnp.mean(x, axis=axis, keepdims=True)
    v = jnp.var(x, axis=axis, keepdims=True)
    return (x - m) / jnp.sqrt(v + eps)

def _scatter_add(tgt, idx, src, axis=0):
    return tgt.at[idx].add(src)

def _segment_sum(src, seg, n):
    return jax.ops.segment_sum(src, seg, n)
kernel_name = 'mk_perceiver_d1_seqx_r4_b12dae'

def setup_inputs(seed: int=0):
    np.random.seed(seed)
    _w = jnp.asarray

    def _rec_inputs():
        import jax
        import jax.numpy as jnp
        _rk = jax.random.key(seed)
        x = -0.0003929 + 0.9999 * jax.random.normal(jax.random.fold_in(_rk, 1), (64, 32, 256), jnp.float32)
        _lenS = 32 - jax.random.randint(jax.random.fold_in(_rk, 7), (64,), 0, max(1, 32 // 4) + 1, jnp.int32)
        _lenS2 = 257 - jax.random.randint(jax.random.fold_in(_rk, 8), (64,), 0, max(1, 257 // 4) + 1, jnp.int32)
        _ctx_1024P = jax.random.normal(jax.random.fold_in(_rk, 11), (64, 16, 256), jnp.float32)
        _ctx_1024c = jax.random.dirichlet(jax.random.fold_in(_rk, 511), 0.3 * jnp.ones((16,), jnp.float32), (64, 257))
        _ctx_1024t = jnp.einsum('bsk,bkd->bsd', _ctx_1024c, _ctx_1024P)
        _ctx_1024t = _ctx_1024t * jax.lax.rsqrt(jnp.mean(jnp.square(_ctx_1024t)) + 1e-12) * 0.953939
        ctx_1024 = 0.00191187 + 0.999416 * (_ctx_1024t + 0.3 * jax.random.normal(jax.random.fold_in(_rk, 611), (64, 257, 256), jnp.float32))
        return (x, ctx_1024)
    x, ctx_1024 = _rec_inputs()

    def _L0_xattn_setup():
        import jax, jax.numpy as jnp
        import numpy as np
        B, S, P, H, R = (4, 1024, 64, 256, 8)
        SCALING = 16.0 / R

        def _lora_linear(x, W, b, A, Bm):
            return x @ W.T + b + x @ A.T @ Bm.T * SCALING
        key = jax.random.key(seed)
        ks = jax.random.split(key, 20)
        d = {'hidden_states': jax.random.normal(ks[0], (B, S, H), jnp.float32), 'past_key': jax.random.normal(ks[1], (B, P, H), jnp.float32), 'past_value': jax.random.normal(ks[2], (B, P, H), jnp.float32)}
        i = 3
        for name in ('q', 'k', 'v', 'o'):
            d[f'W{name}'] = jax.random.normal(ks[i], (H, H), jnp.float32) * (1.0 / np.sqrt(H))
            i += 1
            d[f'b{name}'] = jax.random.normal(ks[i], (H,), jnp.float32) * 0.01
            i += 1
            d[f'A{name}'] = jax.random.normal(ks[i], (R, H), jnp.float32) * 0.02
            i += 1
            d[f'B{name}'] = jax.random.normal(ks[i], (H, R), jnp.float32) * 0.02
            i += 1
        return d
    _L0_xattn_all = _L0_xattn_setup()
    _L0_xattn_in = {k: v for k, v in _L0_xattn_all.items() if k in ('Wq', 'bq', 'Aq', 'Bq', 'Wk', 'bk', 'Ak', 'Bk', 'Wv', 'bv', 'Av', 'Bv', 'Wo', 'bo', 'Ao', 'Bo')}
    del _L0_xattn_all

    def _L0_attn_setup():
        import jax, jax.numpy as jnp
        import numpy as np

        def _ln(x, g, b):
            m = x.mean(-1, keepdims=True)
            v = x.var(-1, keepdims=True)
            return (x - m) * jax.lax.rsqrt(v + 1e-05) * g + b

        def _shift(x):
            return jnp.pad(x, ((0, 0), (1, 0), (0, 0)))[:, :-1]
        key = jax.random.key(seed)
        ks = jax.random.split(key, 20)
        B, S, D, E, F = (2, 512, 256, 8, 512)
        s = 0.02
        return dict(x=jax.random.normal(ks[0], (B, S, D), jnp.float32), ln1_g=jnp.ones((D,), jnp.float32), ln1_b=jnp.zeros((D,), jnp.float32), ln2_g=jnp.ones((D,), jnp.float32), ln2_b=jnp.zeros((D,), jnp.float32), tm_mu_k=jax.random.uniform(ks[1], (D,), jnp.float32), tm_mu_v=jax.random.uniform(ks[2], (D,), jnp.float32), tm_mu_r=jax.random.uniform(ks[3], (D,), jnp.float32), time_decay=jax.random.normal(ks[4], (D,), jnp.float32) * 0.1, time_first=jax.random.normal(ks[5], (D,), jnp.float32) * 0.1, Wk=jax.random.normal(ks[6], (D, D), jnp.float32) * s, Wv=jax.random.normal(ks[7], (D, D), jnp.float32) * s, Wr=jax.random.normal(ks[8], (D, D), jnp.float32) * s, Wo=jax.random.normal(ks[9], (D, D), jnp.float32) * s, router_w=jax.random.normal(ks[10], (D, E), jnp.float32) * s, cm_mu_k=jax.random.uniform(ks[11], (E, D), jnp.float32), cm_mu_r=jax.random.uniform(ks[12], (E, D), jnp.float32), eWk=jax.random.normal(ks[13], (E, D, F), jnp.float32) * s, eWv=jax.random.normal(ks[14], (E, F, D), jnp.float32) * s, eWr=jax.random.normal(ks[15], (E, D, D), jnp.float32) * s)
    _L0_attn_all = _L0_attn_setup()
    _L0_attn_in = {k: v for k, v in _L0_attn_all.items() if k in ('ln1_g', 'ln1_b', 'ln2_g', 'ln2_b', 'tm_mu_k', 'tm_mu_v', 'tm_mu_r', 'time_decay', 'time_first', 'Wk', 'Wv', 'Wr', 'Wo', 'router_w', 'cm_mu_k', 'cm_mu_r', 'eWk', 'eWv', 'eWr')}
    del _L0_attn_all

    def _L0_ffn_setup():
        import jax, jax.numpy as jnp
        import numpy as np
        HIDDEN = 256
        INTER = 1024
        N_EXPERTS = 8

        def geglu(x, w1, w2, w3):
            return jax.nn.gelu(x @ w1, approximate=False) * (x @ w2) @ w3
        key = jax.random.key(seed)
        ks = jax.random.split(key, 8)
        s = 0.02
        x = jax.random.normal(ks[0], (2, 512, HIDDEN), dtype=jnp.float32)
        w1s = jax.random.normal(ks[1], (HIDDEN, INTER), dtype=jnp.float32) * s
        w2s = jax.random.normal(ks[2], (HIDDEN, INTER), dtype=jnp.float32) * s
        w3s = jax.random.normal(ks[3], (INTER, HIDDEN), dtype=jnp.float32) * s
        W1 = jax.random.normal(ks[4], (N_EXPERTS, HIDDEN, INTER), dtype=jnp.float32) * s
        W2 = jax.random.normal(ks[5], (N_EXPERTS, HIDDEN, INTER), dtype=jnp.float32) * s
        W3 = jax.random.normal(ks[6], (N_EXPERTS, INTER, HIDDEN), dtype=jnp.float32) * s
        Wg = jax.random.normal(ks[7], (HIDDEN, N_EXPERTS), dtype=jnp.float32) * s
        return {'x': x, 'w1s': w1s, 'w2s': w2s, 'w3s': w3s, 'W1': W1, 'W2': W2, 'W3': W3, 'Wg': Wg}
    _L0_ffn_all = _L0_ffn_setup()
    _L0_ffn_in = {k: v for k, v in _L0_ffn_all.items() if k in ('w1s', 'w2s', 'w3s', 'W1', 'W2', 'W3', 'Wg')}
    del _L0_ffn_all
    return {'x': x, 'ctx_1024': ctx_1024, 'L0_xattn_Wq': _L0_xattn_in['Wq'], 'L0_xattn_bq': _L0_xattn_in['bq'], 'L0_xattn_Aq': _L0_xattn_in['Aq'], 'L0_xattn_Bq': _L0_xattn_in['Bq'], 'L0_xattn_Wk': _L0_xattn_in['Wk'], 'L0_xattn_bk': _L0_xattn_in['bk'], 'L0_xattn_Ak': _L0_xattn_in['Ak'], 'L0_xattn_Bk': _L0_xattn_in['Bk'], 'L0_xattn_Wv': _L0_xattn_in['Wv'], 'L0_xattn_bv': _L0_xattn_in['bv'], 'L0_xattn_Av': _L0_xattn_in['Av'], 'L0_xattn_Bv': _L0_xattn_in['Bv'], 'L0_xattn_Wo': _L0_xattn_in['Wo'], 'L0_xattn_bo': _L0_xattn_in['bo'], 'L0_xattn_Ao': _L0_xattn_in['Ao'], 'L0_xattn_Bo': _L0_xattn_in['Bo'], 'L0_attn_ln1_g': _L0_attn_in['ln1_g'], 'L0_attn_ln1_b': _L0_attn_in['ln1_b'], 'L0_attn_ln2_g': _L0_attn_in['ln2_g'], 'L0_attn_ln2_b': _L0_attn_in['ln2_b'], 'L0_attn_tm_mu_k': _L0_attn_in['tm_mu_k'], 'L0_attn_tm_mu_v': _L0_attn_in['tm_mu_v'], 'L0_attn_tm_mu_r': _L0_attn_in['tm_mu_r'], 'L0_attn_time_decay': _L0_attn_in['time_decay'], 'L0_attn_time_first': _L0_attn_in['time_first'], 'L0_attn_Wk': _L0_attn_in['Wk'], 'L0_attn_Wv': _L0_attn_in['Wv'], 'L0_attn_Wr': _L0_attn_in['Wr'], 'L0_attn_Wo': _L0_attn_in['Wo'], 'L0_attn_router_w': _L0_attn_in['router_w'], 'L0_attn_cm_mu_k': _L0_attn_in['cm_mu_k'], 'L0_attn_cm_mu_r': _L0_attn_in['cm_mu_r'], 'L0_attn_eWk': _L0_attn_in['eWk'], 'L0_attn_eWv': _L0_attn_in['eWv'], 'L0_attn_eWr': _L0_attn_in['eWr'], 'L0_ffn_w1s': _L0_ffn_in['w1s'], 'L0_ffn_w2s': _L0_ffn_in['w2s'], 'L0_ffn_w3s': _L0_ffn_in['w3s'], 'L0_ffn_W1': _L0_ffn_in['W1'], 'L0_ffn_W2': _L0_ffn_in['W2'], 'L0_ffn_W3': _L0_ffn_in['W3'], 'L0_ffn_Wg': _L0_ffn_in['Wg']}

def reference(x, ctx_1024, L0_xattn_Wq, L0_xattn_bq, L0_xattn_Aq, L0_xattn_Bq, L0_xattn_Wk, L0_xattn_bk, L0_xattn_Ak, L0_xattn_Bk, L0_xattn_Wv, L0_xattn_bv, L0_xattn_Av, L0_xattn_Bv, L0_xattn_Wo, L0_xattn_bo, L0_xattn_Ao, L0_xattn_Bo, L0_attn_ln1_g, L0_attn_ln1_b, L0_attn_ln2_g, L0_attn_ln2_b, L0_attn_tm_mu_k, L0_attn_tm_mu_v, L0_attn_tm_mu_r, L0_attn_time_decay, L0_attn_time_first, L0_attn_Wk, L0_attn_Wv, L0_attn_Wr, L0_attn_Wo, L0_attn_router_w, L0_attn_cm_mu_k, L0_attn_cm_mu_r, L0_attn_eWk, L0_attn_eWv, L0_attn_eWr, L0_ffn_w1s, L0_ffn_w2s, L0_ffn_w3s, L0_ffn_W1, L0_ffn_W2, L0_ffn_W3, L0_ffn_Wg):
    import jax
    import jax.numpy as jnp

    def _L0_xattn_ref(hidden_states, past_key, past_value, Wq, bq, Aq, Bq, Wk, bk, Ak, Bk, Wv, bv, Av, Bv, Wo, bo, Ao, Bo):
        import jax, jax.numpy as jnp
        import numpy as np
        B, S, P, H, R = (4, 1024, 64, 256, 8)
        SCALING = 16.0 / R

        def _lora_linear(x, W, b, A, Bm):
            return x @ W.T + b + x @ A.T @ Bm.T * SCALING
        q = _lora_linear(hidden_states, Wq, bq, Aq, Bq)
        k = _lora_linear(hidden_states, Wk, bk, Ak, Bk)
        v = _lora_linear(hidden_states, Wv, bv, Av, Bv)
        k = jnp.concatenate([past_key, k], axis=1)
        v = jnp.concatenate([past_value, v], axis=1)
        scores = jnp.einsum('bsh,bth->bst', q, k) / jnp.sqrt(jnp.float32(H))
        probs = jax.nn.softmax(scores, axis=-1)
        ctx = jnp.einsum('bst,bth->bsh', probs, v)
        return _lora_linear(ctx, Wo, bo, Ao, Bo)

    def _L0_attn_ref(x, ln1_g, ln1_b, ln2_g, ln2_b, tm_mu_k, tm_mu_v, tm_mu_r, time_decay, time_first, Wk, Wv, Wr, Wo, router_w, cm_mu_k, cm_mu_r, eWk, eWv, eWr):
        import jax, jax.numpy as jnp
        import numpy as np

        def _ln(x, g, b):
            m = x.mean(-1, keepdims=True)
            v = x.var(-1, keepdims=True)
            return (x - m) * jax.lax.rsqrt(v + 1e-05) * g + b

        def _shift(x):
            return jnp.pad(x, ((0, 0), (1, 0), (0, 0)))[:, :-1]
        TOP_K = 2
        E = router_w.shape[1]
        B, S, D = x.shape
        xn = _ln(x, ln1_g, ln1_b)
        xx = _shift(xn)
        xk = xn * tm_mu_k + xx * (1.0 - tm_mu_k)
        xv = xn * tm_mu_v + xx * (1.0 - tm_mu_v)
        xr = xn * tm_mu_r + xx * (1.0 - tm_mu_r)
        k = xk @ Wk
        v = xv @ Wv
        r = jax.nn.sigmoid(xr @ Wr)
        w = -jnp.exp(time_decay)
        u = time_first

        def step(carry, kv_t):
            aa, bb, pp = carry
            kt, vt = kv_t
            qq = jnp.maximum(pp, u + kt)
            e1 = jnp.exp(pp - qq)
            e2 = jnp.exp(u + kt - qq)
            wkv_t = (e1 * aa + e2 * vt) / (e1 * bb + e2)
            qq2 = jnp.maximum(pp + w, kt)
            e1b = jnp.exp(pp + w - qq2)
            e2b = jnp.exp(kt - qq2)
            return ((e1b * aa + e2b * vt, e1b * bb + e2b, qq2), wkv_t)
        init = (jnp.zeros((B, D), x.dtype), jnp.zeros((B, D), x.dtype), jnp.full((B, D), -1e+30, x.dtype))
        _, wkv = jax.lax.scan(step, init, (k.transpose(1, 0, 2), v.transpose(1, 0, 2)))
        wkv = wkv.transpose(1, 0, 2)
        x = x + r * wkv @ Wo
        ei = _ln(x, ln2_g, ln2_b)
        probs = jax.nn.softmax(ei @ router_w, axis=-1)
        vals, idx = jax.lax.top_k(probs, TOP_K)
        wts = vals / vals.sum(-1, keepdims=True)
        tw = jnp.sum(jax.nn.one_hot(idx, E, dtype=x.dtype) * wts[..., None], axis=-2)
        exx = _shift(ei)
        mk = cm_mu_k[:, None, None, :]
        mr = cm_mu_r[:, None, None, :]
        xk_e = ei[None] * mk + exx[None] * (1.0 - mk)
        xr_e = ei[None] * mr + exx[None] * (1.0 - mr)
        k_e = jnp.square(jax.nn.relu(jnp.einsum('ebsd,edf->ebsf', xk_e, eWk)))
        kv_e = jnp.einsum('ebsf,efd->ebsd', k_e, eWv)
        r_e = jax.nn.sigmoid(jnp.einsum('ebsd,edg->ebsg', xr_e, eWr))
        expert_out = r_e * kv_e
        moe = jnp.einsum('ebsd,bse->bsd', expert_out, tw)
        return x + moe

    def _L0_ffn_ref(x, w1s, w2s, w3s, W1, W2, W3, Wg):
        import jax, jax.numpy as jnp
        import numpy as np
        HIDDEN = 256
        INTER = 1024
        N_EXPERTS = 8

        def geglu(x, w1, w2, w3):
            return jax.nn.gelu(x @ w1, approximate=False) * (x @ w2) @ w3
        B, T, C = x.shape
        xf = x.reshape(-1, C)
        shared = geglu(xf, w1s, w2s, w3s)
        logits = xf @ Wg
        idx = jnp.argmax(logits, axis=-1)
        final = jnp.zeros_like(xf)
        for e in range(N_EXPERTS):
            y = geglu(xf, W1[e], W2[e], W3[e])
            final = final + jnp.where((idx == e)[:, None], y, 0.0)
        return (shared + final).reshape(B, T, C)
    x = x + _L0_xattn_ref(_layernorm(x, axis=-1), ctx_1024, ctx_1024, L0_xattn_Wq, L0_xattn_bq, L0_xattn_Aq, L0_xattn_Bq, L0_xattn_Wk, L0_xattn_bk, L0_xattn_Ak, L0_xattn_Bk, L0_xattn_Wv, L0_xattn_bv, L0_xattn_Av, L0_xattn_Bv, L0_xattn_Wo, L0_xattn_bo, L0_xattn_Ao, L0_xattn_Bo)
    x = x + _L0_attn_ref(_layernorm(x, axis=-1), L0_attn_ln1_g, L0_attn_ln1_b, L0_attn_ln2_g, L0_attn_ln2_b, L0_attn_tm_mu_k, L0_attn_tm_mu_v, L0_attn_tm_mu_r, L0_attn_time_decay, L0_attn_time_first, L0_attn_Wk, L0_attn_Wv, L0_attn_Wr, L0_attn_Wo, L0_attn_router_w, L0_attn_cm_mu_k, L0_attn_cm_mu_r, L0_attn_eWk, L0_attn_eWv, L0_attn_eWr)
    x = x + _L0_ffn_ref(_layernorm(x, axis=-1), L0_ffn_w1s, L0_ffn_w2s, L0_ffn_w3s, L0_ffn_W1, L0_ffn_W2, L0_ffn_W3, L0_ffn_Wg)
    return x

_drawn_inputs = setup_inputs


def setup_inputs(seed=0):
    import zlib

    import numpy as np

    out = dict(_drawn_inputs(seed))
    spreads = {'L0_attn_ln1_g': (1.0, 0.6),
     'L0_attn_ln1_b': (0.0, 0.8),
     'L0_attn_ln2_g': (1.0, 0.6),
     'L0_attn_ln2_b': (0.0, 0.8)}
    factors = {'L0_xattn_bq': 8.0,
     'L0_xattn_Aq': 8.0,
     'L0_xattn_Bq': 8.0,
     'L0_xattn_bk': 8.0,
     'L0_xattn_Ak': 8.0,
     'L0_xattn_Bk': 8.0,
     'L0_xattn_bv': 8.0,
     'L0_xattn_Av': 8.0,
     'L0_xattn_Bv': 8.0,
     'L0_xattn_bo': 5.918,
     'L0_xattn_Ao': 3.819,
     'L0_xattn_Bo': 3.724,
     'L0_attn_tm_mu_k': 8.0,
     'L0_attn_tm_mu_v': 8.0,
     'L0_attn_tm_mu_r': 8.0,
     'L0_attn_time_decay': 8.0,
     'L0_attn_time_first': 8.0,
     'L0_attn_Wk': 8.0,
     'L0_attn_Wv': 3.49,
     'L0_attn_Wr': 8.0,
     'L0_attn_Wo': 3.44,
     'L0_attn_router_w': 8.0,
     'L0_attn_cm_mu_k': 8.0,
     'L0_attn_cm_mu_r': 8.0,
     'L0_attn_eWk': 7.827,
     'L0_attn_eWv': 7.17,
     'L0_attn_eWr': 8.0,
     'L0_ffn_w1s': 27.792,
     'L0_ffn_w2s': 27.032,
     'L0_ffn_w3s': 27.136,
     'L0_ffn_W1': 27.632,
     'L0_ffn_W2': 26.992,
     'L0_ffn_W3': 26.96,
     'L0_ffn_Wg': 28.696}
    for name, (base, spread) in spreads.items():
        noise = np.random.default_rng([zlib.crc32(name.encode()), seed]).standard_normal(out[name].shape)
        drawn = base * np.exp(spread * noise) if base else spread * noise
        out[name] = jnp.asarray(drawn.astype(out[name].dtype))
    for name, factor in factors.items():
        out[name] = (out[name] * factor).astype(out[name].dtype)
    return out
```

```python
from contextlib import ExitStack

import concourse.bass as bass
from concourse import mybir

P = 128
F32 = mybir.dt.float32
I32 = mybir.dt.int32
U32 = mybir.dt.uint32
ALU = mybir.AluOpType
ACT = mybir.ActivationFunctionType
AX = mybir.AxisListType.X
EPS = 1e-5
LORA_SCALE = 2.0
NEG = -1e30
R_LOW = 80.0


class Step:

    def __init__(self, trip, offset, ring):
        self.trip, self.offset, self.ring = trip, offset, ring
        self.n = trip * ring + offset
        self.slot = offset % ring
        self.lap = trip + offset // ring

    def back(self, k, count):
        s = Step(self.trip, self.offset - k, self.ring)
        return s if not isinstance(s.n, int) or 0 <= s.n < count else None


def sweep(eng, total, peel, ring, body, tail):
    trips = (total - peel - tail) // ring
    for i in range(peel):
        body(Step(0, i, ring))
    with eng.Fori(0, trips) as trip:
        for b in range(ring):
            body(Step(trip, peel + b, ring))
    for i in range(peel + trips * ring, total):
        body(Step(0, i, ring))


def need(eng, sem, value):
    if not isinstance(value, int) or value > 0:
        eng.wait_ge(sem, value)


class Order:

    def __init__(self, eng, sem, per, step=0):
        self.eng, self.sem, self.per, self.step, self.k = eng, sem, per, step, 0

    def then(self, ins):
        ins.then_inc(self.sem, 1)
        self.k += 1

    def settle(self):
        self.eng.drain()

    def link(self, ins):
        self.then(ins)
        self.settle()

    def close(self):
        assert self.k == self.per, (self.k, self.per)


def perceiver_block(nc, x_in, ctx_in, Wq, bq, Aq, Bq, Wk, bk, Ak, Bk, Wv, bv, Av, Bv, Wo, bo, Ao, Bo,
                    ln1_g, ln1_b, ln2_g, ln2_b, mu_k, mu_v, mu_r, decay, first, tWk, tWv, tWr, tWo,
                    router_w, cm_mu_k, cm_mu_r, eWk, eWv, eWr, w1s, w2s, w3s, W1, W2, W3, Wg, out):
    BATCH, S, D = x_in.shape
    T = ctx_in.shape[1]
    KD = D // P
    G = BATCH * S // P
    BG = P // S
    TC = (T - 1) // P
    R = Aq.shape[0]
    E = eWk.shape[0]
    FK = eWk.shape[2]
    FKC = FK // P
    H = W1.shape[2]
    HC = H // P
    TOK = BATCH * S
    OWN = P + BG
    SP1 = S + 1
    PAD = KD * BG * SP1
    assert T == TC * P + 1 and TC == 2 and KD == 2 and BG == 4

    x_nat = x_in.rearrange("b s d -> (b s) d").rearrange("(c p) d -> p c d", p=P)
    out_nat = out.rearrange("b s d -> (b s) d").rearrange("(c p) d -> c p d", p=P)

    cx = ExitStack()
    with cx, nc.allow_non_contiguous_dma(reason="per-channel vectors, one element a partition"):
        def sb(name, shape, dt=F32, where=cx):
            return where.enter_context(nc.sbuf_tensor(name, shape, dt))

        def sem(name):
            return cx.enter_context(nc.semaphore(name))

        banks = [cx.enter_context(nc.psum_tensor(f"bank{i}", [P, 512], F32)) for i in range(8)]

        def col(v):
            return v.rearrange("(k p) -> p k", p=P)

        def row(v):
            return v.partition_broadcast(P)

        ident = sb("ident", [P, P])
        eps_pow = sb("eps_pow", [P, 1])
        x1 = sb("x1", [P, G, D])
        a_x2 = sb("a_x2", [P, G, D])
        xz = sb("xz", [P, G, D])
        iota_e = sb("iota_e", [P, E])
        iota_p = sb("iota_p", [P, P])
        tile_lo = sb("tile_lo", [P, G])
        token_id = sb("token_id", [P, G])
        before_m = sb("before_m", [P, P])
        ones_m = sb("ones_m", [P, P])
        chunk_on = sb("chunk_on", [P, E, G])
        logits2 = sb("logits2", [P, G, E])

        xs = ExitStack()
        with xs:
            def xb(name, shape, dt=F32):
                return sb(name, shape, dt, xs)
            w_nat = xb("w_nat", [P, 4, KD, D])
            w_T = xb("w_T", [P, 4, KD, D])
            lora_a = xb("lora_a", [R, 4, D])
            lora_b = xb("lora_b", [P, 4, KD, R])
            lora_bT = xb("lora_bT", [R, 4, KD, P])
            bq_c = xb("bq_c", [P, KD])
            bk_c = xb("bk_c", [P, KD])
            bv_b = xb("bv_b", [P, D])
            bo_b = xb("bo_b", [P, D])
            last_nat = xb("last_nat", [BATCH, D])
            last_T = xb("last_T", [P, KD, BATCH])
            v_last = xb("v_last", [BG, G, D])
            mask_l = xb("mask_l", [BG, P])
            mask_r = xb("mask_r", [BG, OWN])
            N3 = 3
            ctx_sb = xb("ctx_sb", [P, N3, BG, TC * D])
            kT = xb("kT", [P, N3, BG, KD * TC * P])
            hn = xb("hn", [P, N3, D])
            hnT = xb("hnT", [P, N3, KD, P])
            qT = xb("qT", [P, N3, KD, P])
            k_own = xb("k_own", [P, N3, KD, OWN])
            v_own = xb("v_own", [P, N3, D])
            vl = xb("vl", [BG, N3, D])
            prob = xb("prob", [P, N3, TC * P + OWN])
            probT = xb("probT", [P, N3, 4, P])
            oT = xb("oT", [P, N3, KD, P])
            st0 = xb("st0", [P, N3, 6])
            mv0 = xb("mv0", [P, N3, 2])
            var0 = xb("var0", [P, N3, 1])
            rs0 = xb("rs0", [P, N3, 1])
            st1 = xb("st1", [P, 2, N3, 6])
            mv1 = xb("mv1", [P, 2, N3, 2])
            var1 = xb("var1", [P, 2, N3, 1])
            rs1 = xb("rs1", [P, 2, N3, 1])
            smx = xb("smx", [P, N3, 1])
            snm = xb("snm", [P, N3, 1])
            ssum = xb("ssum", [P, N3, 1])
            srec = xb("srec", [P, N3, 1])

            bT0, bT1, bPT, bQ, bV, bS, bO, bW = banks
            ld_x, ld_w, ld_l, ld_lora, ld_b = (sem(n) for n in ("ld_x", "ld_w", "ld_l", "ld_lora", "ld_b"))
            ld_ctx = [sem(f"ld_ctx{i}") for i in range(N3)]
            const_ord = sem("const_ord")
            pe_set, dv_set = sem("pe_set"), sem("dv_set")
            pe_t0, pe_t1, pe_q, pe_v, pe_s, pe_pt, pe_o, pe_w = (sem(n) for n in (
                "pe_t0", "pe_t1", "pe_q", "pe_v", "pe_s", "pe_pt", "pe_o", "pe_w"))
            dv_t0, dv_v, dv_o, dv_w, dv_ln0, dv_ln1, dv_max, dv_norm = (sem(n) for n in (
                "dv_t0", "dv_v", "dv_o", "dv_w", "dv_ln0", "dv_ln1", "dv_max", "dv_norm"))
            ac_t1, ac_q, ac_exp, ac_pt = (sem(n) for n in ("ac_t1", "ac_q", "ac_exp", "ac_pt"))
            po_r0, po_r1, po_xb, po_last = (sem(n) for n in ("po_r0", "po_r1", "po_xb", "po_last"))
            CONSTS = 8
            STEPS = G + 3

            with nc.Block() as block:
                @block.sync
                def _(sp):
                    sp.dma_start(xz[:], x_nat).then_inc(ld_x, 16)
                    for i, w in enumerate((Wq, Wk, Wv, Wo)):
                        sp.dma_start(w_nat[:, i], w.rearrange("(k p) i -> p k i", p=P)).then_inc(ld_w, 16)
                    sp.dma_start(bv_b[:], row(bv)).then_inc(ld_w, 16)
                    sp.dma_start(bo_b[:], row(bo)).then_inc(ld_w, 16)
                    sp.dma_start(last_nat[:], ctx_in[:, T - 1, :]).then_inc(ld_l, 16)
                    sp.dma_start(v_last[:], ctx_in[:, T - 1, :].rearrange("(g j) d -> j g d", j=BG)).then_inc(ld_l, 16)

                    def load(s):
                        need(sp, pe_o, s.n - N3 + 1)
                        src = ctx_in[bass.ds(s.n * BG, BG), 0:TC * P, :].rearrange("j (p c) d -> p j (c d)", c=TC)
                        sp.dma_start(ctx_sb[:, s.slot], src).then_inc(ld_ctx[s.slot], 16)
                    sweep(sp, G, N3, N3, load, 0)

                @block.gpsimd
                def _(pool):
                    o = Order(pool, const_ord, CONSTS)
                    o.then(nc.gpsimd.memset(ident[:], 0.0))
                    o.then(nc.gpsimd.memset(mask_l[:], 0.0))
                    o.then(nc.gpsimd.memset(mask_r[:], NEG))
                    o.then(nc.gpsimd.memset(eps_pow[:], -0.5))
                    o.settle()
                    o.then(nc.gpsimd.affine_select(out=ident[:], in_=ident[:], compare_op=ALU.not_equal, fill=1.0,
                                                   base=0, pattern=[[-1, P]], channel_multiplier=1))
                    for m, n, f in ((mask_l[:], P, 1.0), (mask_r[:, 0:P], P, 0.0)):
                        v = m.rearrange("a (j s) -> a j s", j=BG)
                        o.then(nc.gpsimd.affine_select(out=v, in_=v, compare_op=ALU.not_equal, fill=f, base=0,
                                                       pattern=[[-1, BG], [0, S]], channel_multiplier=1))
                    v = mask_r[:, P:OWN]
                    o.then(nc.gpsimd.affine_select(out=v, in_=v, compare_op=ALU.not_equal, fill=0.0, base=0,
                                                   pattern=[[-1, BG]], channel_multiplier=1))
                    o.settle()
                    o.close()
                    pool.wait_ge(ld_w, 16 * 6)
                    pool.wait_ge(ld_l, 32)
                    pool.wait_ge(dv_set, 3)

                    def rstd0(s):
                        pool.wait_ge(dv_ln0, s.n * 4 + 3)
                        nc.gpsimd.tensor_tensor(rs0[:, s.slot], var0[:, s.slot], eps_pow[:], ALU.pow).then_inc(po_r0, 1)

                    def body(s):
                        if s.back(0, G):
                            if s.back(-1, G):
                                rstd0(s.back(-1, G))
                            need(pool, pe_s, s.n - N3 + 1)
                            nc.gpsimd.tensor_copy(k_own[:, s.slot, :, P:OWN], last_T[:, :, bass.ds(s.n * BG, BG)])
                            need(pool, pe_o, s.n - N3 + 1)
                            nc.gpsimd.tensor_copy(vl[:, s.slot], v_last[:, s.n]).then_inc(po_last, 1)
                            pool.wait_ge(dv_ln0, s.n * 4 + 4)
                            nc.gpsimd.tensor_tensor(xz[:, s.n], xz[:, s.n], bo_b[:], ALU.add).then_inc(po_xb, 1)
                        c = s.back(3, G)
                        if c:
                            for h in range(2):
                                pool.wait_ge(dv_ln1, c.n * 8 + 4 * h + 3)
                                nc.gpsimd.tensor_tensor(rs1[:, h, c.slot], var1[:, h, c.slot], eps_pow[:],
                                                        ALU.pow).then_inc(po_r1, 1)
                    rstd0(Step(0, 0, N3))
                    sweep(pool, STEPS, 4, N3, body, 4)

                @block.tensor
                def _(pe):
                    pe.wait_ge(const_ord, CONSTS)
                    pe.wait_ge(ld_w, 16 * 6)
                    pe.wait_ge(ld_lora, 16 * 8)
                    pe.wait_ge(ld_l, 32)
                    for i in range(4):
                        for k in range(KD):
                            nc.tensor.transpose(banks[i // 2][0:R, (i % 2 * KD + k) * P:(i % 2 * KD + k + 1) * P],
                                                lora_b[:, i, k], ident[:]).then_inc(pe_set, 1)
                    for k in range(KD):
                        nc.tensor.transpose(banks[2][:, k * BATCH:(k + 1) * BATCH], last_nat[:, k * P:(k + 1) * P],
                                            ident[0:BATCH, 0:BATCH]).then_inc(pe_set, 1)
                    pe.wait_ge(dv_set, 2)
                    for i in range(4):
                        for ki in range(KD):
                            for ko in range(KD):
                                o = banks[3 + i][:, ki * D + ko * P:ki * D + (ko + 1) * P]
                                nc.tensor.matmul(o, w_nat[:, i, ko, ki * P:(ki + 1) * P], ident[:], start=True, stop=False)
                                nc.tensor.matmul(o, lora_a[:, i, ki * P:(ki + 1) * P], lora_bT[:, i, ko],
                                                 start=False, stop=True).then_inc(pe_set, 1)
                    pe.wait_ge(dv_set, 7)

                    def part_a(s):
                        pe.wait_ge(dv_ln0, s.n * 4 + 4)
                        need(pe, dv_t0, s.n * 3)
                        for k in range(KD):
                            last = nc.tensor.transpose(bT0[:, k * P:(k + 1) * P], hn[:, s.slot, k * P:(k + 1) * P], ident[:])
                        last.then_inc(pe_t0, 1)
                        pe.wait_ge(ld_ctx[s.slot], s.lap * 16 + 16)
                        for j in range(BG):
                            if j % 2 == 0:
                                need(pe, ac_t1, s.n * 2 + j // 2)
                            else:
                                need(pe, dv_t0, s.n * 3 + 1 + j // 2)
                            for k in range(KD):
                                for c in range(TC):
                                    last = nc.tensor.transpose((bT1, bT0)[j % 2][:, (k * TC + c) * P:(k * TC + c + 1) * P],
                                                               ctx_sb[:, s.slot, j, c * D + k * P:c * D + (k + 1) * P],
                                                               ident[:])
                            last.then_inc((pe_t1, pe_t0)[j % 2], 1)

                    def qkv(s):
                        pe.wait_ge(dv_t0, s.n * 3 + 1)
                        need(pe, ac_q, s.n)
                        for i in range(2):
                            for m in range(KD):
                                for k in range(KD):
                                    last = nc.tensor.matmul(bQ[:, (i * KD + m) * P:(i * KD + m + 1) * P],
                                                            w_T[:, i, k, m * P:(m + 1) * P], hnT[:, s.slot, k],
                                                            start=k == 0, stop=k == KD - 1)
                        last.then_inc(pe_q, 1)
                        need(pe, dv_v, s.n)
                        for k in range(KD):
                            last = nc.tensor.matmul(bV[:, 0:D], hnT[:, s.slot, k], w_T[:, 2, k], start=k == 0, stop=k == KD - 1)
                        last.then_inc(pe_v, 1)

                    def scores(s):
                        pe.wait_ge(ac_q, s.n + 1)
                        pe.wait_ge(po_last, s.n + 1)
                        need(pe, ac_exp, s.n)
                        own = bS[:, TC * P:TC * P + OWN]
                        for k in range(KD):
                            nc.tensor.matmul(own, qT[:, s.slot, k], k_own[:, s.slot, k], start=k == 0, stop=False)
                        nc.tensor.matmul(own, mask_l[:], mask_r[:], start=False, stop=True)
                        pe.wait_ge(ac_t1, s.n * 2 + 2)
                        pe.wait_ge(dv_t0, s.n * 3 + 3)
                        for j in range(BG):
                            for k in range(KD):
                                last = nc.tensor.matmul(bS[j * S:(j + 1) * S, 0:TC * P], qT[:, s.slot, k, j * S:(j + 1) * S],
                                                        kT[:, s.slot, j, k * TC * P:(k + 1) * TC * P],
                                                        start=k == 0, stop=k == KD - 1)
                        last.then_inc(pe_s, 1)

                    def prob_T(s):
                        pe.wait_ge(dv_norm, s.n * 2 + 2)
                        need(pe, ac_pt, s.n)
                        for c in range(3):
                            nc.tensor.transpose(bPT[:, c * P:(c + 1) * P], prob[:, s.slot, c * P:(c + 1) * P], ident[:])
                        nc.tensor.transpose(bPT[0:BG, 3 * P:4 * P], prob[:, s.slot, 3 * P:3 * P + BG],
                                            ident[:]).then_inc(pe_pt, 1)

                    def values(s):
                        pe.wait_ge(ac_pt, s.n + 1)
                        pe.wait_ge(dv_v, s.n + 1)
                        need(pe, dv_o, s.n)
                        for k in range(KD):
                            o = bO[:, k * P:(k + 1) * P]
                            nc.tensor.matmul(o, v_own[:, s.slot, k * P:(k + 1) * P], probT[:, s.slot, 2], start=True, stop=False)
                            nc.tensor.matmul(o, vl[:, s.slot, k * P:(k + 1) * P], probT[0:BG, s.slot, 3], start=False, stop=False)
                            for j in range(BG):
                                for c in range(TC):
                                    last = nc.tensor.matmul(o[:, j * S:(j + 1) * S],
                                                            ctx_sb[:, s.slot, j, c * D + k * P:c * D + (k + 1) * P],
                                                            probT[:, s.slot, c, j * S:(j + 1) * S],
                                                            start=False, stop=j == BG - 1 and c == TC - 1)
                        last.then_inc(pe_o, 1)

                    def project(s):
                        pe.wait_ge(dv_o, s.n + 1)
                        need(pe, dv_w, s.n)
                        for k in range(KD):
                            last = nc.tensor.matmul(bW[:, 0:D], oT[:, s.slot, k], w_T[:, 3, k], start=k == 0, stop=k == KD - 1)
                        last.then_inc(pe_w, 1)

                    def body(s):
                        a, b, c = s.back(0, G), s.back(1, G), s.back(2, G)
                        if a:
                            part_a(a)
                        if c:
                            project(c)
                        if a:
                            qkv(a)
                        if b:
                            prob_T(b)
                        if a:
                            scores(a)
                        if b:
                            values(b)
                    sweep(pe, STEPS, 4, N3, body, 4)

                @block.scalar
                def _(act):
                    for i, w in enumerate((Aq, Ak, Av, Ao)):
                        act.dma_start(lora_a[:, i], w).then_inc(ld_lora, 16)
                    for i, w in enumerate((Bq, Bk, Bv, Bo)):
                        act.dma_start(lora_b[:, i], w.rearrange("(k p) r -> p k r", p=P)).then_inc(ld_lora, 16)
                    act.dma_start(bq_c[:], col(bq)).then_inc(ld_b, 16)
                    act.dma_start(bk_c[:], col(bk)).then_inc(ld_b, 16)
                    act.wait_ge(ld_b, 32)

                    def body(s):
                        a, b = s.back(0, G), s.back(1, G)
                        if a:
                            for j in (0, 2):
                                act.wait_ge(pe_t1, a.n * 2 + j // 2 + 1)
                                need(act, pe_s, a.n - N3 + 1)
                                nc.scalar.activation(kT[:, a.slot, j], bT1[:], ACT.Copy).then_inc(ac_t1, 1)
                            act.wait_ge(pe_q, a.n + 1)
                            for k in range(KD):
                                nc.scalar.activation(qT[:, a.slot, k], bQ[:, k * P:(k + 1) * P], ACT.Identity,
                                                     bias=bq_c[:, k:k + 1])
                                last = nc.scalar.activation(k_own[:, a.slot, k, 0:P], bQ[:, (KD + k) * P:(KD + k + 1) * P],
                                                            ACT.Identity, bias=bk_c[:, k:k + 1])
                            last.then_inc(ac_q, 1)
                        if b:
                            act.wait_ge(pe_pt, b.n + 1)
                            need(act, pe_o, b.n - N3 + 1)
                            nc.scalar.activation(probT[:, b.slot, 0:3], bPT[:, 0:3 * P], ACT.Copy)
                            nc.scalar.activation(probT[0:BG, b.slot, 3], bPT[0:BG, 3 * P:4 * P], ACT.Copy).then_inc(ac_pt, 1)
                        if a:
                            act.wait_ge(dv_max, a.n * 2 + 2)
                            need(act, pe_pt, a.n - N3 + 1)
                            nc.scalar.activation(prob[:, a.slot], bS[:, 0:TC * P + OWN], ACT.Exp, bias=snm[:, a.slot],
                                                 scale=float(D) ** -0.5, accum_out=ssum[:, a.slot]).then_inc(ac_exp, 1)
                    sweep(act, STEPS, 4, N3, body, 4)

                @block.vector
                def _(dve):
                    dve.wait_ge(pe_set, 8)
                    for i in range(2):
                        nc.vector.tensor_scalar(lora_bT[:, 2 * i:2 * i + 2].rearrange("r i k p -> r (i k p)"),
                                                banks[i][0:R, :], LORA_SCALE, None, ALU.mult).then_inc(dv_set, 1)
                    dve.wait_ge(pe_set, 10)
                    nc.vector.tensor_copy(last_T[:].rearrange("p k b -> p (k b)"), banks[2][:, 0:KD * BATCH]).then_inc(dv_set, 1)
                    for i in range(4):
                        dve.wait_ge(pe_set, 10 + 4 * (i + 1))
                        nc.vector.tensor_copy(w_T[:, i].rearrange("p k o -> p (k o)"), banks[3 + i][:]).then_inc(dv_set, 1)

                    def norm_stats(o, src, st, mv, var):
                        o.settle()
                        o.link(nc.vector.bn_stats(st, src))
                        o.link(nc.vector.bn_aggr(mv, st))
                        o.then(nc.vector.tensor_scalar(var, mv[:, 1:2], EPS, None, ALU.add))

                    def norm_apply(o, dst, src, mv, rstd):
                        o.then(nc.vector.tensor_scalar(dst, src, mv[:, 0:1], rstd, ALU.subtract, ALU.mult))

                    def ln0(s):
                        o = Order(dve, dv_ln0, 4, s.n)
                        norm_stats(o, xz[:, s.n], st0[:, s.slot], mv0[:, s.slot], var0[:, s.slot])
                        yield
                        dve.wait_ge(po_r0, s.n + 1)
                        need(dve, pe_t0, (s.n - N3) * 3 + 1)
                        norm_apply(o, hn[:, s.slot], xz[:, s.n], mv0[:, s.slot], rs0[:, s.slot])
                        o.close()
                        yield

                    def copy_T0(s, u, dst, n):
                        dve.wait_ge(pe_t0, s.n * 3 + u + 1)
                        nc.vector.tensor_copy(dst, bT0[:, 0:n]).then_inc(dv_t0, 1)

                    def body(s):
                        a, b, c, d = (s.back(k, G) for k in range(4))
                        n0 = ln0(s.back(-1, G)) if a and s.back(-1, G) else None
                        n1 = None
                        if a:
                            need(dve, pe_v, a.n - N3 + 1)
                            copy_T0(a, 0, hnT[:, a.slot].rearrange("p k t -> p (k t)"), KD * P)
                        if d:
                            n1 = Order(dve, dv_ln1, 8, d.n)
                            norm_stats(n1, x1[:, d.n], st1[:, 0, d.slot], mv1[:, 0, d.slot], var1[:, 0, d.slot])
                        if n0:
                            next(n0)
                        if a:
                            need(dve, pe_s, a.n - N3 + 1)
                            copy_T0(a, 1, kT[:, a.slot, 1], 512)
                        if d:
                            dve.wait_ge(po_r1, d.n * 2 + 1)
                            norm_apply(n1, a_x2[:, d.n], x1[:, d.n], mv1[:, 0, d.slot], rs1[:, 0, d.slot])
                            norm_stats(n1, a_x2[:, d.n], st1[:, 1, d.slot], mv1[:, 1, d.slot], var1[:, 1, d.slot])
                        if n0:
                            next(n0)
                        if a:
                            copy_T0(a, 2, kT[:, a.slot, 3], 512)
                        if d:
                            dve.wait_ge(po_r1, d.n * 2 + 2)
                            norm_apply(n1, xz[:, d.n], a_x2[:, d.n], mv1[:, 1, d.slot], rs1[:, 1, d.slot])
                            n1.close()
                        if c:
                            dve.wait_ge(pe_w, c.n + 1)
                            dve.wait_ge(po_xb, c.n + 1)
                            nc.vector.tensor_tensor(x1[:, c.n], bW[:, 0:D], xz[:, c.n], ALU.add).then_inc(dv_w, 1)
                        if a:
                            dve.wait_ge(pe_v, a.n + 1)
                            need(dve, pe_o, a.n - N3 + 1)
                            nc.vector.tensor_tensor(v_own[:, a.slot], bV[:, 0:D], bv_b[:], ALU.add).then_inc(dv_v, 1)
                            o = Order(dve, dv_max, 2, a.n)
                            dve.wait_ge(pe_s, a.n + 1)
                            o.link(nc.vector.reduce_max(smx[:, a.slot], bS[:, 0:TC * P + OWN], AX))
                            o.then(nc.vector.tensor_scalar(snm[:, a.slot], smx[:, a.slot], -float(D) ** -0.5, None, ALU.mult))
                        if b:
                            dve.wait_ge(pe_o, b.n + 1)
                            need(dve, pe_w, b.n - N3 + 1)
                            nc.vector.tensor_copy(oT[:, b.slot].rearrange("p k t -> p (k t)"), bO[:, 0:KD * P]).then_inc(dv_o, 1)
                        if a:
                            o = Order(dve, dv_norm, 2, a.n)
                            dve.wait_ge(ac_exp, a.n + 1)
                            o.link(nc.vector.reciprocal(srec[:, a.slot], ssum[:, a.slot]))
                            o.then(nc.vector.tensor_scalar(prob[:, a.slot], prob[:, a.slot], srec[:, a.slot], None, ALU.mult))
                    dve.wait_ge(ld_x, 16)
                    dve.wait_ge(ld_w, 16 * 6)
                    first_ln = ln0(Step(0, 0, N3))
                    next(first_ln)
                    next(first_ln)
                    sweep(dve, STEPS, 4, N3, body, 4)

        rows_e = nc.dram_tensor("rows_e", [TOK + 1, 2 * D], F32).ap()
        moe = cx.enter_context(ExitStack())
        ewk_sb = sb("ewk_sb", [P, E, KD, FK], where=moe)
        ewv_sb = sb("ewv_sb", [P, E, FKC, D], where=moe)
        ewr_sb = sb("ewr_sb", [P, E, KD, D], where=moe)
        cm_mu = sb("cm_mu", [P, 2, E, KD], where=moe)
        logits = sb("logits", [P, G, E], where=moe)
        ld_moe = [sem(f"ld_moe{i}") for i in range(4)]
        ei_out = [sem(f"ei_out{i}") for i in range(2)]
        zero_out = sem("zero_out")
        ys = ExitStack()
        with ys:
            def yb(name, shape, dt=F32):
                return sb(name, shape, dt, ys)
            NY = 2
            mixed_w = yb("mixed_w", [P, 3, KD, 2, D])
            t_wo = yb("t_wo", [P, KD, D])
            r_w = yb("r_w", [P, KD, E])
            mu = yb("mu", [P, 3, KD])
            one_mu = yb("one_mu", [P, 3, KD])
            g1 = yb("g1", [P, KD])
            b1 = yb("b1", [P, KD])
            g2 = yb("g2", [P, D])
            b2 = yb("b2", [P, D])
            wd = yb("wd", [P, KD])
            wneg = yb("wneg", [P, KD])
            u_c = yb("u_c", [P, KD])
            keep = yb("keep", [P, 1])
            zero_row = yb("zero_row", [1, D])
            w_pad = yb("w_pad", [P, KD, BG, SP1])

            def pad(name):
                return yb(name, [P, NY, KD, BG, SP1])

            def flat(name):
                return yb(name, [P, NY, KD * P])
            z_in = yb("z_in", [P, NY, D])
            xn, kp, vp, pp, e1b, e2b, evb, aa, bb = (pad(n) for n in (
                "xn", "kp", "vp", "pp", "e1b", "e2b", "evb", "aa", "bb"))
            d1, d2, qq, d3, d4, e1, e2, e2v, e1a, e1bb, er, r_lim, rw = (flat(n) for n in (
                "d1", "d2", "qq", "d3", "d4", "e1", "e2", "e2v", "e1a", "e1bb", "er", "r_lim", "rw"))
            z3 = yb("z3", [P, NY, D])
            ei = yb("ei", [P, NY, D])
            ei_shift = yb("ei_shift", [P, NY, D])
            eiT = yb("eiT", [P, NY, KD, P])
            st3 = yb("st3", [P, NY, 6])
            mv3 = yb("mv3", [P, NY, 2])
            var3 = yb("var3", [P, NY, 1])
            rs3 = yb("rs3", [P, NY, 1])
            bZ, bKV, bR, bX, bE, bL = banks[0:6]
            ld_y, ld_yc, y_set, y_pad, y_w = (sem(n) for n in ("ld_y", "ld_yc", "y_set", "y_pad", "y_w"))
            (pe_z, pe_kv, pe_r, pe_x, pe_e, pe_l, ac_z, ac_kv, ac_r, ac_e1b, ac_e2b, ac_e1, ac_e2, ac_ei,
             dv_d1, dv_d3, dv_scan, dv_rw, dv_r, dv_x2, dv_ln3, dv_lg,
             po_z, po_d2, po_d4, po_ev, po_e2v, po_e1a, po_r3, po_ei) = (sem("y_" + n) for n in (
                 "pe_z pe_kv pe_r pe_x pe_e pe_l ac_z ac_kv ac_r ac_e1b ac_e2b ac_e1 ac_e2 ac_ei "
                 "dv_d1 dv_d3 dv_scan dv_rw dv_r dv_x2 dv_ln3 dv_lg "
                 "po_z po_d2 po_d4 po_ev po_e2v po_e1a po_r3 po_ei").split())
            YSTEPS = G + 4

            def body_of(t, s):
                return t[:, s.slot, :, :, 1:SP1].rearrange("p k j s -> p (k j) s")

            def before(t, s):
                return t[:, s.slot, :, :, 0:S].rearrange("p k j s -> p (k j) s")

            def line(t, s):
                return t[:, s.slot].rearrange("p k j s -> p (k j s)")

            def seqs(t, s):
                return t[:, s.slot].rearrange("p (q s) -> p q s", s=S)

            with nc.Block() as block:
                @block.sync
                def _(sp):
                    for i, w in enumerate((tWk, tWv, tWr)):
                        sp.dma_start(mixed_w[:, i, :, 1], w.rearrange("(k p) o -> p k o", p=P)).then_inc(ld_y, 16)
                    sp.dma_start(t_wo[:], tWo.rearrange("(k p) o -> p k o", p=P)).then_inc(ld_y, 16)
                    sp.dma_start(r_w[:], router_w.rearrange("(k p) o -> p k o", p=P)).then_inc(ld_y, 16)
                    sp.dma_start(g2[:], row(ln2_g)).then_inc(ld_y, 16)
                    sp.dma_start(b2[:], row(ln2_b)).then_inc(ld_y, 16)
                    sp.dma_start(ewk_sb[:], eWk.rearrange("e (k p) f -> p e k f", p=P)).then_inc(ld_moe[0], 16)
                    sp.dma_start(ewr_sb[:], eWr.rearrange("e (k p) f -> p e k f", p=P)).then_inc(ld_moe[1], 16)
                    sp.dma_start(ewv_sb[:], eWv.rearrange("e (k p) f -> p e k f", p=P)).then_inc(ld_moe[2], 16)
                    sp.wait_ge(y_pad, 1)
                    sp.dma_start(rows_e[0:1, 0:D], zero_row[:]).then_inc(zero_out, 16)

                    def body(s):
                        d = s.back(4, G)
                        if d:
                            sp.wait_ge(po_ei, d.n + 1)
                            sp.dma_start(rows_e[bass.ds(d.n * P, P), D:2 * D], ei[:, d.slot]).then_inc(ei_out[d.slot], 16)
                            sp.dma_start(rows_e[bass.ds(d.n * P + 1, P), 0:D], ei_shift[:, d.slot]).then_inc(ei_out[d.slot], 16)
                    sweep(sp, YSTEPS, 6, NY, body, 4)
                    sp.wait_ge(zero_out, 16)
                    for i in range(NY):
                        sp.wait_ge(ei_out[i], 32 * G // NY)

                @block.gpsimd
                def _(pool):
                    nc.gpsimd.memset(zero_row[:], 0.0).then_inc(y_pad, 1)
                    nc.gpsimd.memset(kp[:], NEG)
                    for t in (xn, vp, e1b, e2b, evb):
                        nc.gpsimd.memset(t[:], 0.0)
                    nc.gpsimd.memset(w_pad[:], NEG).then_inc(y_pad, 1)
                    nc.gpsimd.memset(keep[:], 1.0)
                    pool.drain()
                    for j in range(BG):
                        nc.gpsimd.affine_select(out=keep[:], in_=keep[:], compare_op=ALU.not_equal, fill=0.0,
                                                base=-(j * S + S - 1), pattern=[[0, 1]], channel_multiplier=1)
                        pool.drain()
                    pool.wait_ge(ld_y, 16 * 7)

                    def body(s):
                        a, w, x = s.back(0, G), s.back(2, G), s.back(3, G)
                        if a:
                            need(pool, pe_z, a.n - NY + 1)
                            nc.gpsimd.tensor_copy(z_in[:, a.slot], xz[:, a.n]).then_inc(po_z, 1)
                        if w:
                            pool.wait_ge(dv_d1, w.n * 2 + 1)
                            nc.gpsimd.tensor_tensor(seqs(d2, w), body_of(kp, w), body_of(pp, w), ALU.subtract).then_inc(po_d2, 1)
                            pool.wait_ge(dv_d3, w.n * 2 + 1)
                            nc.gpsimd.tensor_tensor(seqs(d4, w), body_of(kp, w), seqs(qq, w), ALU.subtract).then_inc(po_d4, 1)
                        if x:
                            pool.wait_ge(dv_ln3, x.n * 2 + 1)
                            nc.gpsimd.tensor_tensor(rs3[:, x.slot], var3[:, x.slot], eps_pow[:], ALU.pow).then_inc(po_r3, 1)
                        if w:
                            pool.wait_ge(ac_e2b, w.n + 1)
                            nc.gpsimd.tensor_tensor(body_of(evb, w), body_of(e2b, w), body_of(vp, w), ALU.mult).then_inc(po_ev, 1)
                            pool.wait_ge(ac_e2, w.n + 1)
                            nc.gpsimd.tensor_tensor(seqs(e2v, w), seqs(e2, w), body_of(vp, w), ALU.mult).then_inc(po_e2v, 1)
                            pool.wait_ge(ac_e1, w.n + 1)
                            pool.wait_ge(dv_scan, w.n * 2 + 1)
                            nc.gpsimd.tensor_tensor(seqs(e1a, w), seqs(e1, w), before(aa, w), ALU.mult)
                            pool.wait_ge(dv_scan, w.n * 2 + 2)
                            nc.gpsimd.tensor_tensor(seqs(e1bb, w), seqs(e1, w), before(bb, w), ALU.mult).then_inc(po_e1a, 1)
                        if x:
                            pool.wait_ge(dv_ln3, x.n * 2 + 2)
                            need(pool, pe_e, x.n - NY + 1)
                            need(pool, ei_out[x.slot], x.lap * 32)
                            nc.gpsimd.tensor_tensor(ei[:, x.slot], z3[:, x.slot], g2[:], ALU.mult)
                            pool.drain()
                            nc.gpsimd.tensor_tensor(ei[:, x.slot], ei[:, x.slot], b2[:], ALU.add)
                            pool.drain()
                            nc.gpsimd.tensor_scalar(ei_shift[:, x.slot], ei[:, x.slot], keep[:], None, ALU.mult).then_inc(po_ei, 1)
                    sweep(pool, YSTEPS, 6, NY, body, 4)

                @block.tensor
                def _(pe):
                    pe.wait_ge(y_w, 7)
                    pe.wait_ge(ld_y, 16 * 7)

                    def body(s):
                        a, b, x, d = s.back(0, G), s.back(1, G), s.back(3, G), s.back(4, G)
                        if x:
                            pe.wait_ge(dv_rw, x.n + 1)
                            need(pe, dv_x2, x.n)
                            for k in range(KD):
                                last = nc.tensor.matmul(bX[:, 0:D], rw[:, x.slot, k * P:(k + 1) * P], t_wo[:, k],
                                                        start=k == 0, stop=k == KD - 1)
                            last.then_inc(pe_x, 1)
                        if b:
                            pe.wait_ge(ac_z, b.n + 1)
                            for i in range(3):
                                if i == 0:
                                    need(pe, ac_kv, b.n)
                                if i == 2:
                                    need(pe, dv_r, b.n)
                                for m in range(KD):
                                    o = (bKV, bKV, bR)[i][:, (i % 2 * KD + m) * P:(i % 2 * KD + m + 1) * P]
                                    for k in range(KD):
                                        for h in range(2):
                                            last = nc.tensor.matmul(o.rearrange("p (j s) -> p j s", j=BG),
                                                                    mixed_w[:, i, k, h, m * P:(m + 1) * P],
                                                                    xn[:, b.slot, k, :, 1 - h:1 - h + S],
                                                                    start=k == 0 and h == 0, stop=k == KD - 1 and h == 1)
                                if i == 1:
                                    last.then_inc(pe_kv, 1)
                            last.then_inc(pe_r, 1)
                        if d:
                            pe.wait_ge(po_ei, d.n + 1)
                            need(pe, ac_ei, d.n)
                            for k in range(KD):
                                last = nc.tensor.transpose(bE[:, k * P:(k + 1) * P], ei[:, d.slot, k * P:(k + 1) * P], ident[:])
                            last.then_inc(pe_e, 1)
                        if a:
                            pe.wait_ge(po_z, a.n + 1)
                            need(pe, ac_z, a.n)
                            for k in range(KD):
                                last = nc.tensor.transpose(bZ[:, k * P:(k + 1) * P], z_in[:, a.slot, k * P:(k + 1) * P], ident[:])
                            last.then_inc(pe_z, 1)
                        if d:
                            pe.wait_ge(ac_ei, d.n + 1)
                            need(pe, dv_lg, d.n)
                            for k in range(KD):
                                last = nc.tensor.matmul(bL[:, 0:E], eiT[:, d.slot, k], r_w[:, k], start=k == 0, stop=k == KD - 1)
                            last.then_inc(pe_l, 1)
                    sweep(pe, YSTEPS, 6, NY, body, 4)

                @block.scalar
                def _(act):
                    for i, m in enumerate((mu_k, mu_v, mu_r)):
                        act.dma_start(mu[:, i], col(m)).then_inc(ld_yc, 16)
                    for t, v in ((g1, ln1_g), (b1, ln1_b), (wd, decay), (u_c, first)):
                        act.dma_start(t[:], col(v)).then_inc(ld_yc, 16)
                    for i, m in enumerate((cm_mu_k, cm_mu_r)):
                        for e in range(E):
                            act.dma_start(cm_mu[:, i, e], m[e].rearrange("(k p) -> p k", p=P)).then_inc(ld_moe[3], 16)
                    act.wait_ge(ld_yc, 16 * 7)
                    nc.scalar.activation(wneg[:], wd[:], ACT.Exp)
                    act.drain()
                    nc.scalar.mul(wneg[:], wneg[:], -1.0).then_inc(y_set, 1)
                    act.drain()
                    act.wait_ge(y_pad, 2)

                    def body(s):
                        a, b, w, d = s.back(0, G), s.back(1, G), s.back(2, G), s.back(4, G)
                        if b:
                            act.wait_ge(pe_kv, b.n + 1)
                            need(act, po_e2v, b.n - NY + 1)
                            need(act, dv_rw, b.n - NY + 1)
                            nc.scalar.activation(body_of(kp, b), bKV[:, 0:KD * P].rearrange("p (q s) -> p q s", s=S), ACT.Copy)
                            nc.scalar.activation(body_of(vp, b), bKV[:, KD * P:].rearrange("p (q s) -> p q s", s=S),
                                                 ACT.Copy).then_inc(ac_kv, 1)
                        if w:
                            act.wait_ge(dv_d1, w.n * 2 + 2)
                            for k in range(KD):
                                last = nc.scalar.activation(e1b[:, w.slot, k, :, 1:SP1],
                                                            d1[:, w.slot, k * P:(k + 1) * P].rearrange("p (j s) -> p j s", s=S),
                                                            ACT.Exp, bias=wneg[:, k:k + 1])
                            last.then_inc(ac_e1b, 1)
                            act.wait_ge(po_d2, w.n + 1)
                            nc.scalar.activation(body_of(e2b, w), seqs(d2, w), ACT.Exp).then_inc(ac_e2b, 1)
                            act.wait_ge(dv_d3, w.n * 2 + 2)
                            nc.scalar.activation(e1[:, w.slot], d3[:, w.slot], ACT.Exp).then_inc(ac_e1, 1)
                            act.wait_ge(po_d4, w.n + 1)
                            for k in range(KD):
                                last = nc.scalar.activation(e2[:, w.slot, k * P:(k + 1) * P], d4[:, w.slot, k * P:(k + 1) * P],
                                                            ACT.Exp, bias=u_c[:, k:k + 1])
                            last.then_inc(ac_e2, 1)
                        if d:
                            act.wait_ge(pe_e, d.n + 1)
                            need(act, pe_l, d.n - NY + 1)
                            nc.scalar.activation(eiT[:, d.slot].rearrange("p k t -> p (k t)"), bE[:, 0:KD * P],
                                                 ACT.Copy).then_inc(ac_ei, 1)
                        if b:
                            act.wait_ge(dv_r, b.n + 1)
                            nc.scalar.activation(er[:, b.slot], r_lim[:, b.slot], ACT.Exp, scale=-1.0).then_inc(ac_r, 1)
                        if a:
                            act.wait_ge(pe_z, a.n + 1)
                            need(act, pe_r, a.n - NY + 1)
                            for k in range(KD):
                                last = nc.scalar.activation(xn[:, a.slot, k, :, 1:SP1],
                                                            bZ[:, k * P:(k + 1) * P].rearrange("p (j s) -> p j s", s=S),
                                                            ACT.Identity, bias=b1[:, k:k + 1], scale=g1[:, k:k + 1])
                            last.then_inc(ac_z, 1)
                    sweep(act, YSTEPS, 6, NY, body, 4)

                @block.vector
                def _(dve):
                    dve.wait_ge(ld_y, 16 * 7)
                    dve.wait_ge(ld_yc, 16 * 7)
                    nc.vector.tensor_scalar(one_mu[:], mu[:], -1.0, 1.0, ALU.mult, ALU.add)
                    dve.drain()
                    for i in range(3):
                        for k in range(KD):
                            for h, m in enumerate((mu, one_mu)):
                                last = nc.vector.tensor_scalar(mixed_w[:, i, k, h], mixed_w[:, i, k, 1], m[:, i, k:k + 1], None, ALU.mult)
                            last.then_inc(y_w, 1)
                    dve.wait_ge(y_pad, 2)
                    dve.wait_ge(y_set, 1)
                    nc.vector.memset(w_pad[:, :, :, 1:SP1].rearrange("p k j s -> p (k j) s"), 0.0)
                    dve.drain()
                    for k in range(KD):
                        nc.vector.tensor_scalar(w_pad[:, k, :, 1:SP1], w_pad[:, k, :, 1:SP1], wneg[:, k:k + 1], None, ALU.add)
                    dve.drain()
                    nc.vector.tensor_copy(one_mu[:, 0, 0:1], one_mu[:, 0, 0:1]).then_inc(y_w, 1)

                    def body(s):
                        b, w, x, d = s.back(1, G), s.back(2, G), s.back(3, G), s.back(4, G)
                        if w:
                            o1, o3 = Order(dve, dv_d1, 2, w.n), Order(dve, dv_d3, 2, w.n)
                            dve.wait_ge(ac_kv, w.n + 1)
                            o1.link(nc.vector.tensor_tensor_scan(line(pp, w), w_pad[:].rearrange("p k j s -> p (k j s)"),
                                                                 line(kp, w), NEG, ALU.add, ALU.max))
                            o1.then(nc.vector.tensor_tensor(seqs(d1, w), before(pp, w), body_of(pp, w), ALU.subtract))
                            for k in range(KD):
                                last = nc.vector.scalar_tensor_tensor(
                                    qq[:, w.slot, k * P:(k + 1) * P].rearrange("p (j s) -> p j s", s=S),
                                    kp[:, w.slot, k, :, 1:SP1], u_c[:, k:k + 1], pp[:, w.slot, k, :, 0:S], ALU.add, ALU.max)
                            o3.link(last)
                            o3.then(nc.vector.tensor_tensor(seqs(d3, w), before(pp, w), seqs(qq, w), ALU.subtract))
                        if x:
                            dve.wait_ge(pe_x, x.n + 1)
                            nc.vector.tensor_tensor(a_x2[:, x.n], bX[:, 0:D], a_x2[:, x.n], ALU.add).then_inc(dv_x2, 1)
                            o = Order(dve, dv_ln3, 2, x.n)
                            dve.drain()
                            nc.vector.bn_stats(st3[:, x.slot], a_x2[:, x.n])
                            dve.drain()
                            nc.vector.bn_aggr(mv3[:, x.slot], st3[:, x.slot])
                            dve.drain()
                            o.then(nc.vector.tensor_scalar(var3[:, x.slot], mv3[:, x.slot, 1:2], EPS, None, ALU.add))
                        if w:
                            osc = Order(dve, dv_scan, 2, w.n)
                            dve.wait_ge(ac_e1b, w.n + 1)
                            dve.wait_ge(po_ev, w.n + 1)
                            osc.then(nc.vector.tensor_tensor_scan(line(aa, w), line(e1b, w), line(evb, w), 0.0, ALU.mult, ALU.add))
                            osc.then(nc.vector.tensor_tensor_scan(line(bb, w), line(e1b, w), line(e2b, w), 0.0, ALU.mult, ALU.add))
                        if x:
                            dve.wait_ge(po_r3, x.n + 1)
                            o.then(nc.vector.tensor_scalar(z3[:, x.slot], a_x2[:, x.n], mv3[:, x.slot, 0:1], rs3[:, x.slot],
                                                           ALU.subtract, ALU.mult))
                        if b:
                            dve.wait_ge(pe_r, b.n + 1)
                            nc.vector.tensor_scalar(r_lim[:, b.slot], bR[:, 0:KD * P], -R_LOW, None, ALU.max).then_inc(dv_r, 1)
                        if d:
                            dve.wait_ge(pe_l, d.n + 1)
                            nc.vector.tensor_copy(logits[:, d.n], bL[:, 0:E]).then_inc(dv_lg, 1)
                        if w:
                            dve.wait_ge(po_e1a, w.n + 1)
                            dve.wait_ge(ac_r, w.n + 1)
                            nc.vector.tensor_tensor(e1bb[:, w.slot], e1bb[:, w.slot], e2[:, w.slot], ALU.add)
                            nc.vector.tensor_tensor(e1a[:, w.slot], e1a[:, w.slot], e2v[:, w.slot], ALU.add)
                            dve.drain()
                            nc.vector.scalar_tensor_tensor(e1bb[:, w.slot], er[:, w.slot], 1.0, e1bb[:, w.slot], ALU.add, ALU.mult)
                            dve.drain()
                            nc.vector.reciprocal(e1bb[:, w.slot], e1bb[:, w.slot])
                            dve.drain()
                            need(dve, pe_x, w.n - NY + 1)
                            nc.vector.tensor_tensor(rw[:, w.slot], e1a[:, w.slot], e1bb[:, w.slot], ALU.mult).then_inc(dv_rw, 1)
                    sweep(dve, YSTEPS, 6, NY, body, 4)

        rt_consts = sem("rt_consts")

        def routing(tag, choices, tiles, scores_in, softmax, table, tile_expert, slot_of, weights):
            with ExitStack() as rs:
                def rb(name, shape, dt=F32):
                    return sb(tag + name, shape, dt, rs)
                tile_id = rb("tile_id", [P, tiles])
                mx, total = rb("mx", [P, G]), rb("total", [P, G])
                pr = rb("pr", [P, G, E])
                top, at = rb("top", [P, G, 8]), rb("at", [P, G, 8], U32)
                at_f = rb("at_f", [P, choices, G])
                hot = rb("hot", [P, choices, G, E])
                mask = rb("mask", [P, G, E])
                tot_ec, run_ec, pos = rb("tot_ec", [P, E, G]), rb("run_ec", [P, E, G]), rb("pos", [P, G, E])
                cmp_eg = rb("cmp_eg", [P, E, G])
                n_tiles, t_end, base = rb("n_tiles", [P, E]), rb("t_end", [P, E]), rb("base", [P, E])
                cmp_te = rb("cmp_te", [P, tiles, E])
                te_f = rb("te_f", [P, tiles])
                prod = rb("prod", [P, G, E])
                slot_f, slot_i = rb("slot_f", [P, choices, G]), rb("slot_i", [P, choices, G], I32)
                q_i, r_i = rb("q_i", [P, choices, G], I32), rb("r_i", [P, choices, G], I32)
                q_f, r_f = rb("q_f", [P, choices, G]), rb("r_f", [P, choices, G])
                hot_r = rb("hot_r", [P, choices, G, P])
                hot_q = rb("hot_q", [P, choices, G, tiles])
                bC, bTab = banks[0], banks[1]
                s_id, s_sub, s_exp, s_mask, s_cnt, s_hot, s_tab = (sem(tag + n) for n in (
                    "id", "sub", "exp", "mask", "cnt", "hot", "tab"))
                with nc.Block() as block:
                    @block.gpsimd
                    def _(pool):
                        nc.gpsimd.iota(tile_id[:], [[1, tiles]], base=0, channel_multiplier=0,
                                       allow_small_or_imprecise_dtypes=True).then_inc(s_id, 1)

                    @block.scalar
                    def _(act):
                        if softmax:
                            act.wait_ge(s_sub, 1)
                            nc.scalar.activation(pr[:], pr[:], ACT.Exp).then_inc(s_exp, 1)

                    @block.tensor
                    def _(pe):
                        pe.wait_ge(s_mask, 1)
                        m = mask[:].rearrange("p c e -> p (c e)")
                        nc.tensor.matmul(bC[:, 0:G * E], before_m[:], m, start=True, stop=True)
                        nc.tensor.matmul(bC[:, G * E:2 * G * E], ones_m[:], m, start=True, stop=True).then_inc(s_cnt, 1)
                        pe.wait_ge(s_hot, 1)
                        for k in range(choices):
                            for c in range(G):
                                last = nc.tensor.matmul(bTab[:, 0:tiles], hot_r[:, k, c], hot_q[:, k, c],
                                                        start=k == 0 and c == 0, stop=k == choices - 1 and c == G - 1)
                        last.then_inc(s_tab, 1)

                    @block.vector
                    def _(dve):
                        def step(ins):
                            dve.drain()
                            return ins

                        def tt(o, a, b, op):
                            return step(nc.vector.tensor_tensor(o, a, b, op))

                        def over_e(v):
                            return v.unsqueeze(2).to_broadcast([P, G, E])

                        def over_g(v):
                            return v.unsqueeze(2).to_broadcast([P, E, G])
                        dve.wait_ge(rt_consts, 9)
                        src = scores_in
                        if softmax:
                            step(nc.vector.reduce_max(mx[:], scores_in[:], AX))
                            nc.vector.tensor_tensor(pr[:], scores_in[:], over_e(mx[:]), ALU.subtract).then_inc(s_sub, 1)
                            dve.wait_ge(s_exp, 1)
                            step(nc.vector.reduce_sum(total[:], pr[:], AX))
                            step(nc.vector.reciprocal(total[:], total[:]))
                            tt(pr[:], pr[:], over_e(total[:]), ALU.mult)
                            src = pr
                        for c in range(G):
                            nc.vector.max(top[:, c], src[:, c])
                        dve.drain()
                        for c in range(G):
                            nc.vector.max_index(at[:, c], top[:, c], src[:, c])
                        dve.drain()
                        if weights is not None:
                            tt(total[:], top[:, :, 0], top[:, :, 1], ALU.add)
                            step(nc.vector.reciprocal(total[:], total[:]))
                            for k in range(choices):
                                nc.vector.tensor_tensor(weights[:, k], top[:, :, k], total[:], ALU.mult)
                        for k in range(choices):
                            nc.vector.tensor_copy(at_f[:, k], at[:, :, k])
                        dve.drain()
                        for k in range(choices):
                            nc.vector.tensor_tensor(hot[:, k], iota_e[:].unsqueeze(1).to_broadcast([P, G, E]),
                                                    over_e(at_f[:, k]), ALU.is_equal)
                        dve.drain()
                        if choices == 2:
                            nc.vector.tensor_tensor(mask[:], hot[:, 0], hot[:, 1], ALU.add).then_inc(s_mask, 1)
                        else:
                            nc.vector.tensor_copy(mask[:], hot[:, 0]).then_inc(s_mask, 1)
                        dve.wait_ge(s_cnt, 1)
                        step(nc.vector.tensor_copy(tot_ec[:], bC[:, G * E:2 * G * E].rearrange("p (c e) -> p e c", e=E)))
                        step(nc.vector.tensor_tensor_scan(run_ec[:].rearrange("p e c -> p (e c)"),
                                                          chunk_on[:].rearrange("p e c -> p (e c)"),
                                                          tot_ec[:].rearrange("p e c -> p (e c)"), 0.0, ALU.mult, ALU.add))
                        tt(cmp_eg[:], over_g(run_ec[:, :, G - 1]), tile_lo[:].unsqueeze(1).to_broadcast([P, E, G]), ALU.is_gt)
                        step(nc.vector.reduce_sum(n_tiles[:], cmp_eg[:], AX))
                        step(nc.vector.tensor_tensor_scan(t_end[:], ones_m[:, 0:E], n_tiles[:], 0.0, ALU.mult, ALU.add))
                        tt(base[:], t_end[:], n_tiles[:], ALU.subtract)
                        step(nc.vector.tensor_scalar(base[:], base[:], float(P), None, ALU.mult))
                        tt(run_ec[:], run_ec[:], tot_ec[:], ALU.subtract)
                        tt(run_ec[:], run_ec[:], over_g(base[:]), ALU.add)
                        tt(pos[:], bC[:, 0:G * E].rearrange("p (c e) -> p c e", e=E),
                           run_ec[:].rearrange("p e c -> p c e"), ALU.add)
                        dve.wait_ge(s_id, 1)
                        tt(cmp_te[:], t_end[:].unsqueeze(1).to_broadcast([P, tiles, E]),
                           tile_id[:].unsqueeze(2).to_broadcast([P, tiles, E]), ALU.is_le)
                        step(nc.vector.reduce_sum(te_f[:], cmp_te[:], AX))
                        nc.vector.tensor_scalar(tile_expert[:], te_f[:], float(E - 1), None, ALU.min)
                        for k in range(choices):
                            tt(prod[:], hot[:, k], pos[:], ALU.mult)
                            step(nc.vector.reduce_sum(slot_f[:, k], prod[:], AX))
                        step(nc.vector.tensor_copy(slot_i[:], slot_f[:]))
                        nc.vector.tensor_copy(slot_of[:], slot_f[:])
                        nc.vector.tensor_scalar(q_i[:], slot_i[:], 7, None, ALU.logical_shift_right)
                        step(nc.vector.tensor_scalar(r_i[:], slot_i[:], P - 1, None, ALU.bitwise_and))
                        nc.vector.tensor_copy(q_f[:], q_i[:])
                        step(nc.vector.tensor_copy(r_f[:], r_i[:]))
                        for k in range(choices):
                            nc.vector.tensor_tensor(hot_r[:, k], iota_p[:].unsqueeze(1).to_broadcast([P, G, P]),
                                                    r_f[:, k].unsqueeze(2).to_broadcast([P, G, P]), ALU.is_equal)
                            tt(hot_q[:, k], tile_id[:].unsqueeze(1).to_broadcast([P, G, tiles]),
                               q_f[:, k].unsqueeze(2).to_broadcast([P, G, tiles]), ALU.is_equal)
                            last = nc.vector.tensor_tensor(hot_q[:, k], hot_q[:, k],
                                                           token_id[:].unsqueeze(2).to_broadcast([P, G, tiles]), ALU.mult)
                        last.then_inc(s_hot, 1)
                        dve.wait_ge(s_tab, 1)
                        nc.vector.tensor_copy(table[:], bTab[:, 0:tiles])

        def most_tiles(pairs):
            return (pairs - E) // P + E

        NT1 = most_tiles(2 * TOK)
        table1 = sb("table1", [P, NT1], U32, moe)
        expert1 = sb("expert1", [P, NT1], I32, moe)
        slot1 = sb("slot1", [P, 2, G], U32, moe)
        gate = sb("gate", [P, 2, G], where=moe)
        with nc.Block() as block:
            @block.gpsimd
            def _(pool):
                def iota(t, pattern, channel):
                    nc.gpsimd.iota(t, pattern, base=0, channel_multiplier=channel,
                                   allow_small_or_imprecise_dtypes=True).then_inc(rt_consts, 1)
                iota(iota_e[:], [[1, E]], 0)
                iota(iota_p[:], [[1, P]], 0)
                iota(tile_lo[:], [[P, G]], 0)
                iota(token_id[:], [[P, G]], 1)
                nc.gpsimd.memset(before_m[:], 1.0).then_inc(rt_consts, 1)
                nc.gpsimd.memset(ones_m[:], 1.0).then_inc(rt_consts, 1)
                nc.gpsimd.memset(chunk_on[:], 1.0)
                pool.drain()
                nc.gpsimd.memset(chunk_on[:, :, 0:1], 0.0).then_inc(rt_consts, 1)
                nc.gpsimd.affine_select(out=before_m[:], in_=before_m[:], compare_op=ALU.is_gt, fill=0.0, base=0,
                                        pattern=[[1, P]], channel_multiplier=-1).then_inc(rt_consts, 2)
        routing("r1_", 2, NT1, logits, True, table1, expert1, slot1, gate)

        rows_y = nc.dram_tensor("rows_y", [NT1 * P, D], F32).ap()
        with ExitStack() as ms:
            NM = 3

            def mb(name, shape, dt=F32):
                return sb(name, shape, dt, ms)
            pick = mb("pick", [P, NM, 1], U32)
            pair = mb("pair", [P, NM, 2 * D])
            mu_e = mb("mu_e", [P, NM, 2, KD])
            prevT, diffT = mb("prevT", [P, NM, KD, P]), mb("diffT", [P, NM, KD, P])
            xk, xr = mb("xk", [P, NM, KD, P]), mb("xr", [P, NM, KD, P])
            h_relu, h_sq = mb("h_relu", [P, NM, FK]), mb("h_sq", [P, NM, FK])
            hT = mb("hT", [P, NM, FKC, P])
            sig = mb("sig", [P, NM, D])
            y = mb("y", [P, NM, D])
            bA, bR, bH, bT, bY = banks[0:5]
            (pe_a, pe_r, pe_h, pe_t, pe_y, ac_p, ac_sig, ac_relu, ac_t, dv_d, dv_x, dv_sq, dv_y, po_mu) = (
                sem("m_" + n) for n in ("pe_a pe_r pe_h pe_t pe_y ac_p ac_sig ac_relu ac_t dv_d dv_x dv_sq dv_y "
                                        "po_mu").split())
            got = [sem(f"m_got{i}") for i in range(NM)]
            put = [sem(f"m_put{i}") for i in range(NM)]
            MSTEPS = NT1 + 3

            with nc.Block() as block:
                @block.gpsimd
                def _(pool):
                    pool.wait_ge(ld_moe[3], 16 * 2 * E)

                    def body(s):
                        need(pool, pe_a, s.n - NM + 1)
                        nc.gpsimd.tensor_copy(pick[:, s.slot], table1[:, bass.ds(s.n, 1)])
                        pool.drain()
                        nc.gpsimd.indirect_dma_start(out=pair[:, s.slot], out_offset=None, in_=rows_e[0:TOK, :],
                                                     in_offset=bass.IndirectOffsetOnAxis(ap=pick[:, s.slot], axis=0)
                                                     ).then_inc(got[s.slot], 16)
                        e = pool.value_load(expert1[0:1, bass.ds(s.n, 1)], min_val=0, max_val=E - 1)
                        need(pool, dv_x, s.n - NM + 1)
                        nc.gpsimd.tensor_copy(mu_e[:, s.slot], cm_mu[:, :, e]).then_inc(po_mu, 1)
                    sweep(pool, NT1, NM, NM, body, 0)

                @block.tensor
                def _(pe):
                    for i in range(3):
                        pe.wait_ge(ld_moe[i], 16)

                    def body(s):
                        a, b, c, d = (s.back(k, NT1) for k in range(4))
                        if a:
                            pe.wait_ge(got[a.slot], a.lap * 16 + 16)
                            need(pe, dv_d, a.n)
                            for q in range(2 * KD):
                                last = nc.tensor.transpose(bA[:, q * P:(q + 1) * P], pair[:, a.slot, q * P:(q + 1) * P], ident[:])
                            last.then_inc(pe_a, 1)
                        if c:
                            pe.wait_ge(dv_sq, c.n + 1)
                            need(pe, ac_t, c.n)
                            for f in range(FKC):
                                last = nc.tensor.transpose(bT[:, f * P:(f + 1) * P], h_sq[:, c.slot, f * P:(f + 1) * P], ident[:])
                            last.then_inc(pe_t, 1)
                        if b:
                            e = pe.value_load(expert1[0:1, bass.ds(b.n, 1)], min_val=0, max_val=E - 1)
                            pe.wait_ge(dv_x, b.n + 1)
                            need(pe, dv_sq, b.n)
                            for k in range(KD):
                                last = nc.tensor.matmul(bH[:], xk[:, b.slot, k], ewk_sb[:, e, k], start=k == 0, stop=k == KD - 1)
                            last.then_inc(pe_h, 1)
                            need(pe, ac_sig, b.n)
                            for k in range(KD):
                                last = nc.tensor.matmul(bR[:, 0:D], xr[:, b.slot, k], ewr_sb[:, e, k], start=k == 0, stop=k == KD - 1)
                            last.then_inc(pe_r, 1)
                        if d:
                            e = pe.value_load(expert1[0:1, bass.ds(d.n, 1)], min_val=0, max_val=E - 1)
                            pe.wait_ge(ac_t, d.n + 1)
                            need(pe, dv_y, d.n)
                            for f in range(FKC):
                                last = nc.tensor.matmul(bY[:, 0:D], hT[:, d.slot, f], ewv_sb[:, e, f], start=f == 0, stop=f == FKC - 1)
                            last.then_inc(pe_y, 1)
                    sweep(pe, MSTEPS, 6, NM, body, 3)

                @block.scalar
                def _(act):
                    def body(s):
                        a, b, c = (s.back(k, NT1) for k in range(3))
                        if a:
                            act.wait_ge(pe_a, a.n + 1)
                            need(act, dv_x, a.n - NM + 1)
                            nc.scalar.activation(prevT[:, a.slot].rearrange("p k t -> p (k t)"), bA[:, 0:KD * P],
                                                 ACT.Copy).then_inc(ac_p, 1)
                        if c:
                            act.wait_ge(pe_t, c.n + 1)
                            need(act, pe_y, c.n - NM + 1)
                            nc.scalar.activation(hT[:, c.slot].rearrange("p f t -> p (f t)"), bT[:], ACT.Copy).then_inc(ac_t, 1)
                        if b:
                            act.wait_ge(pe_h, b.n + 1)
                            need(act, dv_sq, b.n - NM + 1)
                            nc.scalar.activation(h_relu[:, b.slot], bH[:], ACT.Relu).then_inc(ac_relu, 1)
                            act.wait_ge(pe_r, b.n + 1)
                            need(act, dv_y, b.n - NM + 1)
                            nc.scalar.activation(sig[:, b.slot], bR[:, 0:D], ACT.Sigmoid).then_inc(ac_sig, 1)
                    sweep(act, MSTEPS, 6, NM, body, 3)

                @block.vector
                def _(dve):
                    def body(s):
                        a, b, d = s.back(0, NT1), s.back(1, NT1), s.back(3, NT1)
                        if a:
                            dve.wait_ge(ac_p, a.n + 1)
                            nc.vector.tensor_tensor(diffT[:, a.slot].rearrange("p k t -> p (k t)"), bA[:, KD * P:],
                                                    prevT[:, a.slot].rearrange("p k t -> p (k t)"), ALU.subtract).then_inc(dv_d, 1)
                            dve.drain()
                            dve.wait_ge(po_mu, a.n + 1)
                            need(dve, pe_r, a.n - NM + 1)
                            for i, o in enumerate((xk, xr)):
                                for k in range(KD):
                                    last = nc.vector.scalar_tensor_tensor(o[:, a.slot, k], diffT[:, a.slot, k],
                                                                          mu_e[:, a.slot, i, k:k + 1], prevT[:, a.slot, k],
                                                                          ALU.mult, ALU.add)
                            last.then_inc(dv_x, 1)
                        if b:
                            dve.wait_ge(ac_relu, b.n + 1)
                            need(dve, pe_t, b.n - NM + 1)
                            nc.vector.tensor_tensor(h_sq[:, b.slot], bH[:], h_relu[:, b.slot], ALU.mult).then_inc(dv_sq, 1)
                        if d:
                            dve.wait_ge(pe_y, d.n + 1)
                            need(dve, put[d.slot], d.lap * 16)
                            nc.vector.tensor_tensor(y[:, d.slot], bY[:, 0:D], sig[:, d.slot], ALU.mult).then_inc(dv_y, 1)
                    sweep(dve, MSTEPS, 6, NM, body, 3)

                @block.sync
                def _(sp):
                    def body(s):
                        sp.wait_ge(dv_y, s.n + 1)
                        sp.dma_start(rows_y[bass.ds(s.n * P, P), :], y[:, s.slot]).then_inc(put[s.slot], 16)
                    sweep(sp, NT1, NM, NM, body, 0)
                    for i in range(NM):
                        sp.wait_ge(put[i], NT1 // NM * 16)
            assert NT1 % NM == 0

        rows_z = nc.dram_tensor("rows_z", [TOK, D], F32).ap()
        with ExitStack() as cs:
            NC = 3

            def cb(name, shape, dt=F32):
                return sb(name, shape, dt, cs)
            r2_w = cb("r2_w", [P, KD, E])
            pick = cb("pick_c", [P, NC, 2], U32)
            ya, yb2 = cb("ya", [P, NC, D]), cb("yb2", [P, NC, D])
            xsum = cb("xsum", [P, NC, D])
            z4 = cb("z4", [P, NC, D])
            zT = cb("zT", [P, NC, KD, P])
            st4, mv4, var4, rs4 = (cb(n, [P, NC, w]) for n, w in (("st4", 6), ("mv4", 2), ("var4", 1), ("rs4", 1)))
            bZ, bL = banks[0:2]
            (c_pe_z, c_pe_l, c_ac_z, c_dv, c_dv_l, c_po_r, c_po_x, ld_c) = (
                sem(n) for n in "c_pe_z c_pe_l c_ac_z c_dv c_dv_l c_po_r c_po_x ld_c".split())
            got = [sem(f"c_got{i}") for i in range(NC)]
            put = [sem(f"c_put{i}") for i in range(NC)]
            with nc.Block() as block:
                @block.gpsimd
                def _(pool):
                    def body(s):
                        a, b = s.back(0, G), s.back(1, G)
                        if a:
                            need(pool, c_dv, (a.n - NC) * 4 + 2)
                            nc.gpsimd.tensor_copy(pick[:, a.slot], slot1[:, :, a.n])
                            nc.gpsimd.tensor_tensor(xsum[:, a.slot], x1[:, a.n], a_x2[:, a.n], ALU.add).then_inc(c_po_x, 1)
                            pool.drain()
                            for k, t in enumerate((ya, yb2)):
                                nc.gpsimd.indirect_dma_start(out=t[:, a.slot], out_offset=None, in_=rows_y[:, :],
                                                             in_offset=bass.IndirectOffsetOnAxis(ap=pick[:, a.slot, k:k + 1], axis=0)
                                                             ).then_inc(got[a.slot], 16)
                        if b:
                            pool.wait_ge(c_dv, b.n * 4 + 3)
                            nc.gpsimd.tensor_tensor(rs4[:, b.slot], var4[:, b.slot], eps_pow[:], ALU.pow).then_inc(c_po_r, 1)
                    sweep(pool, G + 1, 4, NC, body, 1)

                @block.vector
                def _(dve):
                    def apply(s):
                        dve.wait_ge(c_po_r, s.n + 1)
                        need(dve, c_pe_z, s.n - NC + 1)
                        need(dve, put[s.slot], s.lap * 16)
                        nc.vector.tensor_scalar(z4[:, s.slot], xz[:, s.n], mv4[:, s.slot, 0:1], rs4[:, s.slot],
                                                ALU.subtract, ALU.mult).then_inc(c_dv, 1)

                    def body(s):
                        a, b, d = s.back(0, G), s.back(1, G), s.back(3, G)
                        if a:
                            dve.wait_ge(got[a.slot], a.lap * 32 + 32)
                            dve.wait_ge(c_po_x, a.n + 1)
                            nc.vector.scalar_tensor_tensor(xsum[:, a.slot], ya[:, a.slot], gate[:, 0, bass.ds(a.n, 1)],
                                                           xsum[:, a.slot], ALU.mult, ALU.add).then_inc(c_dv, 1)
                            dve.drain()
                            nc.vector.scalar_tensor_tensor(xz[:, a.n], yb2[:, a.slot], gate[:, 1, bass.ds(a.n, 1)],
                                                           xsum[:, a.slot], ALU.mult, ALU.add).then_inc(c_dv, 1)
                            dve.drain()
                            nc.vector.bn_stats(st4[:, a.slot], xz[:, a.n])
                            dve.drain()
                            nc.vector.bn_aggr(mv4[:, a.slot], st4[:, a.slot])
                            dve.drain()
                            nc.vector.tensor_scalar(var4[:, a.slot], mv4[:, a.slot, 1:2], EPS, None, ALU.add).then_inc(c_dv, 1)
                            apply(a)
                        if d:
                            dve.wait_ge(c_pe_l, d.n + 1)
                            nc.vector.tensor_copy(logits2[:, d.n], bL[:, 0:E]).then_inc(c_dv_l, 1)
                    sweep(dve, G + 3, 6, NC, body, 3)

                @block.tensor
                def _(pe):
                    pe.wait_ge(ld_c, 16)

                    def body(s):
                        a, b = s.back(0, G), s.back(1, G)
                        if a:
                            pe.wait_ge(c_dv, a.n * 4 + 4)
                            need(pe, c_ac_z, a.n)
                            for k in range(KD):
                                last = nc.tensor.transpose(bZ[:, k * P:(k + 1) * P], z4[:, a.slot, k * P:(k + 1) * P], ident[:])
                            last.then_inc(c_pe_z, 1)
                        if b:
                            pe.wait_ge(c_ac_z, b.n + 1)
                            need(pe, c_dv_l, b.n)
                            for k in range(KD):
                                last = nc.tensor.matmul(bL[:, 0:E], zT[:, b.slot, k], r2_w[:, k], start=k == 0, stop=k == KD - 1)
                            last.then_inc(c_pe_l, 1)
                    sweep(pe, G + 1, 4, NC, body, 1)

                @block.scalar
                def _(act):
                    def body(s):
                        act.wait_ge(c_pe_z, s.n + 1)
                        need(act, c_pe_l, s.n - NC + 1)
                        nc.scalar.activation(zT[:, s.slot].rearrange("p k t -> p (k t)"), bZ[:, 0:KD * P],
                                             ACT.Copy).then_inc(c_ac_z, 1)
                    sweep(act, G, 4, NC, body, 0)

                @block.sync
                def _(sp):
                    sp.dma_start(r2_w[:], Wg.rearrange("(k p) e -> p k e", p=P)).then_inc(ld_c, 16)

                    def body(s):
                        sp.wait_ge(c_dv, s.n * 4 + 4)
                        sp.dma_start(rows_z[bass.ds(s.n * P, P), :], z4[:, s.slot]).then_inc(put[s.slot], 16)
                    sweep(sp, G, 4, NC, body, 0)
                    for i in range(NC):
                        sp.wait_ge(put[i], (G - i + NC - 1) // NC * 16)
        moe.close()

        NT2 = most_tiles(TOK)
        assert NT2 > G
        table2 = sb("table2", [P, NT2], U32)
        expert2 = sb("expert2", [P, NT2], I32)
        slot2 = sb("slot2", [P, 1, G], U32)
        rows_f = nc.dram_tensor("rows_f", [NT2 * P, D], F32).ap()
        ws12 = sb("ws12", [P, 2, KD, H])
        ws3 = sb("ws3", [P, HC, D])
        ld_s = sem("ld_s")
        with nc.Block() as block:
            @block.sync
            def _(sp):
                for i, w in enumerate((w1s, w2s)):
                    sp.dma_start(ws12[:, i], w.rearrange("(k p) h -> p k h", p=P)).then_inc(ld_s, 16)
                sp.dma_start(ws3[:], w3s.rearrange("(f p) d -> p f d", p=P)).then_inc(ld_s, 16)
        routing("r2_", 1, NT2, logits2, False, table2, expert2, slot2, None)
        with ExitStack() as fs:
            NF = 2
            HH = HC // 2

            def fb(name, shape, dt=F32):
                return sb(name, shape, dt, fs)
            we12 = fb("we12", [P, NF, 2, KD, H])
            we3 = fb("we3", [P, NF, HC, D])
            pick = fb("pick_f", [P, NF, 1], U32)
            zs, zr = fb("zs", [P, NF, D]), fb("zr", [P, NF, D])
            zT = fb("zT_f", [P, NF, 2, KD, P])
            act_g = fb("act_g", [P, 2, HH * P])
            hT = fb("hT_f", [P, 2, HC, P])
            yr = fb("yr", [P, NF, D])
            bZ = banks[0]
            bU, bG = banks[1:3], banks[3:5]
            bY = banks[5:7]
            pe_z, pe_u, pe_g, pe_y, ac_z, ac_g, dv_h, dv_y = (sem("f_" + n) for n in (
                "pe_z pe_u pe_g pe_y ac_z ac_g dv_h dv_y").split())
            got_s = [sem(f"f_got_s{i}") for i in range(NF)]
            got_r = [sem(f"f_got_r{i}") for i in range(NF)]
            got_w = [sem(f"f_got_w{i}") for i in range(NF)]
            put = [sem(f"f_put{i}") for i in range(NF)]

            def unit_r(s):
                if isinstance(s.n, int) and s.n >= G:
                    return G + s.n, (G + s.n) % 2
                return s.n * 2 + 1, 1

            def fsweep(eng, body, last):
                trips = (G - 1 - 2) // NF
                for i in range(2):
                    body(Step(0, i, NF))
                with eng.Fori(0, trips) as trip:
                    for b in range(NF):
                        body(Step(trip, 2 + b, NF))
                for i in range(2 + trips * NF, last):
                    body(Step(0, i, NF))

            with nc.Block() as block:
                @block.sync
                def _(sp):
                    def body(s):
                        e = sp.value_load(expert2[0:1, bass.ds(s.n, 1)], min_val=0, max_val=E - 1)
                        p = s.back(NF, NT2)
                        if p:
                            sp.wait_ge(pe_g, unit_r(p)[0] * 2 + 2)
                        for i, w in enumerate((W1, W2)):
                            sp.dma_start(we12[:, s.slot, i], w[e].rearrange("(k p) h -> p k h", p=P)).then_inc(got_w[s.slot], 16)
                        if p:
                            sp.wait_ge(pe_y, unit_r(p)[0] + 1)
                        sp.dma_start(we3[:, s.slot], W3[e].rearrange("(f p) d -> p f d", p=P)).then_inc(got_w[s.slot], 16)
                    fsweep(sp, body, NT2)

                @block.gpsimd
                def _(pool):
                    def body(s):
                        need(pool, pe_z, s.n - NF + 1)
                        nc.gpsimd.tensor_copy(pick[:, s.slot], table2[:, bass.ds(s.n, 1)])
                        pool.drain()
                        nc.gpsimd.indirect_dma_start(out=zr[:, s.slot], out_offset=None, in_=rows_z[:, :],
                                                     in_offset=bass.IndirectOffsetOnAxis(ap=pick[:, s.slot], axis=0)
                                                     ).then_inc(got_r[s.slot], 16)
                        if s.back(0, G):
                            pool.dma_start(zs[:, s.slot], rows_z[bass.ds(s.n * P, P), :]).then_inc(got_s[s.slot], 16)
                        w = s.back(NF, NT2)
                        if w:
                            store(w)

                    def store(w):
                        pool.wait_ge(dv_y, unit_r(w)[0] + 1)
                        pool.dma_start(rows_f[bass.ds(w.n * P, P), :], yr[:, w.slot]).then_inc(put[w.slot], 16)
                    fsweep(pool, body, NT2)
                    for i in (NT2 - 2, NT2 - 1):
                        store(Step(0, i, NF))
                    for i in range(NF):
                        pool.wait_ge(put[i], (NT2 - i + NF - 1) // NF * 16)

                @block.tensor
                def _(pe):
                    pe.wait_ge(ld_s, 16 * 3)

                    def transpose_z(s):
                        need(pe, ac_z, s.n)
                        pe.wait_ge(got_r[s.slot], s.lap * 16 + 16)
                        pairs = [(1, zr)]
                        if s.back(0, G):
                            pe.wait_ge(got_s[s.slot], s.lap * 16 + 16)
                            pairs.append((0, zs))
                        for i, z in pairs:
                            for k in range(KD):
                                last = nc.tensor.transpose(bZ[:, (i * KD + k) * P:(i * KD + k + 1) * P],
                                                           z[:, s.slot, k * P:(k + 1) * P], ident[:])
                        last.then_inc(pe_z, 1)

                    def hidden(s, u, routed):
                        w12 = we12[:, s.slot] if routed else ws12[:]
                        for half in range(2):
                            for i, (bank, done, free) in enumerate(((bU, pe_u, ac_g), (bG, pe_g, dv_h))):
                                need(pe, free, u * 2 + half - 1)
                                for f in range(HH):
                                    col0 = (half * HH + f) * P
                                    for k in range(KD):
                                        last = nc.tensor.matmul(bank[half][:, f * P:(f + 1) * P],
                                                                w12[:, i, k, col0:col0 + P], zT[:, s.slot, int(routed), k],
                                                                start=k == 0, stop=k == KD - 1)
                                last.then_inc(done, 1)

                    def down(s, u, parity, routed):
                        w3 = we3[:, s.slot] if routed else ws3[:]
                        pe.wait_ge(dv_h, u * 2 + 2)
                        need(pe, dv_y, u - 1)
                        for f in range(HC):
                            last = nc.tensor.matmul(bY[parity][:, 0:D], hT[:, parity, f], w3[:, f], start=f == 0, stop=f == HC - 1)
                        last.then_inc(pe_y, 1)

                    def body(s):
                        pe.wait_ge(ac_z, s.n + 1)
                        shared, before, after = s.back(0, G), s.back(1, NT2), s.back(-1, NT2)
                        if shared:
                            hidden(s, s.n * 2, False)
                        else:
                            pe.wait_ge(got_w[s.slot], s.lap * 48 + 48)
                            hidden(s, unit_r(s)[0], True)
                        if before:
                            down(before, *unit_r(before), True)
                        if after:
                            transpose_z(after)
                        if shared:
                            pe.wait_ge(got_w[s.slot], s.lap * 48 + 48)
                            hidden(s, unit_r(s)[0], True)
                            down(s, s.n * 2, 0, False)
                    transpose_z(Step(0, 0, NF))
                    fsweep(pe, body, NT2)
                    s = Step(0, NT2 - 1, NF)
                    down(s, *unit_r(s), True)

                @block.scalar
                def _(act):
                    def copy_z(s):
                        act.wait_ge(pe_z, s.n + 1)
                        p = s.back(NF, NT2)
                        if p:
                            act.wait_ge(pe_g, unit_r(p)[0] * 2 + 2)
                        i = 0 if s.back(0, G) else 1
                        nc.scalar.activation(zT[:, s.slot, i:2].rearrange("p i k t -> p (i k t)"), bZ[:, i * KD * P:],
                                             ACT.Copy).then_inc(ac_z, 1)

                    def gelus(u):
                        for half in range(2):
                            act.wait_ge(pe_u, u * 2 + half + 1)
                            need(act, dv_h, u * 2 + half - 1)
                            nc.scalar.activation(act_g[:, half], bU[half][:], ACT.Gelu).then_inc(ac_g, 1)

                    def body(s):
                        shared, after = s.back(0, G), s.back(-1, NT2)
                        gelus(s.n * 2 if shared else unit_r(s)[0])
                        if after:
                            copy_z(after)
                        if shared:
                            gelus(unit_r(s)[0])
                    copy_z(Step(0, 0, NF))
                    fsweep(act, body, NT2)

                @block.vector
                def _(dve):
                    def products(u, parity):
                        for half in range(2):
                            dve.wait_ge(ac_g, u * 2 + half + 1)
                            dve.wait_ge(pe_g, u * 2 + half + 1)
                            if half == 0:
                                need(dve, pe_y, u - 1)
                            nc.vector.tensor_tensor(hT[:, parity, half * HH:(half + 1) * HH].rearrange("p f t -> p (f t)"),
                                                    bG[half][:], act_g[:, half], ALU.mult).then_inc(dv_h, 1)

                    def take(s, u, parity, routed):
                        dve.wait_ge(pe_y, u + 1)
                        if routed:
                            need(dve, put[s.slot], s.lap * 16)
                            nc.vector.tensor_copy(yr[:, s.slot], bY[parity][:, 0:D]).then_inc(dv_y, 1)
                        else:
                            nc.vector.tensor_tensor(xz[:, s.n], bY[parity][:, 0:D], xz[:, s.n], ALU.add).then_inc(dv_y, 1)

                    def body(s):
                        shared, before = s.back(0, G), s.back(1, NT2)
                        if shared:
                            products(s.n * 2, 0)
                        else:
                            products(*unit_r(s))
                        if before:
                            take(before, *unit_r(before), True)
                        if shared:
                            products(*unit_r(s))
                            take(s, s.n * 2, 0, False)
                    fsweep(dve, body, NT2)
                    s = Step(0, NT2 - 1, NF)
                    take(s, *unit_r(s), True)

        with ExitStack() as es:
            NE = 4
            yg = sb("yg", [P, NE, D], where=es)
            got = [sem(f"e_got{i}") for i in range(NE)]
            e_sum, e_out = sem("e_sum"), sem("e_out")
            with nc.Block() as block:
                @block.gpsimd
                def _(pool):
                    for c in range(G):
                        need(pool, e_sum, c - NE + 1)
                        nc.gpsimd.indirect_dma_start(out=yg[:, c % NE], out_offset=None, in_=rows_f[:, :],
                                                     in_offset=bass.IndirectOffsetOnAxis(ap=slot2[:, 0, c:c + 1], axis=0)
                                                     ).then_inc(got[c % NE], 16)

                @block.vector
                def _(dve):
                    for c in range(G):
                        dve.wait_ge(got[c % NE], (c // NE + 1) * 16)
                        nc.vector.tensor_tensor(xz[:, c], xz[:, c], yg[:, c % NE], ALU.add).then_inc(e_sum, 1)

                @block.sync
                def _(sp):
                    for c in range(G):
                        sp.wait_ge(e_sum, c + 1)
                        sp.dma_start(out_nat[c], xz[:, c]).then_inc(e_out, 16)
                    sp.wait_ge(e_out, 16 * G)


_INS = ['x', 'ctx_1024'] + ['L0_xattn_' + m + n for n in 'qkvo' for m in ('W', 'b', 'A', 'B')] + [
    'L0_attn_' + n for n in ('ln1_g', 'ln1_b', 'ln2_g', 'ln2_b', 'tm_mu_k', 'tm_mu_v', 'tm_mu_r', 'time_decay',
                             'time_first', 'Wk', 'Wv', 'Wr', 'Wo', 'router_w', 'cm_mu_k', 'cm_mu_r', 'eWk', 'eWv',
                             'eWr')] + ['L0_ffn_' + n for n in ('w1s', 'w2s', 'w3s', 'W1', 'W2', 'W3', 'Wg')]


def kernel(**inputs):
    import numpy as _np
    import concourse.bacc as _bacc
    from concourse import mybir as _mybir
    from concourse.bass_utils import run_bass_kernel_spmd as _run

    nc = _bacc.Bacc("TRN2", target_bir_lowering=False, num_devices=1)
    arrays, args = {}, []
    for name in _INS:
        a = _np.ascontiguousarray(inputs[name])
        arrays[f"in_{name}_dram"] = a
        args.append(nc.dram_tensor(f"in_{name}_dram", a.shape, _mybir.dt.from_np(a.dtype), kind="ExternalInput").ap())
    shape = inputs['x'].shape
    args.append(nc.dram_tensor("out_0_dram", shape, _mybir.dt.float32, kind="ExternalOutput").ap())
    perceiver_block(nc, *args)
    r = _run(nc, [arrays], core_ids=[0])
    return r.results[0]["out_0_dram"]
```

```python
from contextlib import ExitStack

import concourse.bass as bass
from concourse import mybir

P = 128
F32 = mybir.dt.float32
I32 = mybir.dt.int32
U32 = mybir.dt.uint32
ALU = mybir.AluOpType
ACT = mybir.ActivationFunctionType
AX = mybir.AxisListType.X
EPS = 1e-5
LORA_SCALE = 2.0
NEG = -1e30
R_LOW = 80.0


class Step:

    def __init__(self, trip, offset, ring):
        self.trip, self.offset, self.ring = trip, offset, ring
        self.n = trip * ring + offset
        self.slot = offset % ring
        self.lap = trip + offset // ring

    def back(self, k, count):
        s = Step(self.trip, self.offset - k, self.ring)
        return s if not isinstance(s.n, int) or 0 <= s.n < count else None


def sweep(eng, total, peel, ring, body, tail):
    trips = (total - peel - tail) // ring
    for i in range(peel):
        body(Step(0, i, ring))
    with eng.Fori(0, trips) as trip:
        for b in range(ring):
            body(Step(trip, peel + b, ring))
    for i in range(peel + trips * ring, total):
        body(Step(0, i, ring))


def need(eng, sem, value):
    if not isinstance(value, int) or value > 0:
        eng.wait_ge(sem, value)


class Order:

    def __init__(self, eng, sem, per, step=0):
        self.eng, self.sem, self.per, self.step, self.k = eng, sem, per, step, 0

    def then(self, ins):
        ins.then_inc(self.sem, 1)
        self.k += 1

    def settle(self):
        self.eng.drain()

    def link(self, ins):
        self.then(ins)
        self.settle()

    def close(self):
        assert self.k == self.per, (self.k, self.per)


def perceiver_block(nc, x_in, ctx_in, Wq, bq, Aq, Bq, Wk, bk, Ak, Bk, Wv, bv, Av, Bv, Wo, bo, Ao, Bo,
                    ln1_g, ln1_b, ln2_g, ln2_b, mu_k, mu_v, mu_r, decay, first, tWk, tWv, tWr, tWo,
                    router_w, cm_mu_k, cm_mu_r, eWk, eWv, eWr, w1s, w2s, w3s, W1, W2, W3, Wg, out):
    BATCH, S, D = x_in.shape
    T = ctx_in.shape[1]
    KD = D // P
    G = BATCH * S // P
    BG = P // S
    TC = (T - 1) // P
    R = Aq.shape[0]
    E = eWk.shape[0]
    FK = eWk.shape[2]
    FKC = FK // P
    H = W1.shape[2]
    HC = H // P
    TOK = BATCH * S
    OWN = P + BG
    SP1 = S + 1
    PAD = KD * BG * SP1
    assert T == TC * P + 1 and TC == 2 and KD == 2 and BG == 4

    x_nat = x_in.rearrange("b s d -> (b s) d").rearrange("(c p) d -> p c d", p=P)
    out_nat = out.rearrange("b s d -> (b s) d").rearrange("(c p) d -> c p d", p=P)

    cx = ExitStack()
    with cx, nc.allow_non_contiguous_dma(reason="per-channel vectors, one element a partition"):
        def sb(name, shape, dt=F32, where=cx):
            return where.enter_context(nc.sbuf_tensor(name, shape, dt))

        def sem(name):
            return cx.enter_context(nc.semaphore(name))

        banks = [cx.enter_context(nc.psum_tensor(f"bank{i}", [P, 512], F32)) for i in range(8)]

        def col(v):
            return v.rearrange("(k p) -> p k", p=P)

        def row(v):
            return v.partition_broadcast(P)

        ident = sb("ident", [P, P])
        eps_pow = sb("eps_pow", [P, 1])
        x1 = sb("x1", [P, G, D])
        a_x2 = sb("a_x2", [P, G, D])
        xz = sb("xz", [P, G, D])
        iota_e = sb("iota_e", [P, E])
        iota_p = sb("iota_p", [P, P])
        tile_lo = sb("tile_lo", [P, G])
        token_id = sb("token_id", [P, G])
        before_m = sb("before_m", [P, P])
        ones_m = sb("ones_m", [P, P])
        chunk_on = sb("chunk_on", [P, E, G])
        logits2 = sb("logits2", [P, G, E])
        mixed_w = sb("mixed_w", [P, 3, KD, 2, D])
        t_wo = sb("t_wo", [P, KD, D])
        r_w = sb("r_w", [P, KD, E])
        mu = sb("mu", [P, 3, KD])
        one_mu = sb("one_mu", [P, 3, KD])
        g1 = sb("g1", [P, KD])
        b1 = sb("b1", [P, KD])
        g2 = sb("g2", [P, D])
        b2 = sb("b2", [P, D])
        wd = sb("wd", [P, KD])
        wneg = sb("wneg", [P, KD])
        u_c = sb("u_c", [P, KD])
        keep = sb("keep", [P, 1])
        zero_row = sb("zero_row", [1, D])
        w_pad = sb("w_pad", [P, KD, BG, SP1])
        ld_y, ld_yc, wneg_done, zero_out = (sem(n) for n in ("ld_y", "ld_yc", "wneg_done", "zero_out"))

        xs = ExitStack()
        with xs:
            def xb(name, shape, dt=F32):
                return sb(name, shape, dt, xs)
            w_nat = xb("w_nat", [P, 4, KD, D])
            w_T = xb("w_T", [P, 4, KD, D])
            lora_a = xb("lora_a", [R, 4, D])
            lora_b = xb("lora_b", [P, 4, KD, R])
            lora_bT = xb("lora_bT", [R, 4, KD, P])
            bq_c = xb("bq_c", [P, KD])
            bk_c = xb("bk_c", [P, KD])
            bv_b = xb("bv_b", [P, D])
            bo_b = xb("bo_b", [P, D])
            last_nat = xb("last_nat", [BATCH, D])
            last_T = xb("last_T", [P, KD, BATCH])
            v_last = xb("v_last", [BG, G, D])
            mask_l = xb("mask_l", [BG, P])
            mask_r = xb("mask_r", [BG, OWN])
            N3 = 3
            ctx_sb = xb("ctx_sb", [P, N3, BG, TC * D])
            kT = xb("kT", [P, N3, BG, KD * TC * P])
            hn = xb("hn", [P, N3, D])
            hnT = xb("hnT", [P, N3, KD, P])
            qT = xb("qT", [P, N3, KD, P])
            k_own = xb("k_own", [P, N3, KD, OWN])
            v_own = xb("v_own", [P, N3, D])
            vl = xb("vl", [BG, N3, D])
            prob = xb("prob", [P, N3, TC * P + OWN])
            probT = xb("probT", [P, N3, 4, P])
            oT = xb("oT", [P, N3, KD, P])
            o_nat = xb("o_nat", [P, N3, D])
            st0 = xb("st0", [P, N3, 6])
            mv0 = xb("mv0", [P, N3, 2])
            var0 = xb("var0", [P, N3, 1])
            rs0 = xb("rs0", [P, N3, 1])
            st1 = xb("st1", [P, 2, N3, 6])
            mv1 = xb("mv1", [P, 2, N3, 2])
            var1 = xb("var1", [P, 2, N3, 1])
            rs1 = xb("rs1", [P, 2, N3, 1])
            smx = xb("smx", [P, N3, 1])
            snm = xb("snm", [P, N3, 1])
            ssum = xb("ssum", [P, N3, 1])
            srec = xb("srec", [P, N3, 1])

            bT0, bT1, bPT, bQ, bV, bS, bO, bW = banks
            ld_x, ld_w, ld_l, ld_lora, ld_b = (sem(n) for n in ("ld_x", "ld_w", "ld_l", "ld_lora", "ld_b"))
            ld_ctx = [sem(f"ld_ctx{i}") for i in range(N3)]
            const_ord = sem("const_ord")
            pe_set, dv_set = sem("pe_set"), sem("dv_set")
            pe_t0, pe_t1, pe_q, pe_v, pe_s, pe_pt, pe_o, pe_w = (sem(n) for n in (
                "pe_t0", "pe_t1", "pe_q", "pe_v", "pe_s", "pe_pt", "pe_o", "pe_w"))
            dv_t0, dv_v, dv_o, dv_w, dv_ln0, dv_ln1, dv_max = (sem(n) for n in (
                "dv_t0", "dv_v", "dv_o", "dv_w", "dv_ln0", "dv_ln1", "dv_max"))
            ac_t1, ac_q, ac_exp, ac_pt, ac_o = (sem(n) for n in ("ac_t1", "ac_q", "ac_exp", "ac_pt", "ac_o"))
            po_r0, po_r1, po_xb, po_last = (sem(n) for n in ("po_r0", "po_r1", "po_xb", "po_last"))
            CONSTS = 8
            STEPS = G + 3

            with nc.Block() as block:
                @block.sync
                def _(sp):
                    sp.dma_start(xz[:], x_nat).then_inc(ld_x, 16)
                    for i, w in enumerate((Wq, Wk, Wv, Wo)):
                        sp.dma_start(w_nat[:, i], w.rearrange("(k p) i -> p k i", p=P)).then_inc(ld_w, 16)
                    sp.dma_start(bv_b[:], row(bv)).then_inc(ld_w, 16)
                    sp.dma_start(bo_b[:], row(bo)).then_inc(ld_w, 16)
                    sp.dma_start(last_nat[:], ctx_in[:, T - 1, :]).then_inc(ld_l, 16)
                    sp.dma_start(v_last[:], ctx_in[:, T - 1, :].rearrange("(g j) d -> j g d", j=BG)).then_inc(ld_l, 16)

                    def load(s):
                        need(sp, pe_o, s.n - N3 + 1)
                        src = ctx_in[bass.ds(s.n * BG, BG), 0:TC * P, :].rearrange("j (p c) d -> p j (c d)", c=TC)
                        sp.dma_start(ctx_sb[:, s.slot], src).then_inc(ld_ctx[s.slot], 16)
                    for c in range(N3):
                        load(Step(0, c, N3))
                    for i, w in enumerate((tWk, tWv, tWr)):
                        sp.dma_start(mixed_w[:, i, :, 1], w.rearrange("(k p) o -> p k o", p=P)).then_inc(ld_y, 16)
                    sp.dma_start(t_wo[:], tWo.rearrange("(k p) o -> p k o", p=P)).then_inc(ld_y, 16)
                    sp.dma_start(r_w[:], router_w.rearrange("(k p) o -> p k o", p=P)).then_inc(ld_y, 16)
                    sp.dma_start(g2[:], row(ln2_g)).then_inc(ld_y, 16)
                    sp.dma_start(b2[:], row(ln2_b)).then_inc(ld_y, 16)
                    with sp.Fori(0, (G - N3) // N3) as trip:
                        for c in range(N3):
                            load(Step(trip, N3 + c, N3))
                    for c in range(G - (G - N3) % N3, G):
                        load(Step(0, c, N3))

                @block.gpsimd
                def _(pool):
                    o = Order(pool, const_ord, CONSTS)
                    o.then(nc.gpsimd.memset(ident[:], 0.0))
                    o.then(nc.gpsimd.memset(mask_l[:], 0.0))
                    o.then(nc.gpsimd.memset(mask_r[:], NEG))
                    o.then(nc.gpsimd.memset(eps_pow[:], -0.5))
                    o.settle()
                    o.then(nc.gpsimd.affine_select(out=ident[:], in_=ident[:], compare_op=ALU.not_equal, fill=1.0,
                                                   base=0, pattern=[[-1, P]], channel_multiplier=1))
                    for m, n, f in ((mask_l[:], P, 1.0), (mask_r[:, 0:P], P, 0.0)):
                        v = m.rearrange("a (j s) -> a j s", j=BG)
                        o.then(nc.gpsimd.affine_select(out=v, in_=v, compare_op=ALU.not_equal, fill=f, base=0,
                                                       pattern=[[-1, BG], [0, S]], channel_multiplier=1))
                    v = mask_r[:, P:OWN]
                    o.then(nc.gpsimd.affine_select(out=v, in_=v, compare_op=ALU.not_equal, fill=0.0, base=0,
                                                   pattern=[[-1, BG]], channel_multiplier=1))
                    o.settle()
                    o.close()
                    pool.wait_ge(ld_w, 16 * 6)
                    pool.wait_ge(ld_l, 32)
                    pool.wait_ge(dv_set, 3)

                    def time_mix_constants(part):
                        if part == 0:
                            pool.wait_ge(ld_y, 16 * 7)
                            pool.wait_ge(ld_yc, 16 * 7)
                            nc.gpsimd.tensor_scalar(one_mu[:], mu[:], -1.0, 1.0, ALU.mult, ALU.add)
                            nc.gpsimd.memset(zero_row[:], 0.0)
                            nc.gpsimd.memset(keep[:], 1.0)
                            nc.gpsimd.memset(w_pad[:], 0.0)
                            for j in range(BG):
                                pool.drain()
                                nc.gpsimd.affine_select(out=keep[:], in_=keep[:], compare_op=ALU.not_equal, fill=0.0,
                                                        base=-(j * S + S - 1), pattern=[[0, 1]], channel_multiplier=1)
                            pool.wait_ge(wneg_done, 1)
                            for k in range(KD):
                                nc.gpsimd.tensor_scalar(w_pad[:, k], w_pad[:, k], wneg[:, k:k + 1], None, ALU.add)
                            pool.drain()
                            nc.gpsimd.memset(w_pad[:, :, :, 0:1], NEG)
                        else:
                            i = part - 1
                            for k in range(KD):
                                for h, m in enumerate((mu, one_mu)):
                                    nc.gpsimd.tensor_scalar(mixed_w[:, i, k, h], mixed_w[:, i, k, 1], m[:, i, k:k + 1],
                                                            None, ALU.mult)

                    def rstd0(s):
                        pool.wait_ge(dv_ln0, s.n * 4 + 3)
                        nc.gpsimd.tensor_tensor(rs0[:, s.slot], var0[:, s.slot], eps_pow[:], ALU.pow).then_inc(po_r0, 1)

                    def body(s):
                        if s.back(0, G):
                            if s.back(-1, G):
                                rstd0(s.back(-1, G))
                            need(pool, pe_s, s.n - N3 + 1)
                            nc.gpsimd.tensor_copy(k_own[:, s.slot, :, P:OWN], last_T[:, :, bass.ds(s.n * BG, BG)])
                            need(pool, pe_o, s.n - N3 + 1)
                            nc.gpsimd.tensor_copy(vl[:, s.slot], v_last[:, s.n]).then_inc(po_last, 1)
                            pool.wait_ge(dv_ln0, s.n * 4 + 4)
                            nc.gpsimd.tensor_tensor(xz[:, s.n], xz[:, s.n], bo_b[:], ALU.add).then_inc(po_xb, 1)
                        c = s.back(3, G)
                        if c:
                            for h in range(2):
                                pool.wait_ge(dv_ln1, c.n * 8 + 4 * h + 3)
                                nc.gpsimd.tensor_tensor(rs1[:, h, c.slot], var1[:, h, c.slot], eps_pow[:],
                                                        ALU.pow).then_inc(po_r1, 1)
                        if isinstance(s.n, int) and s.n < 4:
                            time_mix_constants(s.n)
                    rstd0(Step(0, 0, N3))
                    sweep(pool, STEPS, 4, N3, body, 4)

                @block.tensor
                def _(pe):
                    pe.wait_ge(const_ord, CONSTS)
                    pe.wait_ge(ld_w, 16 * 6)
                    pe.wait_ge(ld_lora, 16 * 8)
                    pe.wait_ge(ld_l, 32)
                    for i in range(4):
                        for k in range(KD):
                            nc.tensor.transpose(banks[i // 2][0:R, (i % 2 * KD + k) * P:(i % 2 * KD + k + 1) * P],
                                                lora_b[:, i, k], ident[:]).then_inc(pe_set, 1)
                    for k in range(KD):
                        nc.tensor.transpose(banks[2][:, k * BATCH:(k + 1) * BATCH], last_nat[:, k * P:(k + 1) * P],
                                            ident[0:BATCH, 0:BATCH]).then_inc(pe_set, 1)
                    pe.wait_ge(dv_set, 2)
                    for i in range(4):
                        for ki in range(KD):
                            for ko in range(KD):
                                o = banks[3 + i][:, ki * D + ko * P:ki * D + (ko + 1) * P]
                                nc.tensor.matmul(o, w_nat[:, i, ko, ki * P:(ki + 1) * P], ident[:], start=True, stop=False)
                                nc.tensor.matmul(o, lora_a[:, i, ki * P:(ki + 1) * P], lora_bT[:, i, ko],
                                                 start=False, stop=True).then_inc(pe_set, 1)
                    pe.wait_ge(dv_set, 7)

                    def hidden_T(s):
                        pe.wait_ge(dv_ln0, s.n * 4 + 4)
                        need(pe, dv_t0, s.n * 3)
                        for k in range(KD):
                            last = nc.tensor.transpose(bT0[:, k * P:(k + 1) * P], hn[:, s.slot, k * P:(k + 1) * P], ident[:])
                        last.then_inc(pe_t0, 1)

                    def context_T(s, j):
                        if j == 0:
                            pe.wait_ge(ld_ctx[s.slot], s.lap * 16 + 16)
                        if j % 2 == 0:
                            need(pe, ac_t1, s.n * 2 + j // 2)
                        else:
                            need(pe, dv_t0, s.n * 3 + 1 + j // 2)
                        for k in range(KD):
                            for c in range(TC):
                                last = nc.tensor.transpose((bT1, bT0)[j % 2][:, (k * TC + c) * P:(k * TC + c + 1) * P],
                                                           ctx_sb[:, s.slot, j, c * D + k * P:c * D + (k + 1) * P],
                                                           ident[:])
                        last.then_inc((pe_t1, pe_t0)[j % 2], 1)

                    def query_key(s):
                        pe.wait_ge(dv_t0, s.n * 3 + 1)
                        need(pe, ac_q, s.n)
                        for i in range(2):
                            for m in range(KD):
                                for k in range(KD):
                                    last = nc.tensor.matmul(bQ[:, (i * KD + m) * P:(i * KD + m + 1) * P],
                                                            w_T[:, i, k, m * P:(m + 1) * P], hnT[:, s.slot, k],
                                                            start=k == 0, stop=k == KD - 1)
                        last.then_inc(pe_q, 1)

                    def value(s):
                        need(pe, dv_v, s.n)
                        for k in range(KD):
                            last = nc.tensor.matmul(bV[:, 0:D], hnT[:, s.slot, k], w_T[:, 2, k], start=k == 0, stop=k == KD - 1)
                        last.then_inc(pe_v, 1)

                    def scores(s):
                        pe.wait_ge(ac_q, s.n + 1)
                        pe.wait_ge(po_last, s.n + 1)
                        need(pe, ac_exp, s.n)
                        own = bS[:, TC * P:TC * P + OWN]
                        for k in range(KD):
                            nc.tensor.matmul(own, qT[:, s.slot, k], k_own[:, s.slot, k], start=k == 0, stop=False)
                        nc.tensor.matmul(own, mask_l[:], mask_r[:], start=False, stop=True)
                        pe.wait_ge(ac_t1, s.n * 2 + 2)
                        pe.wait_ge(dv_t0, s.n * 3 + 3)
                        for j in range(BG):
                            for k in range(KD):
                                last = nc.tensor.matmul(bS[j * S:(j + 1) * S, 0:TC * P], qT[:, s.slot, k, j * S:(j + 1) * S],
                                                        kT[:, s.slot, j, k * TC * P:(k + 1) * TC * P],
                                                        start=k == 0, stop=k == KD - 1)
                        last.then_inc(pe_s, 1)

                    def prob_T(s):
                        pe.wait_ge(ac_exp, s.n + 1)
                        need(pe, ac_pt, s.n)
                        for c in range(3):
                            nc.tensor.transpose(bPT[:, c * P:(c + 1) * P], prob[:, s.slot, c * P:(c + 1) * P], ident[:])
                        nc.tensor.transpose(bPT[0:BG, 3 * P:4 * P], prob[:, s.slot, 3 * P:3 * P + BG],
                                            ident[:]).then_inc(pe_pt, 1)

                    def values(s):
                        pe.wait_ge(ac_pt, s.n + 1)
                        pe.wait_ge(dv_v, s.n + 1)
                        need(pe, dv_o, s.n * 2)
                        nc.tensor.matmul(bO[:, 0:D], probT[:, s.slot, 2], v_own[:, s.slot], start=True, stop=False)
                        nc.tensor.matmul(bO[:, 0:D], probT[0:BG, s.slot, 3], vl[:, s.slot], start=False, stop=False)
                        for c in range(TC):
                            for j in range(BG):
                                last = nc.tensor.matmul(bO[j * S:(j + 1) * S, 0:D], probT[:, s.slot, c, j * S:(j + 1) * S],
                                                        ctx_sb[:, s.slot, j, c * D:(c + 1) * D],
                                                        start=False, stop=c == TC - 1)
                        last.then_inc(pe_o, 1)

                    def out_T(s):
                        pe.wait_ge(dv_o, s.n * 2 + 2)
                        need(pe, dv_w, s.n)
                        for k in range(KD):
                            last = nc.tensor.transpose(bW[:, k * P:(k + 1) * P], o_nat[:, s.slot, k * P:(k + 1) * P], ident[:])
                        last.then_inc(pe_w, 1)

                    def project(s):
                        pe.wait_ge(ac_o, s.n + 1)
                        for k in range(KD):
                            last = nc.tensor.matmul(bW[:, 0:D], oT[:, s.slot, k], w_T[:, 3, k], start=k == 0, stop=k == KD - 1)
                        last.then_inc(pe_w, 1)

                    def body(s):
                        a, b, c = s.back(0, G), s.back(1, G), s.back(2, G)
                        if a:
                            hidden_T(a)
                        if c:
                            out_T(c)
                        if a:
                            context_T(a, 0)
                            context_T(a, 1)
                            query_key(a)
                            context_T(a, 2)
                        if b:
                            prob_T(b)
                        if a:
                            value(a)
                            context_T(a, 3)
                        if c:
                            project(c)
                        if b:
                            values(b)
                        if a:
                            scores(a)
                    sweep(pe, STEPS, 4, N3, body, 4)

                @block.scalar
                def _(act):
                    for i, w in enumerate((Aq, Ak, Av, Ao)):
                        act.dma_start(lora_a[:, i], w).then_inc(ld_lora, 16)
                    for i, w in enumerate((Bq, Bk, Bv, Bo)):
                        act.dma_start(lora_b[:, i], w.rearrange("(k p) r -> p k r", p=P)).then_inc(ld_lora, 16)
                    act.dma_start(bq_c[:], col(bq)).then_inc(ld_b, 16)
                    act.dma_start(bk_c[:], col(bk)).then_inc(ld_b, 16)
                    for i, m in enumerate((mu_k, mu_v, mu_r)):
                        act.dma_start(mu[:, i], col(m)).then_inc(ld_yc, 16)
                    for t, v in ((g1, ln1_g), (b1, ln1_b), (wd, decay), (u_c, first)):
                        act.dma_start(t[:], col(v)).then_inc(ld_yc, 16)
                    act.wait_ge(ld_b, 32)
                    act.wait_ge(ld_yc, 16 * 7)
                    nc.scalar.activation(wneg[:], wd[:], ACT.Exp)
                    act.drain()
                    nc.scalar.mul(wneg[:], wneg[:], -1.0).then_inc(wneg_done, 1)

                    def context(s, j):
                        act.wait_ge(pe_t1, s.n * 2 + j // 2 + 1)
                        need(act, pe_s, s.n - N3 + 1)
                        nc.scalar.activation(kT[:, s.slot, j], bT1[:], ACT.Copy).then_inc(ac_t1, 1)

                    def body(s):
                        a, b, c = s.back(0, G), s.back(1, G), s.back(2, G)
                        if c:
                            act.wait_ge(pe_w, c.n * 2 + 1)
                            nc.scalar.activation(oT[:, c.slot].rearrange("p k t -> p (k t)"), bW[:, 0:D], ACT.Copy).then_inc(ac_o, 1)
                        if a:
                            context(a, 0)
                            act.wait_ge(pe_q, a.n + 1)
                            for k in range(KD):
                                nc.scalar.activation(qT[:, a.slot, k], bQ[:, k * P:(k + 1) * P], ACT.Identity,
                                                     bias=bq_c[:, k:k + 1])
                                last = nc.scalar.activation(k_own[:, a.slot, k, 0:P], bQ[:, (KD + k) * P:(KD + k + 1) * P],
                                                            ACT.Identity, bias=bk_c[:, k:k + 1])
                            last.then_inc(ac_q, 1)
                            context(a, 2)
                        if b:
                            act.wait_ge(pe_pt, b.n + 1)
                            need(act, pe_o, b.n - N3 + 1)
                            nc.scalar.activation(probT[:, b.slot, 0:3], bPT[:, 0:3 * P], ACT.Copy)
                            nc.scalar.activation(probT[0:BG, b.slot, 3], bPT[0:BG, 3 * P:4 * P], ACT.Copy).then_inc(ac_pt, 1)
                        if a:
                            act.wait_ge(dv_max, a.n * 2 + 2)
                            need(act, pe_pt, a.n - N3 + 1)
                            nc.scalar.activation(prob[:, a.slot], bS[:, 0:TC * P + OWN], ACT.Exp, bias=snm[:, a.slot],
                                                 scale=float(D) ** -0.5, accum_out=ssum[:, a.slot]).then_inc(ac_exp, 1)
                    sweep(act, STEPS, 4, N3, body, 4)

                @block.vector
                def _(dve):
                    dve.wait_ge(pe_set, 8)
                    for i in range(2):
                        nc.vector.tensor_scalar(lora_bT[:, 2 * i:2 * i + 2].rearrange("r i k p -> r (i k p)"),
                                                banks[i][0:R, :], LORA_SCALE, None, ALU.mult).then_inc(dv_set, 1)
                    dve.wait_ge(pe_set, 10)
                    nc.vector.tensor_copy(last_T[:].rearrange("p k b -> p (k b)"), banks[2][:, 0:KD * BATCH]).then_inc(dv_set, 1)
                    for i in range(4):
                        dve.wait_ge(pe_set, 10 + 4 * (i + 1))
                        nc.vector.tensor_copy(w_T[:, i].rearrange("p k o -> p (k o)"), banks[3 + i][:]).then_inc(dv_set, 1)

                    def norm_stats(o, src, st, mv, var):
                        o.settle()
                        o.link(nc.vector.bn_stats(st, src))
                        o.link(nc.vector.bn_aggr(mv, st))
                        o.then(nc.vector.tensor_scalar(var, mv[:, 1:2], EPS, None, ALU.add))

                    def norm_apply(o, dst, src, mv, rstd):
                        o.then(nc.vector.tensor_scalar(dst, src, mv[:, 0:1], rstd, ALU.subtract, ALU.mult))

                    def ln0(s):
                        o = Order(dve, dv_ln0, 4, s.n)
                        norm_stats(o, xz[:, s.n], st0[:, s.slot], mv0[:, s.slot], var0[:, s.slot])
                        yield
                        dve.wait_ge(po_r0, s.n + 1)
                        need(dve, pe_t0, (s.n - N3) * 3 + 1)
                        norm_apply(o, hn[:, s.slot], xz[:, s.n], mv0[:, s.slot], rs0[:, s.slot])
                        o.close()
                        yield

                    def copy_T0(s, u, dst, n):
                        dve.wait_ge(pe_t0, s.n * 3 + u + 1)
                        nc.vector.tensor_copy(dst, bT0[:, 0:n]).then_inc(dv_t0, 1)

                    def body(s):
                        a, b, c, d = (s.back(k, G) for k in range(4))
                        n0 = ln0(s.back(-1, G)) if a and s.back(-1, G) else None
                        n1 = None
                        if a:
                            need(dve, pe_v, a.n - N3 + 1)
                            copy_T0(a, 0, hnT[:, a.slot].rearrange("p k t -> p (k t)"), KD * P)
                        if d:
                            n1 = Order(dve, dv_ln1, 8, d.n)
                            norm_stats(n1, x1[:, d.n], st1[:, 0, d.slot], mv1[:, 0, d.slot], var1[:, 0, d.slot])
                        if a:
                            need(dve, pe_s, a.n - N3 + 1)
                            copy_T0(a, 1, kT[:, a.slot, 1], 512)
                        if n0:
                            next(n0)
                        if d:
                            dve.wait_ge(po_r1, d.n * 2 + 1)
                            norm_apply(n1, a_x2[:, d.n], x1[:, d.n], mv1[:, 0, d.slot], rs1[:, 0, d.slot])
                            norm_stats(n1, a_x2[:, d.n], st1[:, 1, d.slot], mv1[:, 1, d.slot], var1[:, 1, d.slot])
                        if n0:
                            next(n0)
                        if a:
                            dve.wait_ge(pe_v, a.n + 1)
                            need(dve, pe_o, a.n - N3 + 1)
                            nc.vector.tensor_tensor(v_own[:, a.slot], bV[:, 0:D], bv_b[:], ALU.add).then_inc(dv_v, 1)
                            copy_T0(a, 2, kT[:, a.slot, 3], 512)
                        if c:
                            dve.wait_ge(pe_w, c.n * 2 + 2)
                            dve.wait_ge(po_xb, c.n + 1)
                            nc.vector.tensor_tensor(x1[:, c.n], bW[:, 0:D], xz[:, c.n], ALU.add).then_inc(dv_w, 1)
                        if d:
                            dve.wait_ge(po_r1, d.n * 2 + 2)
                            norm_apply(n1, xz[:, d.n], a_x2[:, d.n], mv1[:, 1, d.slot], rs1[:, 1, d.slot])
                            n1.close()
                        if b:
                            o = Order(dve, dv_o, 2, b.n)
                            dve.wait_ge(ac_exp, b.n + 1)
                            o.link(nc.vector.reciprocal(srec[:, b.slot], ssum[:, b.slot]))
                            dve.wait_ge(pe_o, b.n + 1)
                            need(dve, pe_w, (b.n - N3) * 2 + 1)
                            o.then(nc.vector.tensor_scalar(o_nat[:, b.slot], bO[:, 0:D], srec[:, b.slot], None, ALU.mult))
                        if a:
                            o = Order(dve, dv_max, 2, a.n)
                            dve.wait_ge(pe_s, a.n + 1)
                            o.link(nc.vector.reduce_max(smx[:, a.slot], bS[:, 0:TC * P + OWN], AX))
                            o.then(nc.vector.tensor_scalar(snm[:, a.slot], smx[:, a.slot], -float(D) ** -0.5, None, ALU.mult))
                    dve.wait_ge(ld_x, 16)
                    dve.wait_ge(ld_w, 16 * 6)
                    first_ln = ln0(Step(0, 0, N3))
                    next(first_ln)
                    next(first_ln)
                    sweep(dve, STEPS, 4, N3, body, 4)

        rows_e = nc.dram_tensor("rows_e", [TOK + 1, 2 * D], F32).ap()
        moe = cx.enter_context(ExitStack())
        ewk_sb = sb("ewk_sb", [P, E, KD, FK], where=moe)
        ewv_sb = sb("ewv_sb", [P, E, FKC, D], where=moe)
        ewr_sb = sb("ewr_sb", [P, E, KD, D], where=moe)
        cm_mu = sb("cm_mu", [P, 2, E, KD], where=moe)
        logits = sb("logits", [P, G, E], where=moe)
        ld_moe = [sem(f"ld_moe{i}") for i in range(4)]
        ei_out = [sem(f"ei_out{i}") for i in range(2)]
        ys = ExitStack()
        with ys:
            def yb(name, shape, dt=F32):
                return sb(name, shape, dt, ys)
            NY = 2
            def pad(name):
                return yb(name, [P, NY, KD, BG, SP1])

            def flat(name):
                return yb(name, [P, NY, KD * P])
            z_in = yb("z_in", [P, NY, D])
            xn, kp, vp, pp, e1b, e2b, evb, aa, bb = (pad(n) for n in (
                "xn", "kp", "vp", "pp", "e1b", "e2b", "evb", "aa", "bb"))
            d1, d2, qq, d3, d4, e1, e2, e2v, e1a, e1bb, er, r_lim, rw = (flat(n) for n in (
                "d1", "d2", "qq", "d3", "d4", "e1", "e2", "e2v", "e1a", "e1bb", "er", "r_lim", "rw"))
            z3 = yb("z3", [P, NY, D])
            ei = yb("ei", [P, NY, D])
            ei_shift = yb("ei_shift", [P, NY, D])
            eiT = yb("eiT", [P, NY, KD, P])
            st3 = yb("st3", [P, NY, 6])
            mv3 = yb("mv3", [P, NY, 2])
            var3 = yb("var3", [P, NY, 1])
            rs3 = yb("rs3", [P, NY, 1])
            bZ, bKV, bR, bX, bE, bL = banks[0:6]
            y_pad = sem("y_pad")
            (pe_z, pe_kv, pe_r, pe_x, pe_e, pe_l,
             ac_zin, ac_z, ac_kv, ac_r, ac_e1b, ac_e2b, ac_e1, ac_e2, ac_ei, ac_sh,
             dv_pp, dv_d1, dv_qq, dv_d3, dv_scan, dv_rw, dv_r, dv_x2, dv_var, dv_z3, dv_lg,
             po_d2, po_d4, po_ev, po_e2v, po_e1a, po_r3, po_ei) = (sem("y_" + n) for n in (
                 "pe_z pe_kv pe_r pe_x pe_e pe_l "
                 "ac_zin ac_z ac_kv ac_r ac_e1b ac_e2b ac_e1 ac_e2 ac_ei ac_sh "
                 "dv_pp dv_d1 dv_qq dv_d3 dv_scan dv_rw dv_r dv_x2 dv_var dv_z3 dv_lg "
                 "po_d2 po_d4 po_ev po_e2v po_e1a po_r3 po_ei").split())
            YSTEPS = G + 6
            YPEEL = 8
            YTAIL = 7

            def body_of(t, s):
                return t[:, s.slot, :, :, 1:SP1].rearrange("p k j s -> p (k j) s")

            def before(t, s):
                return t[:, s.slot, :, :, 0:S].rearrange("p k j s -> p (k j) s")

            def line(t, s):
                return t[:, s.slot].rearrange("p k j s -> p (k j s)")

            def seqs(t, s):
                return t[:, s.slot].rearrange("p (q s) -> p q s", s=S)

            with nc.Block() as block:
                @block.sync
                def _(sp):
                    sp.dma_start(ewk_sb[:], eWk.rearrange("e (k p) f -> p e k f", p=P)).then_inc(ld_moe[0], 16)
                    sp.dma_start(ewr_sb[:], eWr.rearrange("e (k p) f -> p e k f", p=P)).then_inc(ld_moe[1], 16)
                    sp.dma_start(ewv_sb[:], eWv.rearrange("e (k p) f -> p e k f", p=P)).then_inc(ld_moe[2], 16)
                    sp.dma_start(rows_e[0:1, 0:D], zero_row[:]).then_inc(zero_out, 16)

                    def body(s):
                        d = s.back(5, G)
                        if d:
                            sp.wait_ge(po_ei, d.n + 1)
                            sp.dma_start(rows_e[bass.ds(d.n * P, P), D:2 * D], ei[:, d.slot]).then_inc(ei_out[d.slot], 16)
                            sp.wait_ge(ac_sh, d.n + 1)
                            sp.dma_start(rows_e[bass.ds(d.n * P + 1, P), 0:D], ei_shift[:, d.slot]).then_inc(ei_out[d.slot], 16)
                    sweep(sp, YSTEPS, YPEEL, NY, body, YTAIL)
                    sp.wait_ge(zero_out, 16)
                    for i in range(NY):
                        sp.wait_ge(ei_out[i], 32 * G // NY)

                @block.gpsimd
                def _(pool):
                    for t in (xn, e1b, evb, e2b, vp):
                        nc.gpsimd.memset(t[:, :, :, :, 0:1], 0.0)
                    nc.gpsimd.memset(kp[:, :, :, :, 0:1], NEG).then_inc(y_pad, 1)

                    def body(s):
                        w, v, x, d = s.back(2, G), s.back(3, G), s.back(4, G), s.back(5, G)
                        if w:
                            need(pool, ac_e2, w.n - NY + 1)
                            pool.wait_ge(dv_pp, w.n + 1)
                            nc.gpsimd.tensor_tensor(seqs(d2, w), body_of(kp, w), body_of(pp, w), ALU.subtract).then_inc(po_d2, 1)
                        if v:
                            pool.wait_ge(dv_scan, v.n + 1)
                            pool.wait_ge(ac_e1, v.n + 1)
                            need(pool, dv_rw, v.n - NY + 1)
                            nc.gpsimd.tensor_tensor(seqs(e1bb, v), seqs(e1, v), before(bb, v), ALU.mult)
                            nc.gpsimd.tensor_tensor(seqs(e1a, v), seqs(e1, v), before(aa, v), ALU.mult).then_inc(po_e1a, 1)
                        if d:
                            pool.wait_ge(dv_z3, d.n + 1)
                            need(pool, pe_e, d.n - NY + 1)
                            need(pool, ac_sh, d.n - NY + 1)
                            need(pool, ei_out[d.slot], d.lap * 32)
                            nc.gpsimd.tensor_tensor(ei[:, d.slot], z3[:, d.slot], g2[:], ALU.mult)
                            pool.drain()
                            nc.gpsimd.tensor_tensor(ei[:, d.slot], ei[:, d.slot], b2[:], ALU.add).then_inc(po_ei, 1)
                        if w:
                            pool.wait_ge(dv_qq, w.n + 1)
                            nc.gpsimd.tensor_tensor(seqs(d4, w), body_of(kp, w), seqs(qq, w), ALU.subtract).then_inc(po_d4, 1)
                            pool.wait_ge(ac_e2b, w.n + 1)
                            need(pool, dv_scan, w.n - NY + 1)
                            nc.gpsimd.tensor_tensor(body_of(evb, w), body_of(e2b, w), body_of(vp, w), ALU.mult).then_inc(po_ev, 1)
                            pool.wait_ge(ac_e2, w.n + 1)
                            need(pool, dv_rw, w.n - NY + 1)
                            nc.gpsimd.tensor_tensor(seqs(e2v, w), seqs(e2, w), body_of(vp, w), ALU.mult).then_inc(po_e2v, 1)
                        if x:
                            pool.wait_ge(dv_var, x.n + 1)
                            need(pool, dv_z3, x.n - NY + 1)
                            nc.gpsimd.tensor_tensor(rs3[:, x.slot], var3[:, x.slot], eps_pow[:], ALU.pow).then_inc(po_r3, 1)
                    sweep(pool, YSTEPS, YPEEL, NY, body, YTAIL)

                @block.tensor
                def _(pe):
                    def products(s, i):
                        for m in range(KD):
                            o = (bKV, bKV, bR)[i][:, (i % 2 * KD + m) * P:(i % 2 * KD + m + 1) * P]
                            for k in range(KD):
                                for h in range(2):
                                    last = nc.tensor.matmul(o.rearrange("p (j s) -> p j s", j=BG),
                                                            mixed_w[:, i, k, h, m * P:(m + 1) * P],
                                                            xn[:, s.slot, k, :, 1 - h:1 - h + S],
                                                            start=k == 0 and h == 0, stop=k == KD - 1 and h == 1)
                        return last

                    def body(s):
                        a, b, x, g = s.back(0, G), s.back(1, G), s.back(4, G), s.back(6, G)
                        if b:
                            pe.wait_ge(ac_z, b.n + 1)
                            need(pe, ac_kv, b.n)
                            products(b, 0)
                            products(b, 1).then_inc(pe_kv, 1)
                        if a:
                            pe.wait_ge(ac_zin, a.n + 1)
                            need(pe, ac_z, a.n)
                            for k in range(KD):
                                last = nc.tensor.transpose(bZ[:, k * P:(k + 1) * P], z_in[:, a.slot, k * P:(k + 1) * P], ident[:])
                            last.then_inc(pe_z, 1)
                        if g:
                            pe.wait_ge(po_ei, g.n + 1)
                            need(pe, ac_ei, g.n)
                            for k in range(KD):
                                last = nc.tensor.transpose(bE[:, k * P:(k + 1) * P], ei[:, g.slot, k * P:(k + 1) * P], ident[:])
                            last.then_inc(pe_e, 1)
                        if b:
                            need(pe, dv_r, b.n)
                            products(b, 2).then_inc(pe_r, 1)
                        if g:
                            pe.wait_ge(ac_ei, g.n + 1)
                            need(pe, dv_lg, g.n)
                            for k in range(KD):
                                last = nc.tensor.matmul(bL[:, 0:E], eiT[:, g.slot, k], r_w[:, k], start=k == 0, stop=k == KD - 1)
                            last.then_inc(pe_l, 1)
                        if x:
                            pe.wait_ge(dv_rw, x.n + 1)
                            need(pe, dv_x2, x.n)
                            for k in range(KD):
                                last = nc.tensor.matmul(bX[:, 0:D], rw[:, x.slot, k * P:(k + 1) * P], t_wo[:, k],
                                                        start=k == 0, stop=k == KD - 1)
                            last.then_inc(pe_x, 1)
                    sweep(pe, YSTEPS, YPEEL, NY, body, YTAIL)

                @block.scalar
                def _(act):
                    for i, m in enumerate((cm_mu_k, cm_mu_r)):
                        for e in range(E):
                            act.dma_start(cm_mu[:, i, e], m[e].rearrange("(k p) -> p k", p=P)).then_inc(ld_moe[3], 16)
                    act.wait_ge(y_pad, 1)

                    def copy_in(s):
                        need(act, pe_z, s.n - NY + 1)
                        nc.scalar.activation(z_in[:, s.slot], xz[:, s.n], ACT.Copy).then_inc(ac_zin, 1)

                    def body(s):
                        a, b, w, d, g = (s.back(k, G) for k in (0, 1, 2, 5, 6))
                        if b:
                            act.wait_ge(pe_kv, b.n + 1)
                            need(act, po_e2v, b.n - NY + 1)
                            need(act, dv_qq, b.n - NY + 1)
                            nc.scalar.activation(body_of(kp, b), bKV[:, 0:KD * P].rearrange("p (q s) -> p q s", s=S), ACT.Copy)
                            nc.scalar.activation(body_of(vp, b), bKV[:, KD * P:].rearrange("p (q s) -> p q s", s=S),
                                                 ACT.Copy).then_inc(ac_kv, 1)
                        if a:
                            act.wait_ge(pe_z, a.n + 1)
                            need(act, pe_r, a.n - NY + 1)
                            for k in range(KD):
                                last = nc.scalar.activation(xn[:, a.slot, k, :, 1:SP1],
                                                            bZ[:, k * P:(k + 1) * P].rearrange("p (j s) -> p j s", s=S),
                                                            ACT.Identity, bias=b1[:, k:k + 1], scale=g1[:, k:k + 1])
                            last.then_inc(ac_z, 1)
                        if g:
                            act.wait_ge(pe_e, g.n + 1)
                            need(act, pe_l, g.n - NY + 1)
                            nc.scalar.activation(eiT[:, g.slot].rearrange("p k t -> p (k t)"), bE[:, 0:KD * P],
                                                 ACT.Copy).then_inc(ac_ei, 1)
                        if w:
                            act.wait_ge(dv_r, w.n + 1)
                            need(act, dv_rw, w.n - NY + 1)
                            nc.scalar.activation(er[:, w.slot], r_lim[:, w.slot], ACT.Exp, scale=-1.0).then_inc(ac_r, 1)
                            need(act, dv_scan, w.n - NY + 1)
                            need(act, po_ev, w.n - NY + 1)
                            act.wait_ge(dv_d1, w.n + 1)
                            for k in range(KD):
                                last = nc.scalar.activation(e1b[:, w.slot, k, :, 1:SP1],
                                                            d1[:, w.slot, k * P:(k + 1) * P].rearrange("p (j s) -> p j s", s=S),
                                                            ACT.Exp, bias=wneg[:, k:k + 1])
                            last.then_inc(ac_e1b, 1)
                            act.wait_ge(po_d2, w.n + 1)
                            nc.scalar.activation(body_of(e2b, w), seqs(d2, w), ACT.Exp).then_inc(ac_e2b, 1)
                            act.wait_ge(dv_d3, w.n + 1)
                            need(act, po_e1a, w.n - NY + 1)
                            nc.scalar.activation(e1[:, w.slot], d3[:, w.slot], ACT.Exp).then_inc(ac_e1, 1)
                            act.wait_ge(po_d4, w.n + 1)
                            need(act, po_e2v, w.n - NY + 1)
                            for k in range(KD):
                                last = nc.scalar.activation(e2[:, w.slot, k * P:(k + 1) * P], d4[:, w.slot, k * P:(k + 1) * P],
                                                            ACT.Exp, bias=u_c[:, k:k + 1])
                            last.then_inc(ac_e2, 1)
                        if s.back(-1, G):
                            copy_in(s.back(-1, G))
                        if d:
                            act.wait_ge(po_ei, d.n + 1)
                            need(act, ei_out[d.slot], d.lap * 32)
                            nc.scalar.activation(ei_shift[:, d.slot], ei[:, d.slot], ACT.Copy, scale=keep[:]).then_inc(ac_sh, 1)
                    copy_in(Step(0, 0, NY))
                    sweep(act, YSTEPS, YPEEL, NY, body, YTAIL)

                @block.vector
                def _(dve):
                    dve.wait_ge(y_pad, 1)

                    def body(s):
                        b, w, v, x, d, g = (s.back(k, G) for k in range(1, 7))
                        if w:
                            dve.wait_ge(ac_kv, w.n + 1)
                            need(dve, po_d4, w.n - NY + 1)
                            nc.vector.tensor_tensor_scan(line(pp, w), w_pad[:].rearrange("p k j s -> p (k j s)"),
                                                         line(kp, w), NEG, ALU.add, ALU.max).then_inc(dv_pp, 1)
                        if v:
                            dve.wait_ge(ac_e1b, v.n + 1)
                            dve.wait_ge(ac_e2b, v.n + 1)
                            need(dve, po_e1a, v.n - NY + 1)
                            nc.vector.tensor_tensor_scan(line(bb, v), line(e1b, v), line(e2b, v), 0.0, ALU.mult, ALU.add)
                            dve.wait_ge(po_ev, v.n + 1)
                            nc.vector.tensor_tensor_scan(line(aa, v), line(e1b, v), line(evb, v), 0.0, ALU.mult,
                                                         ALU.add).then_inc(dv_scan, 1)
                        if d:
                            dve.wait_ge(po_r3, d.n + 1)
                            need(dve, po_ei, d.n - NY + 1)
                            nc.vector.tensor_scalar(z3[:, d.slot], a_x2[:, d.n], mv3[:, d.slot, 0:1], rs3[:, d.slot],
                                                    ALU.subtract, ALU.mult).then_inc(dv_z3, 1)
                        if w:
                            dve.drain()
                            need(dve, ac_e1b, w.n - NY + 1)
                            nc.vector.tensor_tensor(seqs(d1, w), before(pp, w), body_of(pp, w), ALU.subtract).then_inc(dv_d1, 1)
                            for k in range(KD):
                                last = nc.vector.scalar_tensor_tensor(
                                    qq[:, w.slot, k * P:(k + 1) * P].rearrange("p (j s) -> p j s", s=S),
                                    kp[:, w.slot, k, :, 1:SP1], u_c[:, k:k + 1], pp[:, w.slot, k, :, 0:S], ALU.add, ALU.max)
                            last.then_inc(dv_qq, 1)
                            dve.drain()
                            need(dve, ac_e1, w.n - NY + 1)
                            nc.vector.tensor_tensor(seqs(d3, w), before(pp, w), seqs(qq, w), ALU.subtract).then_inc(dv_d3, 1)
                        if v:
                            dve.wait_ge(po_e1a, v.n + 1)
                            dve.wait_ge(ac_e2, v.n + 1)
                            nc.vector.tensor_tensor(e1bb[:, v.slot], e1bb[:, v.slot], e2[:, v.slot], ALU.add)
                            dve.wait_ge(po_e2v, v.n + 1)
                            nc.vector.tensor_tensor(e1a[:, v.slot], e1a[:, v.slot], e2v[:, v.slot], ALU.add)
                            dve.drain()
                            dve.wait_ge(ac_r, v.n + 1)
                            nc.vector.scalar_tensor_tensor(e1bb[:, v.slot], er[:, v.slot], 1.0, e1bb[:, v.slot], ALU.add, ALU.mult)
                            dve.drain()
                            nc.vector.reciprocal(e1bb[:, v.slot], e1bb[:, v.slot])
                        if b:
                            dve.wait_ge(pe_r, b.n + 1)
                            need(dve, ac_r, b.n - NY + 1)
                            nc.vector.tensor_scalar(r_lim[:, b.slot], bR[:, 0:KD * P], -R_LOW, None, ALU.max).then_inc(dv_r, 1)
                        if x:
                            dve.wait_ge(pe_x, x.n + 1)
                            nc.vector.tensor_tensor(a_x2[:, x.n], bX[:, 0:D], a_x2[:, x.n], ALU.add).then_inc(dv_x2, 1)
                        if v or x:
                            dve.drain()
                        if v:
                            need(dve, pe_x, v.n - NY + 1)
                            nc.vector.tensor_tensor(rw[:, v.slot], e1a[:, v.slot], e1bb[:, v.slot], ALU.mult).then_inc(dv_rw, 1)
                        if x:
                            nc.vector.bn_stats(st3[:, x.slot], a_x2[:, x.n])
                        if g:
                            dve.wait_ge(pe_l, g.n + 1)
                            nc.vector.tensor_copy(logits[:, g.n], bL[:, 0:E]).then_inc(dv_lg, 1)
                        if x:
                            dve.drain()
                            nc.vector.bn_aggr(mv3[:, x.slot], st3[:, x.slot])
                            dve.drain()
                            need(dve, po_r3, x.n - NY + 1)
                            nc.vector.tensor_scalar(var3[:, x.slot], mv3[:, x.slot, 1:2], EPS, None, ALU.add).then_inc(dv_var, 1)
                    sweep(dve, YSTEPS, YPEEL, NY, body, YTAIL)

        rt_consts = sem("rt_consts")

        def routing(tag, choices, tiles, scores_in, softmax, table, tile_expert, slot_of, weights):
            with ExitStack() as rs:
                def rb(name, shape, dt=F32):
                    return sb(tag + name, shape, dt, rs)
                tile_id = rb("tile_id", [P, tiles])
                mx, total = rb("mx", [P, G]), rb("total", [P, G])
                pr = rb("pr", [P, G, E])
                top, at = rb("top", [P, G, 8]), rb("at", [P, G, 8], U32)
                at_f = rb("at_f", [P, choices, G])
                hot = rb("hot", [P, choices, G, E])
                mask = rb("mask", [P, G, E])
                tot_ec, run_ec, pos = rb("tot_ec", [P, E, G]), rb("run_ec", [P, E, G]), rb("pos", [P, G, E])
                cmp_eg = rb("cmp_eg", [P, E, G])
                n_tiles, t_end, base = rb("n_tiles", [P, E]), rb("t_end", [P, E]), rb("base", [P, E])
                cmp_te = rb("cmp_te", [P, tiles, E])
                te_f = rb("te_f", [P, tiles])
                prod = rb("prod", [P, G, E])
                slot_f, slot_i = rb("slot_f", [P, choices, G]), rb("slot_i", [P, choices, G], I32)
                q_i, r_i = rb("q_i", [P, choices, G], I32), rb("r_i", [P, choices, G], I32)
                q_f, r_f = rb("q_f", [P, choices, G]), rb("r_f", [P, choices, G])
                hot_r = rb("hot_r", [P, choices, G, P])
                hot_q = rb("hot_q", [P, choices, G, tiles])
                bC, bTab = banks[0], banks[1]
                s_id, s_sub, s_exp, s_mask, s_cnt, s_hot, s_tab = (sem(tag + n) for n in (
                    "id", "sub", "exp", "mask", "cnt", "hot", "tab"))
                with nc.Block() as block:
                    @block.gpsimd
                    def _(pool):
                        nc.gpsimd.iota(tile_id[:], [[1, tiles]], base=0, channel_multiplier=0,
                                       allow_small_or_imprecise_dtypes=True).then_inc(s_id, 1)

                    @block.scalar
                    def _(act):
                        if softmax:
                            act.wait_ge(s_sub, 1)
                            nc.scalar.activation(pr[:], pr[:], ACT.Exp).then_inc(s_exp, 1)

                    @block.tensor
                    def _(pe):
                        pe.wait_ge(s_mask, 1)
                        m = mask[:].rearrange("p c e -> p (c e)")
                        nc.tensor.matmul(bC[:, 0:G * E], before_m[:], m, start=True, stop=True)
                        nc.tensor.matmul(bC[:, G * E:2 * G * E], ones_m[:], m, start=True, stop=True).then_inc(s_cnt, 1)
                        pe.wait_ge(s_hot, 1)
                        for k in range(choices):
                            for c in range(G):
                                last = nc.tensor.matmul(bTab[:, 0:tiles], hot_r[:, k, c], hot_q[:, k, c],
                                                        start=k == 0 and c == 0, stop=k == choices - 1 and c == G - 1)
                        last.then_inc(s_tab, 1)

                    @block.vector
                    def _(dve):
                        def step(ins):
                            dve.drain()
                            return ins

                        def tt(o, a, b, op):
                            return step(nc.vector.tensor_tensor(o, a, b, op))

                        def over_e(v):
                            return v.unsqueeze(2).to_broadcast([P, G, E])

                        def over_g(v):
                            return v.unsqueeze(2).to_broadcast([P, E, G])
                        dve.wait_ge(rt_consts, 9)
                        src = scores_in
                        if softmax:
                            step(nc.vector.reduce_max(mx[:], scores_in[:], AX))
                            nc.vector.tensor_tensor(pr[:], scores_in[:], over_e(mx[:]), ALU.subtract).then_inc(s_sub, 1)
                            dve.wait_ge(s_exp, 1)
                            step(nc.vector.reduce_sum(total[:], pr[:], AX))
                            step(nc.vector.reciprocal(total[:], total[:]))
                            tt(pr[:], pr[:], over_e(total[:]), ALU.mult)
                            src = pr
                        for c in range(G):
                            nc.vector.max(top[:, c], src[:, c])
                        dve.drain()
                        for c in range(G):
                            nc.vector.max_index(at[:, c], top[:, c], src[:, c])
                        dve.drain()
                        if weights is not None:
                            tt(total[:], top[:, :, 0], top[:, :, 1], ALU.add)
                            step(nc.vector.reciprocal(total[:], total[:]))
                            for k in range(choices):
                                nc.vector.tensor_tensor(weights[:, k], top[:, :, k], total[:], ALU.mult)
                        for k in range(choices):
                            nc.vector.tensor_copy(at_f[:, k], at[:, :, k])
                        dve.drain()
                        for k in range(choices):
                            nc.vector.tensor_tensor(hot[:, k], iota_e[:].unsqueeze(1).to_broadcast([P, G, E]),
                                                    over_e(at_f[:, k]), ALU.is_equal)
                        dve.drain()
                        if choices == 2:
                            nc.vector.tensor_tensor(mask[:], hot[:, 0], hot[:, 1], ALU.add).then_inc(s_mask, 1)
                        else:
                            nc.vector.tensor_copy(mask[:], hot[:, 0]).then_inc(s_mask, 1)
                        dve.wait_ge(s_cnt, 1)
                        step(nc.vector.tensor_copy(tot_ec[:], bC[:, G * E:2 * G * E].rearrange("p (c e) -> p e c", e=E)))
                        step(nc.vector.tensor_tensor_scan(run_ec[:].rearrange("p e c -> p (e c)"),
                                                          chunk_on[:].rearrange("p e c -> p (e c)"),
                                                          tot_ec[:].rearrange("p e c -> p (e c)"), 0.0, ALU.mult, ALU.add))
                        tt(cmp_eg[:], over_g(run_ec[:, :, G - 1]), tile_lo[:].unsqueeze(1).to_broadcast([P, E, G]), ALU.is_gt)
                        step(nc.vector.reduce_sum(n_tiles[:], cmp_eg[:], AX))
                        step(nc.vector.tensor_tensor_scan(t_end[:], ones_m[:, 0:E], n_tiles[:], 0.0, ALU.mult, ALU.add))
                        tt(base[:], t_end[:], n_tiles[:], ALU.subtract)
                        step(nc.vector.tensor_scalar(base[:], base[:], float(P), None, ALU.mult))
                        tt(run_ec[:], run_ec[:], tot_ec[:], ALU.subtract)
                        tt(run_ec[:], run_ec[:], over_g(base[:]), ALU.add)
                        tt(pos[:], bC[:, 0:G * E].rearrange("p (c e) -> p c e", e=E),
                           run_ec[:].rearrange("p e c -> p c e"), ALU.add)
                        dve.wait_ge(s_id, 1)
                        tt(cmp_te[:], t_end[:].unsqueeze(1).to_broadcast([P, tiles, E]),
                           tile_id[:].unsqueeze(2).to_broadcast([P, tiles, E]), ALU.is_le)
                        step(nc.vector.reduce_sum(te_f[:], cmp_te[:], AX))
                        nc.vector.tensor_scalar(tile_expert[:], te_f[:], float(E - 1), None, ALU.min)
                        for k in range(choices):
                            tt(prod[:], hot[:, k], pos[:], ALU.mult)
                            step(nc.vector.reduce_sum(slot_f[:, k], prod[:], AX))
                        step(nc.vector.tensor_copy(slot_i[:], slot_f[:]))
                        nc.vector.tensor_copy(slot_of[:], slot_f[:])
                        nc.vector.tensor_scalar(q_i[:], slot_i[:], 7, None, ALU.logical_shift_right)
                        step(nc.vector.tensor_scalar(r_i[:], slot_i[:], P - 1, None, ALU.bitwise_and))
                        nc.vector.tensor_copy(q_f[:], q_i[:])
                        step(nc.vector.tensor_copy(r_f[:], r_i[:]))
                        for k in range(choices):
                            nc.vector.tensor_tensor(hot_r[:, k], iota_p[:].unsqueeze(1).to_broadcast([P, G, P]),
                                                    r_f[:, k].unsqueeze(2).to_broadcast([P, G, P]), ALU.is_equal)
                            tt(hot_q[:, k], tile_id[:].unsqueeze(1).to_broadcast([P, G, tiles]),
                               q_f[:, k].unsqueeze(2).to_broadcast([P, G, tiles]), ALU.is_equal)
                            last = nc.vector.tensor_tensor(hot_q[:, k], hot_q[:, k],
                                                           token_id[:].unsqueeze(2).to_broadcast([P, G, tiles]), ALU.mult)
                        last.then_inc(s_hot, 1)
                        dve.wait_ge(s_tab, 1)
                        nc.vector.tensor_copy(table[:], bTab[:, 0:tiles])

        def most_tiles(pairs):
            return (pairs - E) // P + E

        NT1 = most_tiles(2 * TOK)
        table1 = sb("table1", [P, NT1], U32, moe)
        expert1 = sb("expert1", [P, NT1], I32, moe)
        slot1 = sb("slot1", [P, 2, G], U32, moe)
        gate = sb("gate", [P, 2, G], where=moe)
        with nc.Block() as block:
            @block.gpsimd
            def _(pool):
                def iota(t, pattern, channel):
                    nc.gpsimd.iota(t, pattern, base=0, channel_multiplier=channel,
                                   allow_small_or_imprecise_dtypes=True).then_inc(rt_consts, 1)
                iota(iota_e[:], [[1, E]], 0)
                iota(iota_p[:], [[1, P]], 0)
                iota(tile_lo[:], [[P, G]], 0)
                iota(token_id[:], [[P, G]], 1)
                nc.gpsimd.memset(before_m[:], 1.0).then_inc(rt_consts, 1)
                nc.gpsimd.memset(ones_m[:], 1.0).then_inc(rt_consts, 1)
                nc.gpsimd.memset(chunk_on[:], 1.0)
                pool.drain()
                nc.gpsimd.memset(chunk_on[:, :, 0:1], 0.0).then_inc(rt_consts, 1)
                nc.gpsimd.affine_select(out=before_m[:], in_=before_m[:], compare_op=ALU.is_gt, fill=0.0, base=0,
                                        pattern=[[1, P]], channel_multiplier=-1).then_inc(rt_consts, 2)
        routing("r1_", 2, NT1, logits, True, table1, expert1, slot1, gate)

        rows_y = nc.dram_tensor("rows_y", [NT1 * P, D], F32).ap()
        with ExitStack() as ms:
            NM = 3

            def mb(name, shape, dt=F32):
                return sb(name, shape, dt, ms)
            pick = mb("pick", [P, NM, 1], U32)
            pair = mb("pair", [P, NM, 2 * D])
            mu_e = mb("mu_e", [P, NM, 2, KD])
            prevT, diffT = mb("prevT", [P, NM, KD, P]), mb("diffT", [P, NM, KD, P])
            xk, xr = mb("xk", [P, NM, KD, P]), mb("xr", [P, NM, KD, P])
            h_relu, h_sq = mb("h_relu", [P, NM, FK]), mb("h_sq", [P, NM, FK])
            hT = mb("hT", [P, NM, FKC, P])
            sig = mb("sig", [P, NM, D])
            y = mb("y", [P, NM, D])
            bA, bR, bH, bT, bY = banks[0:5]
            (pe_a, pe_r, pe_h, pe_t, pe_y, ac_p, ac_sig, ac_relu, ac_t, dv_d, dv_x, dv_sq, dv_y, po_mu) = (
                sem("m_" + n) for n in ("pe_a pe_r pe_h pe_t pe_y ac_p ac_sig ac_relu ac_t dv_d dv_x dv_sq dv_y "
                                        "po_mu").split())
            got = [sem(f"m_got{i}") for i in range(NM)]
            put = [sem(f"m_put{i}") for i in range(NM)]
            MSTEPS = NT1 + 3

            with nc.Block() as block:
                @block.gpsimd
                def _(pool):
                    pool.wait_ge(ld_moe[3], 16 * 2 * E)

                    def body(s):
                        need(pool, pe_a, s.n - NM + 1)
                        nc.gpsimd.tensor_copy(pick[:, s.slot], table1[:, bass.ds(s.n, 1)])
                        pool.drain()
                        nc.gpsimd.indirect_dma_start(out=pair[:, s.slot], out_offset=None, in_=rows_e[0:TOK, :],
                                                     in_offset=bass.IndirectOffsetOnAxis(ap=pick[:, s.slot], axis=0)
                                                     ).then_inc(got[s.slot], 16)
                        e = pool.value_load(expert1[0:1, bass.ds(s.n, 1)], min_val=0, max_val=E - 1)
                        need(pool, dv_x, s.n - NM + 1)
                        nc.gpsimd.tensor_copy(mu_e[:, s.slot], cm_mu[:, :, e]).then_inc(po_mu, 1)
                    sweep(pool, NT1, NM, NM, body, 0)

                @block.tensor
                def _(pe):
                    for i in range(3):
                        pe.wait_ge(ld_moe[i], 16)

                    def body(s):
                        a, b, c, d = (s.back(k, NT1) for k in range(4))
                        if a:
                            pe.wait_ge(got[a.slot], a.lap * 16 + 16)
                            need(pe, dv_d, a.n)
                            for q in range(2 * KD):
                                last = nc.tensor.transpose(bA[:, q * P:(q + 1) * P], pair[:, a.slot, q * P:(q + 1) * P], ident[:])
                            last.then_inc(pe_a, 1)
                        if c:
                            pe.wait_ge(dv_sq, c.n + 1)
                            need(pe, ac_t, c.n)
                            for f in range(FKC):
                                last = nc.tensor.transpose(bT[:, f * P:(f + 1) * P], h_sq[:, c.slot, f * P:(f + 1) * P], ident[:])
                            last.then_inc(pe_t, 1)
                        if b:
                            e = pe.value_load(expert1[0:1, bass.ds(b.n, 1)], min_val=0, max_val=E - 1)
                            pe.wait_ge(dv_x, b.n + 1)
                            need(pe, dv_sq, b.n)
                            for k in range(KD):
                                last = nc.tensor.matmul(bH[:], xk[:, b.slot, k], ewk_sb[:, e, k], start=k == 0, stop=k == KD - 1)
                            last.then_inc(pe_h, 1)
                            need(pe, ac_sig, b.n)
                            for k in range(KD):
                                last = nc.tensor.matmul(bR[:, 0:D], xr[:, b.slot, k], ewr_sb[:, e, k], start=k == 0, stop=k == KD - 1)
                            last.then_inc(pe_r, 1)
                        if d:
                            e = pe.value_load(expert1[0:1, bass.ds(d.n, 1)], min_val=0, max_val=E - 1)
                            pe.wait_ge(ac_t, d.n + 1)
                            need(pe, dv_y, d.n)
                            for f in range(FKC):
                                last = nc.tensor.matmul(bY[:, 0:D], hT[:, d.slot, f], ewv_sb[:, e, f], start=f == 0, stop=f == FKC - 1)
                            last.then_inc(pe_y, 1)
                    sweep(pe, MSTEPS, 6, NM, body, 3)

                @block.scalar
                def _(act):
                    def body(s):
                        a, b, c = (s.back(k, NT1) for k in range(3))
                        if a:
                            act.wait_ge(pe_a, a.n + 1)
                            need(act, dv_x, a.n - NM + 1)
                            nc.scalar.activation(prevT[:, a.slot].rearrange("p k t -> p (k t)"), bA[:, 0:KD * P],
                                                 ACT.Copy).then_inc(ac_p, 1)
                        if c:
                            act.wait_ge(pe_t, c.n + 1)
                            need(act, pe_y, c.n - NM + 1)
                            nc.scalar.activation(hT[:, c.slot].rearrange("p f t -> p (f t)"), bT[:], ACT.Copy).then_inc(ac_t, 1)
                        if b:
                            act.wait_ge(pe_h, b.n + 1)
                            need(act, dv_sq, b.n - NM + 1)
                            nc.scalar.activation(h_relu[:, b.slot], bH[:], ACT.Relu).then_inc(ac_relu, 1)
                            act.wait_ge(pe_r, b.n + 1)
                            need(act, dv_y, b.n - NM + 1)
                            nc.scalar.activation(sig[:, b.slot], bR[:, 0:D], ACT.Sigmoid).then_inc(ac_sig, 1)
                    sweep(act, MSTEPS, 6, NM, body, 3)

                @block.vector
                def _(dve):
                    def body(s):
                        a, b, d = s.back(0, NT1), s.back(1, NT1), s.back(3, NT1)
                        if a:
                            dve.wait_ge(ac_p, a.n + 1)
                            nc.vector.tensor_tensor(diffT[:, a.slot].rearrange("p k t -> p (k t)"), bA[:, KD * P:],
                                                    prevT[:, a.slot].rearrange("p k t -> p (k t)"), ALU.subtract).then_inc(dv_d, 1)
                            dve.drain()
                            dve.wait_ge(po_mu, a.n + 1)
                            need(dve, pe_r, a.n - NM + 1)
                            for i, o in enumerate((xk, xr)):
                                for k in range(KD):
                                    last = nc.vector.scalar_tensor_tensor(o[:, a.slot, k], diffT[:, a.slot, k],
                                                                          mu_e[:, a.slot, i, k:k + 1], prevT[:, a.slot, k],
                                                                          ALU.mult, ALU.add)
                            last.then_inc(dv_x, 1)
                        if b:
                            dve.wait_ge(ac_relu, b.n + 1)
                            need(dve, pe_t, b.n - NM + 1)
                            nc.vector.tensor_tensor(h_sq[:, b.slot], bH[:], h_relu[:, b.slot], ALU.mult).then_inc(dv_sq, 1)
                        if d:
                            dve.wait_ge(pe_y, d.n + 1)
                            need(dve, put[d.slot], d.lap * 16)
                            nc.vector.tensor_tensor(y[:, d.slot], bY[:, 0:D], sig[:, d.slot], ALU.mult).then_inc(dv_y, 1)
                    sweep(dve, MSTEPS, 6, NM, body, 3)

                @block.sync
                def _(sp):
                    def body(s):
                        sp.wait_ge(dv_y, s.n + 1)
                        sp.dma_start(rows_y[bass.ds(s.n * P, P), :], y[:, s.slot]).then_inc(put[s.slot], 16)
                    sweep(sp, NT1, NM, NM, body, 0)
                    for i in range(NM):
                        sp.wait_ge(put[i], NT1 // NM * 16)
            assert NT1 % NM == 0

        rows_z = nc.dram_tensor("rows_z", [TOK, D], F32).ap()
        with ExitStack() as cs:
            NC = 3

            def cb(name, shape, dt=F32):
                return sb(name, shape, dt, cs)
            r2_w = cb("r2_w", [P, KD, E])
            pick = cb("pick_c", [P, NC, 2], U32)
            ya, yb2 = cb("ya", [P, NC, D]), cb("yb2", [P, NC, D])
            xsum = cb("xsum", [P, NC, D])
            z4 = cb("z4", [P, NC, D])
            zT = cb("zT", [P, NC, KD, P])
            st4, mv4, var4, rs4 = (cb(n, [P, NC, w]) for n, w in (("st4", 6), ("mv4", 2), ("var4", 1), ("rs4", 1)))
            bZ, bL = banks[0:2]
            (c_pe_z, c_pe_l, c_ac_z, c_dv, c_dv_l, c_po_r, c_po_x, ld_c) = (
                sem(n) for n in "c_pe_z c_pe_l c_ac_z c_dv c_dv_l c_po_r c_po_x ld_c".split())
            got = [sem(f"c_got{i}") for i in range(NC)]
            put = [sem(f"c_put{i}") for i in range(NC)]
            with nc.Block() as block:
                @block.gpsimd
                def _(pool):
                    def body(s):
                        a, b = s.back(0, G), s.back(1, G)
                        if a:
                            need(pool, c_dv, (a.n - NC) * 4 + 2)
                            nc.gpsimd.tensor_copy(pick[:, a.slot], slot1[:, :, a.n])
                            nc.gpsimd.tensor_tensor(xsum[:, a.slot], x1[:, a.n], a_x2[:, a.n], ALU.add).then_inc(c_po_x, 1)
                            pool.drain()
                            for k, t in enumerate((ya, yb2)):
                                nc.gpsimd.indirect_dma_start(out=t[:, a.slot], out_offset=None, in_=rows_y[:, :],
                                                             in_offset=bass.IndirectOffsetOnAxis(ap=pick[:, a.slot, k:k + 1], axis=0)
                                                             ).then_inc(got[a.slot], 16)
                        if b:
                            pool.wait_ge(c_dv, b.n * 4 + 3)
                            nc.gpsimd.tensor_tensor(rs4[:, b.slot], var4[:, b.slot], eps_pow[:], ALU.pow).then_inc(c_po_r, 1)
                    sweep(pool, G + 1, 4, NC, body, 1)

                @block.vector
                def _(dve):
                    def apply(s):
                        dve.wait_ge(c_po_r, s.n + 1)
                        need(dve, c_pe_z, s.n - NC + 1)
                        need(dve, put[s.slot], s.lap * 16)
                        nc.vector.tensor_scalar(z4[:, s.slot], xz[:, s.n], mv4[:, s.slot, 0:1], rs4[:, s.slot],
                                                ALU.subtract, ALU.mult).then_inc(c_dv, 1)

                    def body(s):
                        a, b, d = s.back(0, G), s.back(1, G), s.back(3, G)
                        if a:
                            dve.wait_ge(got[a.slot], a.lap * 32 + 32)
                            dve.wait_ge(c_po_x, a.n + 1)
                            nc.vector.scalar_tensor_tensor(xsum[:, a.slot], ya[:, a.slot], gate[:, 0, bass.ds(a.n, 1)],
                                                           xsum[:, a.slot], ALU.mult, ALU.add).then_inc(c_dv, 1)
                            dve.drain()
                            nc.vector.scalar_tensor_tensor(xz[:, a.n], yb2[:, a.slot], gate[:, 1, bass.ds(a.n, 1)],
                                                           xsum[:, a.slot], ALU.mult, ALU.add).then_inc(c_dv, 1)
                            dve.drain()
                            nc.vector.bn_stats(st4[:, a.slot], xz[:, a.n])
                            dve.drain()
                            nc.vector.bn_aggr(mv4[:, a.slot], st4[:, a.slot])
                            dve.drain()
                            nc.vector.tensor_scalar(var4[:, a.slot], mv4[:, a.slot, 1:2], EPS, None, ALU.add).then_inc(c_dv, 1)
                            apply(a)
                        if d:
                            dve.wait_ge(c_pe_l, d.n + 1)
                            nc.vector.tensor_copy(logits2[:, d.n], bL[:, 0:E]).then_inc(c_dv_l, 1)
                    sweep(dve, G + 3, 6, NC, body, 3)

                @block.tensor
                def _(pe):
                    pe.wait_ge(ld_c, 16)

                    def body(s):
                        a, b = s.back(0, G), s.back(1, G)
                        if a:
                            pe.wait_ge(c_dv, a.n * 4 + 4)
                            need(pe, c_ac_z, a.n)
                            for k in range(KD):
                                last = nc.tensor.transpose(bZ[:, k * P:(k + 1) * P], z4[:, a.slot, k * P:(k + 1) * P], ident[:])
                            last.then_inc(c_pe_z, 1)
                        if b:
                            pe.wait_ge(c_ac_z, b.n + 1)
                            need(pe, c_dv_l, b.n)
                            for k in range(KD):
                                last = nc.tensor.matmul(bL[:, 0:E], zT[:, b.slot, k], r2_w[:, k], start=k == 0, stop=k == KD - 1)
                            last.then_inc(c_pe_l, 1)
                    sweep(pe, G + 1, 4, NC, body, 1)

                @block.scalar
                def _(act):
                    def body(s):
                        act.wait_ge(c_pe_z, s.n + 1)
                        need(act, c_pe_l, s.n - NC + 1)
                        nc.scalar.activation(zT[:, s.slot].rearrange("p k t -> p (k t)"), bZ[:, 0:KD * P],
                                             ACT.Copy).then_inc(c_ac_z, 1)
                    sweep(act, G, 4, NC, body, 0)

                @block.sync
                def _(sp):
                    sp.dma_start(r2_w[:], Wg.rearrange("(k p) e -> p k e", p=P)).then_inc(ld_c, 16)

                    def body(s):
                        sp.wait_ge(c_dv, s.n * 4 + 4)
                        sp.dma_start(rows_z[bass.ds(s.n * P, P), :], z4[:, s.slot]).then_inc(put[s.slot], 16)
                    sweep(sp, G, 4, NC, body, 0)
                    for i in range(NC):
                        sp.wait_ge(put[i], (G - i + NC - 1) // NC * 16)
        moe.close()

        NT2 = most_tiles(TOK)
        assert NT2 > G
        table2 = sb("table2", [P, NT2], U32)
        expert2 = sb("expert2", [P, NT2], I32)
        slot2 = sb("slot2", [P, 1, G], U32)
        rows_f = nc.dram_tensor("rows_f", [NT2 * P, D], F32).ap()
        ws12 = sb("ws12", [P, 2, KD, H])
        ws3 = sb("ws3", [P, HC, D])
        ld_s = sem("ld_s")
        with nc.Block() as block:
            @block.sync
            def _(sp):
                for i, w in enumerate((w1s, w2s)):
                    sp.dma_start(ws12[:, i], w.rearrange("(k p) h -> p k h", p=P)).then_inc(ld_s, 16)
                sp.dma_start(ws3[:], w3s.rearrange("(f p) d -> p f d", p=P)).then_inc(ld_s, 16)
        routing("r2_", 1, NT2, logits2, False, table2, expert2, slot2, None)
        with ExitStack() as fs:
            NF = 2
            HH = HC // 2

            def fb(name, shape, dt=F32):
                return sb(name, shape, dt, fs)
            we12 = fb("we12", [P, NF, 2, KD, H])
            we3 = fb("we3", [P, NF, HC, D])
            pick = fb("pick_f", [P, NF, 1], U32)
            zs, zr = fb("zs", [P, NF, D]), fb("zr", [P, NF, D])
            zT = fb("zT_f", [P, NF, 2, KD, P])
            act_g = fb("act_g", [P, 2, HH * P])
            hT = fb("hT_f", [P, 2, HC, P])
            yr = fb("yr", [P, NF, D])
            bZ = banks[0]
            bU, bG = banks[1:3], banks[3:5]
            bY = banks[5:7]
            pe_z, pe_u, pe_g, pe_y, ac_z, ac_g, dv_h, dv_y = (sem("f_" + n) for n in (
                "pe_z pe_u pe_g pe_y ac_z ac_g dv_h dv_y").split())
            got_s = [sem(f"f_got_s{i}") for i in range(NF)]
            got_r = [sem(f"f_got_r{i}") for i in range(NF)]
            got_w = [sem(f"f_got_w{i}") for i in range(NF)]
            put = [sem(f"f_put{i}") for i in range(NF)]

            def unit_r(s):
                if isinstance(s.n, int) and s.n >= G:
                    return G + s.n, (G + s.n) % 2
                return s.n * 2 + 1, 1

            def fsweep(eng, body, last):
                trips = (G - 1 - 2) // NF
                for i in range(2):
                    body(Step(0, i, NF))
                with eng.Fori(0, trips) as trip:
                    for b in range(NF):
                        body(Step(trip, 2 + b, NF))
                for i in range(2 + trips * NF, last):
                    body(Step(0, i, NF))

            with nc.Block() as block:
                @block.sync
                def _(sp):
                    def body(s):
                        e = sp.value_load(expert2[0:1, bass.ds(s.n, 1)], min_val=0, max_val=E - 1)
                        p = s.back(NF, NT2)
                        if p:
                            sp.wait_ge(pe_g, unit_r(p)[0] * 2 + 2)
                        for i, w in enumerate((W1, W2)):
                            sp.dma_start(we12[:, s.slot, i], w[e].rearrange("(k p) h -> p k h", p=P)).then_inc(got_w[s.slot], 16)
                        if p:
                            sp.wait_ge(pe_y, unit_r(p)[0] + 1)
                        sp.dma_start(we3[:, s.slot], W3[e].rearrange("(f p) d -> p f d", p=P)).then_inc(got_w[s.slot], 16)
                    fsweep(sp, body, NT2)

                @block.gpsimd
                def _(pool):
                    def body(s):
                        need(pool, pe_z, s.n - NF + 1)
                        nc.gpsimd.tensor_copy(pick[:, s.slot], table2[:, bass.ds(s.n, 1)])
                        pool.drain()
                        nc.gpsimd.indirect_dma_start(out=zr[:, s.slot], out_offset=None, in_=rows_z[:, :],
                                                     in_offset=bass.IndirectOffsetOnAxis(ap=pick[:, s.slot], axis=0)
                                                     ).then_inc(got_r[s.slot], 16)
                        if s.back(0, G):
                            pool.dma_start(zs[:, s.slot], rows_z[bass.ds(s.n * P, P), :]).then_inc(got_s[s.slot], 16)
                        w = s.back(NF, NT2)
                        if w:
                            store(w)

                    def store(w):
                        pool.wait_ge(dv_y, unit_r(w)[0] + 1)
                        pool.dma_start(rows_f[bass.ds(w.n * P, P), :], yr[:, w.slot]).then_inc(put[w.slot], 16)
                    fsweep(pool, body, NT2)
                    for i in (NT2 - 2, NT2 - 1):
                        store(Step(0, i, NF))
                    for i in range(NF):
                        pool.wait_ge(put[i], (NT2 - i + NF - 1) // NF * 16)

                @block.tensor
                def _(pe):
                    pe.wait_ge(ld_s, 16 * 3)

                    def transpose_z(s):
                        need(pe, ac_z, s.n)
                        pe.wait_ge(got_r[s.slot], s.lap * 16 + 16)
                        pairs = [(1, zr)]
                        if s.back(0, G):
                            pe.wait_ge(got_s[s.slot], s.lap * 16 + 16)
                            pairs.append((0, zs))
                        for i, z in pairs:
                            for k in range(KD):
                                last = nc.tensor.transpose(bZ[:, (i * KD + k) * P:(i * KD + k + 1) * P],
                                                           z[:, s.slot, k * P:(k + 1) * P], ident[:])
                        last.then_inc(pe_z, 1)

                    def hidden(s, u, routed):
                        w12 = we12[:, s.slot] if routed else ws12[:]
                        for half in range(2):
                            for i, (bank, done, free) in enumerate(((bU, pe_u, ac_g), (bG, pe_g, dv_h))):
                                need(pe, free, u * 2 + half - 1)
                                for f in range(HH):
                                    col0 = (half * HH + f) * P
                                    for k in range(KD):
                                        last = nc.tensor.matmul(bank[half][:, f * P:(f + 1) * P],
                                                                w12[:, i, k, col0:col0 + P], zT[:, s.slot, int(routed), k],
                                                                start=k == 0, stop=k == KD - 1)
                                last.then_inc(done, 1)

                    def down(s, u, parity, routed):
                        w3 = we3[:, s.slot] if routed else ws3[:]
                        pe.wait_ge(dv_h, u * 2 + 2)
                        need(pe, dv_y, u - 1)
                        for f in range(HC):
                            last = nc.tensor.matmul(bY[parity][:, 0:D], hT[:, parity, f], w3[:, f], start=f == 0, stop=f == HC - 1)
                        last.then_inc(pe_y, 1)

                    def body(s):
                        pe.wait_ge(ac_z, s.n + 1)
                        shared, before, after = s.back(0, G), s.back(1, NT2), s.back(-1, NT2)
                        if shared:
                            hidden(s, s.n * 2, False)
                        else:
                            pe.wait_ge(got_w[s.slot], s.lap * 48 + 48)
                            hidden(s, unit_r(s)[0], True)
                        if before:
                            down(before, *unit_r(before), True)
                        if after:
                            transpose_z(after)
                        if shared:
                            pe.wait_ge(got_w[s.slot], s.lap * 48 + 48)
                            hidden(s, unit_r(s)[0], True)
                            down(s, s.n * 2, 0, False)
                    transpose_z(Step(0, 0, NF))
                    fsweep(pe, body, NT2)
                    s = Step(0, NT2 - 1, NF)
                    down(s, *unit_r(s), True)

                @block.scalar
                def _(act):
                    def copy_z(s):
                        act.wait_ge(pe_z, s.n + 1)
                        p = s.back(NF, NT2)
                        if p:
                            act.wait_ge(pe_g, unit_r(p)[0] * 2 + 2)
                        i = 0 if s.back(0, G) else 1
                        nc.scalar.activation(zT[:, s.slot, i:2].rearrange("p i k t -> p (i k t)"), bZ[:, i * KD * P:],
                                             ACT.Copy).then_inc(ac_z, 1)

                    def gelus(u):
                        for half in range(2):
                            act.wait_ge(pe_u, u * 2 + half + 1)
                            need(act, dv_h, u * 2 + half - 1)
                            nc.scalar.activation(act_g[:, half], bU[half][:], ACT.Gelu).then_inc(ac_g, 1)

                    def body(s):
                        shared, after = s.back(0, G), s.back(-1, NT2)
                        gelus(s.n * 2 if shared else unit_r(s)[0])
                        if after:
                            copy_z(after)
                        if shared:
                            gelus(unit_r(s)[0])
                    copy_z(Step(0, 0, NF))
                    fsweep(act, body, NT2)

                @block.vector
                def _(dve):
                    def products(u, parity):
                        for half in range(2):
                            dve.wait_ge(ac_g, u * 2 + half + 1)
                            dve.wait_ge(pe_g, u * 2 + half + 1)
                            if half == 0:
                                need(dve, pe_y, u - 1)
                            nc.vector.tensor_tensor(hT[:, parity, half * HH:(half + 1) * HH].rearrange("p f t -> p (f t)"),
                                                    bG[half][:], act_g[:, half], ALU.mult).then_inc(dv_h, 1)

                    def take(s, u, parity, routed):
                        dve.wait_ge(pe_y, u + 1)
                        if routed:
                            need(dve, put[s.slot], s.lap * 16)
                            nc.vector.tensor_copy(yr[:, s.slot], bY[parity][:, 0:D]).then_inc(dv_y, 1)
                        else:
                            nc.vector.tensor_tensor(xz[:, s.n], bY[parity][:, 0:D], xz[:, s.n], ALU.add).then_inc(dv_y, 1)

                    def body(s):
                        shared, before = s.back(0, G), s.back(1, NT2)
                        if shared:
                            products(s.n * 2, 0)
                        else:
                            products(*unit_r(s))
                        if before:
                            take(before, *unit_r(before), True)
                        if shared:
                            products(*unit_r(s))
                            take(s, s.n * 2, 0, False)
                    fsweep(dve, body, NT2)
                    s = Step(0, NT2 - 1, NF)
                    take(s, *unit_r(s), True)

        with ExitStack() as es:
            NE = 4
            yg = sb("yg", [P, NE, D], where=es)
            got = [sem(f"e_got{i}") for i in range(NE)]
            e_sum, e_out = sem("e_sum"), sem("e_out")
            with nc.Block() as block:
                @block.gpsimd
                def _(pool):
                    for c in range(G):
                        need(pool, e_sum, c - NE + 1)
                        nc.gpsimd.indirect_dma_start(out=yg[:, c % NE], out_offset=None, in_=rows_f[:, :],
                                                     in_offset=bass.IndirectOffsetOnAxis(ap=slot2[:, 0, c:c + 1], axis=0)
                                                     ).then_inc(got[c % NE], 16)

                @block.vector
                def _(dve):
                    for c in range(G):
                        dve.wait_ge(got[c % NE], (c // NE + 1) * 16)
                        nc.vector.tensor_tensor(xz[:, c], xz[:, c], yg[:, c % NE], ALU.add).then_inc(e_sum, 1)

                @block.sync
                def _(sp):
                    for c in range(G):
                        sp.wait_ge(e_sum, c + 1)
                        sp.dma_start(out_nat[c], xz[:, c]).then_inc(e_out, 16)
                    sp.wait_ge(e_out, 16 * G)


_INS = ['x', 'ctx_1024'] + ['L0_xattn_' + m + n for n in 'qkvo' for m in ('W', 'b', 'A', 'B')] + [
    'L0_attn_' + n for n in ('ln1_g', 'ln1_b', 'ln2_g', 'ln2_b', 'tm_mu_k', 'tm_mu_v', 'tm_mu_r', 'time_decay',
                             'time_first', 'Wk', 'Wv', 'Wr', 'Wo', 'router_w', 'cm_mu_k', 'cm_mu_r', 'eWk', 'eWv',
                             'eWr')] + ['L0_ffn_' + n for n in ('w1s', 'w2s', 'w3s', 'W1', 'W2', 'W3', 'Wg')]


def kernel(**inputs):
    import numpy as _np
    import concourse.bacc as _bacc
    from concourse import mybir as _mybir
    from concourse.bass_utils import run_bass_kernel_spmd as _run

    nc = _bacc.Bacc("TRN2", target_bir_lowering=False, num_devices=1)
    arrays, args = {}, []
    for name in _INS:
        a = _np.ascontiguousarray(inputs[name])
        arrays[f"in_{name}_dram"] = a
        args.append(nc.dram_tensor(f"in_{name}_dram", a.shape, _mybir.dt.from_np(a.dtype), kind="ExternalInput").ap())
    shape = inputs['x'].shape
    args.append(nc.dram_tensor("out_0_dram", shape, _mybir.dt.float32, kind="ExternalOutput").ap())
    perceiver_block(nc, *args)
    r = _run(nc, [arrays], core_ids=[0])
    return r.results[0]["out_0_dram"]
```

```python
from contextlib import ExitStack

import concourse.bass as bass
from concourse import mybir

P = 128
F32 = mybir.dt.float32
BF16 = mybir.dt.bfloat16
I32 = mybir.dt.int32
U32 = mybir.dt.uint32
ALU = mybir.AluOpType
ACT = mybir.ActivationFunctionType
AX = mybir.AxisListType.X
EPS = 1e-5
LORA_SCALE = 2.0
NEG = -1e30
R_LOW = 80.0


class Step:

    def __init__(self, trip, offset, ring):
        self.trip, self.offset, self.ring = trip, offset, ring
        self.n = trip * ring + offset
        self.slot = offset % ring
        self.lap = trip + offset // ring

    def back(self, k, count):
        s = Step(self.trip, self.offset - k, self.ring)
        return s if not isinstance(s.n, int) or 0 <= s.n < count else None


def sweep(eng, total, peel, ring, body, tail):
    trips = (total - peel - tail) // ring
    for i in range(peel):
        body(Step(0, i, ring))
    with eng.Fori(0, trips) as trip:
        for b in range(ring):
            body(Step(trip, peel + b, ring))
    for i in range(peel + trips * ring, total):
        body(Step(0, i, ring))


def need(eng, sem, value):
    if not isinstance(value, int) or value > 0:
        eng.wait_ge(sem, value)


class Order:

    def __init__(self, eng, sem, per, step=0):
        self.eng, self.sem, self.per, self.step, self.k = eng, sem, per, step, 0

    def then(self, ins):
        ins.then_inc(self.sem, 1)
        self.k += 1

    def settle(self):
        self.eng.drain()

    def link(self, ins):
        self.then(ins)
        self.settle()

    def close(self):
        assert self.k == self.per, (self.k, self.per)


def perceiver_block(nc, x_in, ctx_in, Wq, bq, Aq, Bq, Wk, bk, Ak, Bk, Wv, bv, Av, Bv, Wo, bo, Ao, Bo,
                    ln1_g, ln1_b, ln2_g, ln2_b, mu_k, mu_v, mu_r, decay, first, tWk, tWv, tWr, tWo,
                    router_w, cm_mu_k, cm_mu_r, eWk, eWv, eWr, w1s, w2s, w3s, W1, W2, W3, Wg, out):
    BATCH, S, D = x_in.shape
    T = ctx_in.shape[1]
    KD = D // P
    G = BATCH * S // P
    BG = P // S
    TC = (T - 1) // P
    R = Aq.shape[0]
    E = eWk.shape[0]
    FK = eWk.shape[2]
    FKC = FK // P
    H = W1.shape[2]
    HC = H // P
    TOK = BATCH * S
    OWN = P + BG
    SP1 = S + 1
    PAD = KD * BG * SP1
    assert T == TC * P + 1 and TC == 2 and KD == 2 and BG == 4

    x_nat = x_in.rearrange("b s d -> (b s) d").rearrange("(c p) d -> p c d", p=P)
    out_nat = out.rearrange("b s d -> (b s) d").rearrange("(c p) d -> c p d", p=P)

    cx = ExitStack()
    with cx, nc.allow_non_contiguous_dma(reason="per-channel vectors, one element a partition"):
        def sb(name, shape, dt=F32, where=cx):
            return where.enter_context(nc.sbuf_tensor(name, shape, dt))

        def sem(name):
            return cx.enter_context(nc.semaphore(name))

        banks = [cx.enter_context(nc.psum_tensor(f"bank{i}", [P, 512], F32)) for i in range(8)]

        def col(v):
            return v.rearrange("(k p) -> p k", p=P)

        def row(v):
            return v.partition_broadcast(P)

        ident = sb("ident", [P, P])
        eps_pow = sb("eps_pow", [P, 1])
        x1 = sb("x1", [P, G, D])
        a_x2 = sb("a_x2", [P, G, D])
        xz = sb("xz", [P, G, D])
        iota_e = sb("iota_e", [P, E])
        tile_lo = sb("tile_lo", [P, G])
        NT1 = (2 * TOK - E) // P + E
        iota_t = sb("iota_t", [P, NT1])
        iota_bf = sb("iota_bf", [P, P], BF16)
        tile_bf = sb("tile_bf", [P, NT1], BF16)
        chunk_id = sb("chunk_id", [P, G])
        part_id = sb("part_id", [P, 1])
        ws12 = a_x2[:].rearrange("p c d -> p (c d)").rearrange("p (i k h) -> p i k h", i=2, k=KD)
        r2_w = sb("r2_w", [P, KD, E])
        before_m = sb("before_m", [P, P], BF16)
        ones_m = sb("ones_m", [P, P], BF16)
        ones_e = sb("ones_e", [P, E])
        chunk_on = sb("chunk_on", [P, E, G])
        logits2 = sb("logits2", [P, G, E])
        picked = sem("picked")

        def wait_picked(pool, before, s):
            if isinstance(s.n, int):
                pool.wait_ge(picked, before + s.n + 1)
            else:
                pool.drain()
        slot1 = sb("slot1", [P, 2, G], U32)
        gate = sb("gate", [P, 2, G])
        mixed_w = sb("mixed_w", [P, 3, KD, 2, D])
        t_wo = sb("t_wo", [P, KD, D])
        r_w = sb("r_w", [P, KD, E])
        mu = sb("mu", [P, 3, KD])
        one_mu = sb("one_mu", [P, 3, KD])
        g1 = sb("g1", [P, KD])
        b1 = sb("b1", [P, KD])
        g2 = sb("g2", [P, D])
        b2 = sb("b2", [P, D])
        wd = sb("wd", [P, KD])
        wneg = sb("wneg", [P, KD])
        u_c = sb("u_c", [P, KD])
        keep = sb("keep", [P, 1])
        zero_row = sb("zero_row", [1, D])
        w_pad = sb("w_pad", [P, KD, BG, SP1])
        ld_y, ld_yc, wneg_done, zero_out = (sem(n) for n in ("ld_y", "ld_yc", "wneg_done", "zero_out"))

        xs = ExitStack()
        with xs:
            def xb(name, shape, dt=F32):
                return sb(name, shape, dt, xs)
            w_nat = xb("w_nat", [P, 4, KD, D])
            w_T = xb("w_T", [P, 4, KD, D])
            lora_a = xb("lora_a", [R, 4, D])
            lora_b = xb("lora_b", [P, 4, KD, R])
            lora_bT = xb("lora_bT", [R, 4, KD, P])
            bq_c = xb("bq_c", [P, KD])
            bk_c = xb("bk_c", [P, KD])
            bv_b = xb("bv_b", [P, D])
            bo_b = xb("bo_b", [P, D])
            last_nat = xb("last_nat", [BATCH, D])
            last_T = xb("last_T", [P, KD, BATCH])
            v_last = xb("v_last", [BG, G, D])
            mask_l = xb("mask_l", [BG, P])
            mask_r = xb("mask_r", [BG, OWN])
            N3 = 3
            ctx_sb = xb("ctx_sb", [P, N3, BG, TC * D])
            kT = xb("kT", [P, N3, BG, KD * TC * P])
            hn = xb("hn", [P, N3, D])
            hnT = xb("hnT", [P, N3, KD, P])
            qT = xb("qT", [P, N3, KD, P])
            k_own = xb("k_own", [P, N3, KD, OWN])
            v_own = xb("v_own", [P, N3, D])
            vl = xb("vl", [BG, N3, D])
            prob = xb("prob", [P, N3, TC * P + OWN])
            probT = xb("probT", [P, N3, 4, P])
            oT = xb("oT", [P, N3, KD, P])
            o_nat = xb("o_nat", [P, N3, D])
            st0 = xb("st0", [P, N3, 6])
            mv0 = xb("mv0", [P, N3, 2])
            var0 = xb("var0", [P, N3, 1])
            rs0 = xb("rs0", [P, N3, 1])
            st1 = xb("st1", [P, 2, N3, 6])
            mv1 = xb("mv1", [P, 2, N3, 2])
            var1 = xb("var1", [P, 2, N3, 1])
            rs1 = xb("rs1", [P, 2, N3, 1])
            smx = xb("smx", [P, N3, 1])
            snm = xb("snm", [P, N3, 1])
            ssum = xb("ssum", [P, N3, 1])
            srec = xb("srec", [P, N3, 1])

            bT0, bT1, bPT, bQ, bV, bS, bO, bW = banks
            ld_x, ld_w, ld_l, ld_lora = (sem(n) for n in ("ld_x", "ld_w", "ld_l", "ld_lora"))
            ld_ctx = [sem(f"ld_ctx{i}") for i in range(N3)]
            const_ord = sem("const_ord")
            pe_set, dv_set, pe_wt, ac_wt = (sem(n) for n in ("pe_set", "dv_set", "pe_wt", "ac_wt"))
            pe_t0, pe_t1, pe_q, pe_v, pe_s, pe_pt, pe_o, pe_w = (sem(n) for n in (
                "pe_t0", "pe_t1", "pe_q", "pe_v", "pe_s", "pe_pt", "pe_o", "pe_w"))
            dv_t0, dv_v, dv_o, dv_w, dv_ln0, dv_ln1, dv_max = (sem(n) for n in (
                "dv_t0", "dv_v", "dv_o", "dv_w", "dv_ln0", "dv_ln1", "dv_max"))
            ac_t1, ac_q, ac_exp, ac_pt, ac_o = (sem(n) for n in ("ac_t1", "ac_q", "ac_exp", "ac_pt", "ac_o"))
            po_r0, po_r1, po_xb, po_last = (sem(n) for n in ("po_r0", "po_r1", "po_xb", "po_last"))
            CONSTS = 8
            STEPS = G + 3

            with nc.Block() as block:
                @block.sync
                def _(sp):
                    for i, w in enumerate((Wq, Wk, Wv, Wo)):
                        sp.dma_start(w_nat[:, i], w.rearrange("(k p) i -> p k i", p=P)).then_inc(ld_w, 16)
                    sp.dma_start(bv_b[:], row(bv)).then_inc(ld_w, 16)
                    sp.dma_start(bo_b[:], row(bo)).then_inc(ld_w, 16)
                    sp.dma_start(bq_c[:], col(bq)).then_inc(ld_w, 16)
                    sp.dma_start(bk_c[:], col(bk)).then_inc(ld_w, 16)
                    sp.dma_start(last_nat[:], ctx_in[:, T - 1, :]).then_inc(ld_l, 16)
                    sp.dma_start(v_last[:], ctx_in[:, T - 1, :].rearrange("(g j) d -> j g d", j=BG)).then_inc(ld_l, 16)

                    sp.dma_start(xz[:], x_nat).then_inc(ld_x, 16)

                    def load(s):
                        need(sp, pe_o, s.n - N3 + 1)
                        src = ctx_in[bass.ds(s.n * BG, BG), 0:TC * P, :].rearrange("j (p c) d -> p j (c d)", c=TC)
                        sp.dma_start(ctx_sb[:, s.slot], src).then_inc(ld_ctx[s.slot], 16)
                    for c in range(N3):
                        load(Step(0, c, N3))
                    for i, w in enumerate((tWk, tWv, tWr)):
                        sp.dma_start(mixed_w[:, i, :, 1], w.rearrange("(k p) o -> p k o", p=P)).then_inc(ld_y, 16)
                    sp.dma_start(t_wo[:], tWo.rearrange("(k p) o -> p k o", p=P)).then_inc(ld_y, 16)
                    sp.dma_start(r_w[:], router_w.rearrange("(k p) o -> p k o", p=P)).then_inc(ld_y, 16)
                    sp.dma_start(g2[:], row(ln2_g)).then_inc(ld_y, 16)
                    sp.dma_start(b2[:], row(ln2_b)).then_inc(ld_y, 16)
                    for i, m in enumerate((mu_k, mu_v, mu_r)):
                        sp.dma_start(mu[:, i], col(m)).then_inc(ld_yc, 16)
                    for t, v in ((g1, ln1_g), (b1, ln1_b), (wd, decay), (u_c, first)):
                        sp.dma_start(t[:], col(v)).then_inc(ld_yc, 16)
                    with sp.Fori(0, (G - N3) // N3) as trip:
                        for c in range(N3):
                            load(Step(trip, N3 + c, N3))
                    for c in range(G - (G - N3) % N3, G):
                        load(Step(0, c, N3))

                @block.gpsimd
                def _(pool):
                    o = Order(pool, const_ord, CONSTS)
                    o.then(nc.gpsimd.memset(ident[:], 0.0))
                    o.then(nc.gpsimd.memset(mask_l[:], 0.0))
                    o.then(nc.gpsimd.memset(mask_r[:], NEG))
                    o.then(nc.gpsimd.memset(eps_pow[:], -0.5))
                    o.settle()
                    o.then(nc.gpsimd.affine_select(out=ident[:], in_=ident[:], compare_op=ALU.not_equal, fill=1.0,
                                                   base=0, pattern=[[-1, P]], channel_multiplier=1))
                    for m, n, f in ((mask_l[:], P, 1.0), (mask_r[:, 0:P], P, 0.0)):
                        v = m.rearrange("a (j s) -> a j s", j=BG)
                        o.then(nc.gpsimd.affine_select(out=v, in_=v, compare_op=ALU.not_equal, fill=f, base=0,
                                                       pattern=[[-1, BG], [0, S]], channel_multiplier=1))
                    v = mask_r[:, P:OWN]
                    o.then(nc.gpsimd.affine_select(out=v, in_=v, compare_op=ALU.not_equal, fill=0.0, base=0,
                                                   pattern=[[-1, BG]], channel_multiplier=1))
                    o.settle()
                    o.close()
                    pool.wait_ge(ld_w, 16 * 8)
                    pool.wait_ge(ld_l, 32)
                    pool.wait_ge(dv_set, 3)

                    def time_mix_constants(part):
                        if part == 0:
                            pool.wait_ge(ld_y, 16 * 7)
                            pool.wait_ge(ld_yc, 16 * 7)
                            nc.gpsimd.tensor_scalar(one_mu[:], mu[:], -1.0, 1.0, ALU.mult, ALU.add)
                            nc.gpsimd.memset(zero_row[:], 0.0)
                            nc.gpsimd.memset(keep[:], 1.0)
                            nc.gpsimd.memset(w_pad[:], 0.0)
                            for j in range(BG):
                                pool.drain()
                                nc.gpsimd.affine_select(out=keep[:], in_=keep[:], compare_op=ALU.not_equal, fill=0.0,
                                                        base=-(j * S + S - 1), pattern=[[0, 1]], channel_multiplier=1)
                            pool.wait_ge(wneg_done, 1)
                            for k in range(KD):
                                nc.gpsimd.tensor_scalar(w_pad[:, k], w_pad[:, k], wneg[:, k:k + 1], None, ALU.add)
                            pool.drain()
                            nc.gpsimd.memset(w_pad[:, :, :, 0:1], NEG)
                        else:
                            i = part - 1
                            for k in range(KD):
                                for h, m in enumerate((mu, one_mu)):
                                    nc.gpsimd.tensor_scalar(mixed_w[:, i, k, h], mixed_w[:, i, k, 1], m[:, i, k:k + 1],
                                                            None, ALU.mult)

                    def rstd0(s):
                        pool.wait_ge(dv_ln0, s.n * 4 + 3)
                        nc.gpsimd.tensor_tensor(rs0[:, s.slot], var0[:, s.slot], eps_pow[:], ALU.pow).then_inc(po_r0, 1)

                    def rstd1(s, h):
                        pool.wait_ge(dv_ln1, s.n * 8 + 4 * h + 3)
                        nc.gpsimd.tensor_tensor(rs1[:, h, s.slot], var1[:, h, s.slot], eps_pow[:], ALU.pow).then_inc(po_r1, 1)

                    def body(s):
                        a, d = s.back(0, G), s.back(3, G)
                        if a and s.back(-1, G):
                            rstd0(s.back(-1, G))
                        if d:
                            rstd1(d, 0)
                        if a:
                            need(pool, pe_s, s.n - N3 + 1)
                            nc.gpsimd.tensor_copy(k_own[:, s.slot, :, P:OWN], last_T[:, :, bass.ds(s.n * BG, BG)])
                            need(pool, pe_o, s.n - N3 + 1)
                            nc.gpsimd.tensor_copy(vl[:, s.slot], v_last[:, s.n]).then_inc(po_last, 1)
                        if d:
                            rstd1(d, 1)
                        if a:
                            pool.wait_ge(dv_ln0, s.n * 4 + 4)
                            nc.gpsimd.tensor_tensor(xz[:, s.n], xz[:, s.n], bo_b[:], ALU.add).then_inc(po_xb, 1)
                        if isinstance(s.n, int) and s.n < 4:
                            time_mix_constants(s.n)
                    rstd0(Step(0, 0, N3))
                    sweep(pool, STEPS, 4, N3, body, 4)

                @block.tensor
                def _(pe):
                    pe.wait_ge(const_ord, CONSTS)
                    pe.wait_ge(ld_w, 16 * 8)
                    for i in range(4):
                        for ki in range(KD):
                            for ko in range(KD):
                                last = nc.tensor.transpose(banks[3 + i][:, ki * D + ko * P:ki * D + (ko + 1) * P],
                                                           w_nat[:, i, ko, ki * P:(ki + 1) * P], ident[:])
                        last.then_inc(pe_wt, 1)
                    pe.wait_ge(ld_lora, 16 * 8)
                    pe.wait_ge(ld_l, 32)
                    for i in range(4):
                        for k in range(KD):
                            nc.tensor.transpose(banks[i // 2][0:R, (i % 2 * KD + k) * P:(i % 2 * KD + k + 1) * P],
                                                lora_b[:, i, k], ident[:]).then_inc(pe_set, 1)
                    for k in range(KD):
                        nc.tensor.transpose(banks[2][:, k * BATCH:(k + 1) * BATCH], last_nat[:, k * P:(k + 1) * P],
                                            ident[0:BATCH, 0:BATCH]).then_inc(pe_set, 1)
                    pe.wait_ge(dv_set, 2)
                    for i in range(4):
                        pe.wait_ge(ac_wt, i + 1)
                        for ki in range(KD):
                            nc.tensor.matmul(banks[3 + i][:, ki * D:(ki + 1) * D], lora_a[:, i, ki * P:(ki + 1) * P],
                                             lora_bT[:, i].rearrange("r k p -> r (k p)"),
                                             start=True, stop=True).then_inc(pe_set, 1)
                    pe.wait_ge(dv_set, 7)

                    def hidden_T(s):
                        pe.wait_ge(dv_ln0, s.n * 4 + 4)
                        need(pe, dv_t0, s.n * 3)
                        for k in range(KD):
                            last = nc.tensor.transpose(bT0[:, k * P:(k + 1) * P], hn[:, s.slot, k * P:(k + 1) * P], ident[:])
                        last.then_inc(pe_t0, 1)

                    def context_T(s, j):
                        if j == 0:
                            pe.wait_ge(ld_ctx[s.slot], s.lap * 16 + 16)
                        if j % 2 == 0:
                            need(pe, ac_t1, s.n * 2 + j // 2)
                        else:
                            need(pe, dv_t0, s.n * 3 + 1 + j // 2)
                        for k in range(KD):
                            for c in range(TC):
                                last = nc.tensor.transpose((bT1, bT0)[j % 2][:, (k * TC + c) * P:(k * TC + c + 1) * P],
                                                           ctx_sb[:, s.slot, j, c * D + k * P:c * D + (k + 1) * P],
                                                           ident[:])
                        last.then_inc((pe_t1, pe_t0)[j % 2], 1)

                    def query_key(s):
                        pe.wait_ge(dv_t0, s.n * 3 + 1)
                        need(pe, ac_q, s.n)
                        for i in range(2):
                            for m in range(KD):
                                for k in range(KD):
                                    last = nc.tensor.matmul(bQ[:, (i * KD + m) * P:(i * KD + m + 1) * P],
                                                            w_T[:, i, k, m * P:(m + 1) * P], hnT[:, s.slot, k],
                                                            start=k == 0, stop=k == KD - 1)
                        last.then_inc(pe_q, 1)

                    def value(s):
                        need(pe, dv_v, s.n)
                        for k in range(KD):
                            last = nc.tensor.matmul(bV[:, 0:D], hnT[:, s.slot, k], w_T[:, 2, k], start=k == 0, stop=k == KD - 1)
                        last.then_inc(pe_v, 1)

                    def scores(s):
                        pe.wait_ge(ac_q, s.n + 1)
                        pe.wait_ge(po_last, s.n + 1)
                        need(pe, ac_exp, s.n)
                        own = bS[:, TC * P:TC * P + OWN]
                        for k in range(KD):
                            nc.tensor.matmul(own, qT[:, s.slot, k], k_own[:, s.slot, k], start=k == 0, stop=False)
                        nc.tensor.matmul(own, mask_l[:], mask_r[:], start=False, stop=True)
                        pe.wait_ge(ac_t1, s.n * 2 + 2)
                        pe.wait_ge(dv_t0, s.n * 3 + 3)
                        for j in range(BG):
                            for k in range(KD):
                                last = nc.tensor.matmul(bS[j * S:(j + 1) * S, 0:TC * P], qT[:, s.slot, k, j * S:(j + 1) * S],
                                                        kT[:, s.slot, j, k * TC * P:(k + 1) * TC * P],
                                                        start=k == 0, stop=k == KD - 1)
                        last.then_inc(pe_s, 1)

                    def prob_T(s):
                        pe.wait_ge(ac_exp, s.n + 1)
                        need(pe, ac_pt, s.n)
                        for c in range(3):
                            nc.tensor.transpose(bPT[:, c * P:(c + 1) * P], prob[:, s.slot, c * P:(c + 1) * P], ident[:])
                        nc.tensor.transpose(bPT[0:BG, 3 * P:4 * P], prob[:, s.slot, 3 * P:3 * P + BG],
                                            ident[:]).then_inc(pe_pt, 1)

                    def values(s):
                        pe.wait_ge(ac_pt, s.n + 1)
                        pe.wait_ge(dv_v, s.n + 1)
                        need(pe, dv_o, s.n * 2)
                        nc.tensor.matmul(bO[:, 0:D], probT[:, s.slot, 2], v_own[:, s.slot], start=True, stop=False)
                        nc.tensor.matmul(bO[:, 0:D], probT[0:BG, s.slot, 3], vl[:, s.slot], start=False, stop=False)
                        for c in range(TC):
                            for j in range(BG):
                                last = nc.tensor.matmul(bO[j * S:(j + 1) * S, 0:D], probT[:, s.slot, c, j * S:(j + 1) * S],
                                                        ctx_sb[:, s.slot, j, c * D:(c + 1) * D],
                                                        start=False, stop=c == TC - 1)
                        last.then_inc(pe_o, 1)

                    def out_T(s):
                        pe.wait_ge(dv_o, s.n * 2 + 2)
                        need(pe, dv_w, s.n)
                        for k in range(KD):
                            last = nc.tensor.transpose(bW[:, k * P:(k + 1) * P], o_nat[:, s.slot, k * P:(k + 1) * P], ident[:])
                        last.then_inc(pe_w, 1)

                    def project(s):
                        pe.wait_ge(ac_o, s.n + 1)
                        for k in range(KD):
                            last = nc.tensor.matmul(bW[:, 0:D], oT[:, s.slot, k], w_T[:, 3, k], start=k == 0, stop=k == KD - 1)
                        last.then_inc(pe_w, 1)

                    def body(s):
                        a, b, c = s.back(0, G), s.back(1, G), s.back(2, G)
                        if c:
                            out_T(c)
                        if a:
                            context_T(a, 0)
                            context_T(a, 1)
                            query_key(a)
                            context_T(a, 2)
                        if b:
                            prob_T(b)
                        if a:
                            value(a)
                            context_T(a, 3)
                        if c:
                            project(c)
                        if b:
                            values(b)
                        if a and s.back(-1, G):
                            hidden_T(s.back(-1, G))
                        if a:
                            scores(a)
                    hidden_T(Step(0, 0, N3))
                    sweep(pe, STEPS, 4, N3, body, 4)

                @block.scalar
                def _(act):
                    for i, w in enumerate((Aq, Ak, Av, Ao)):
                        act.dma_start(lora_a[:, i], w).then_inc(ld_lora, 16)
                    for i, w in enumerate((Bq, Bk, Bv, Bo)):
                        act.dma_start(lora_b[:, i], w.rearrange("(k p) r -> p k r", p=P)).then_inc(ld_lora, 16)
                    act.wait_ge(ld_w, 16 * 8)
                    for i in range(4):
                        act.wait_ge(pe_wt, i + 1)
                        nc.scalar.activation(w_T[:, i].rearrange("p k o -> p (k o)"), banks[3 + i][:], ACT.Copy).then_inc(ac_wt, 1)

                    def context(s, j):
                        act.wait_ge(pe_t1, s.n * 2 + j // 2 + 1)
                        need(act, pe_s, s.n - N3 + 1)
                        nc.scalar.activation(kT[:, s.slot, j], bT1[:], ACT.Copy).then_inc(ac_t1, 1)

                    def body(s):
                        a, b, c = s.back(0, G), s.back(1, G), s.back(2, G)
                        if c:
                            act.wait_ge(pe_w, c.n * 2 + 1)
                            nc.scalar.activation(oT[:, c.slot].rearrange("p k t -> p (k t)"), bW[:, 0:D], ACT.Copy).then_inc(ac_o, 1)
                        if a:
                            context(a, 0)
                            act.wait_ge(pe_q, a.n + 1)
                            for k in range(KD):
                                nc.scalar.activation(qT[:, a.slot, k], bQ[:, k * P:(k + 1) * P], ACT.Identity,
                                                     bias=bq_c[:, k:k + 1])
                                last = nc.scalar.activation(k_own[:, a.slot, k, 0:P], bQ[:, (KD + k) * P:(KD + k + 1) * P],
                                                            ACT.Identity, bias=bk_c[:, k:k + 1])
                            last.then_inc(ac_q, 1)
                            context(a, 2)
                        if b:
                            act.wait_ge(pe_pt, b.n + 1)
                            need(act, pe_o, b.n - N3 + 1)
                            nc.scalar.activation(probT[:, b.slot, 0:3], bPT[:, 0:3 * P], ACT.Copy)
                            nc.scalar.activation(probT[0:BG, b.slot, 3], bPT[0:BG, 3 * P:4 * P], ACT.Copy).then_inc(ac_pt, 1)
                        if a:
                            act.wait_ge(dv_max, a.n * 2 + 2)
                            need(act, pe_pt, a.n - N3 + 1)
                            nc.scalar.activation(prob[:, a.slot], bS[:, 0:TC * P + OWN], ACT.Exp, bias=snm[:, a.slot],
                                                 scale=float(D) ** -0.5, accum_out=ssum[:, a.slot]).then_inc(ac_exp, 1)
                        if isinstance(s.n, int) and s.n == 0:
                            act.wait_ge(ld_yc, 16 * 7)
                            nc.scalar.activation(wneg[:], wd[:], ACT.Exp)
                            act.drain()
                            nc.scalar.mul(wneg[:], wneg[:], -1.0).then_inc(wneg_done, 1)
                    sweep(act, STEPS, 4, N3, body, 4)

                @block.vector
                def _(dve):
                    dve.wait_ge(pe_set, 8)
                    for i in range(2):
                        nc.vector.tensor_scalar(lora_bT[:, 2 * i:2 * i + 2].rearrange("r i k p -> r (i k p)"),
                                                banks[i][0:R, :], LORA_SCALE, None, ALU.mult).then_inc(dv_set, 1)
                    dve.wait_ge(pe_set, 10)
                    nc.vector.tensor_copy(last_T[:].rearrange("p k b -> p (k b)"), banks[2][:, 0:KD * BATCH]).then_inc(dv_set, 1)
                    for i in range(4):
                        dve.wait_ge(pe_set, 10 + KD * (i + 1))
                        w = w_T[:, i].rearrange("p k o -> p (k o)")
                        nc.vector.tensor_tensor(w, banks[3 + i][:], w, ALU.add).then_inc(dv_set, 1)

                    def norm_stats(o, src, st, mv, var):
                        o.settle()
                        o.link(nc.vector.bn_stats(st, src))
                        o.link(nc.vector.bn_aggr(mv, st))
                        o.then(nc.vector.tensor_scalar(var, mv[:, 1:2], EPS, None, ALU.add))

                    def norm_apply(o, dst, src, mv, rstd):
                        o.then(nc.vector.tensor_scalar(dst, src, mv[:, 0:1], rstd, ALU.subtract, ALU.mult))

                    def ln0(s):
                        o = Order(dve, dv_ln0, 4, s.n)
                        norm_stats(o, xz[:, s.n], st0[:, s.slot], mv0[:, s.slot], var0[:, s.slot])
                        yield
                        dve.wait_ge(po_r0, s.n + 1)
                        need(dve, pe_t0, (s.n - N3) * 3 + 1)
                        norm_apply(o, hn[:, s.slot], xz[:, s.n], mv0[:, s.slot], rs0[:, s.slot])
                        o.close()
                        yield

                    def copy_T0(s, u, dst, n):
                        dve.wait_ge(pe_t0, s.n * 3 + u + 1)
                        nc.vector.tensor_copy(dst, bT0[:, 0:n]).then_inc(dv_t0, 1)

                    def copy_hidden(s):
                        need(dve, pe_v, s.n - N3 + 1)
                        copy_T0(s, 0, hnT[:, s.slot].rearrange("p k t -> p (k t)"), KD * P)

                    def body(s):
                        a, b, c, d = (s.back(k, G) for k in range(4))
                        n0 = ln0(s.back(-1, G)) if a and s.back(-1, G) else None
                        n1 = None
                        if n0:
                            next(n0)
                        if d:
                            n1 = Order(dve, dv_ln1, 8, d.n)
                            norm_stats(n1, x1[:, d.n], st1[:, 0, d.slot], mv1[:, 0, d.slot], var1[:, 0, d.slot])
                        if a:
                            need(dve, pe_s, a.n - N3 + 1)
                            copy_T0(a, 1, kT[:, a.slot, 1], 512)
                        if n0:
                            next(n0)
                        if d:
                            dve.wait_ge(po_r1, d.n * 2 + 1)
                            norm_apply(n1, a_x2[:, d.n], x1[:, d.n], mv1[:, 0, d.slot], rs1[:, 0, d.slot])
                            norm_stats(n1, a_x2[:, d.n], st1[:, 1, d.slot], mv1[:, 1, d.slot], var1[:, 1, d.slot])
                        if a:
                            dve.wait_ge(pe_v, a.n + 1)
                            need(dve, pe_o, a.n - N3 + 1)
                            nc.vector.tensor_tensor(v_own[:, a.slot], bV[:, 0:D], bv_b[:], ALU.add).then_inc(dv_v, 1)
                            copy_T0(a, 2, kT[:, a.slot, 3], 512)
                        if c:
                            dve.wait_ge(pe_w, c.n * 2 + 2)
                            dve.wait_ge(po_xb, c.n + 1)
                            nc.vector.tensor_tensor(x1[:, c.n], bW[:, 0:D], xz[:, c.n], ALU.add).then_inc(dv_w, 1)
                        if d:
                            dve.wait_ge(po_r1, d.n * 2 + 2)
                            norm_apply(n1, xz[:, d.n], a_x2[:, d.n], mv1[:, 1, d.slot], rs1[:, 1, d.slot])
                            n1.close()
                        if b:
                            o = Order(dve, dv_o, 2, b.n)
                            dve.wait_ge(ac_exp, b.n + 1)
                            o.link(nc.vector.reciprocal(srec[:, b.slot], ssum[:, b.slot]))
                            dve.wait_ge(pe_o, b.n + 1)
                            need(dve, pe_w, (b.n - N3) * 2 + 1)
                            o.then(nc.vector.tensor_scalar(o_nat[:, b.slot], bO[:, 0:D], srec[:, b.slot], None, ALU.mult))
                        if n0:
                            copy_hidden(s.back(-1, G))
                        if a:
                            o = Order(dve, dv_max, 2, a.n)
                            dve.wait_ge(pe_s, a.n + 1)
                            o.link(nc.vector.reduce_max(smx[:, a.slot], bS[:, 0:TC * P + OWN], AX))
                            o.then(nc.vector.tensor_scalar(snm[:, a.slot], smx[:, a.slot], -float(D) ** -0.5, None, ALU.mult))
                    dve.wait_ge(ld_x, 16)
                    dve.wait_ge(ld_w, 16 * 8)
                    first_ln = ln0(Step(0, 0, N3))
                    next(first_ln)
                    next(first_ln)
                    copy_hidden(Step(0, 0, N3))
                    sweep(dve, STEPS, 4, N3, body, 4)

        rows_e = nc.dram_tensor("rows_e", [TOK + 1, 2 * D], F32).ap()
        moe = cx.enter_context(ExitStack())
        ewk_sb = sb("ewk_sb", [P, E, KD, FK], where=moe)
        ewv_sb = sb("ewv_sb", [P, E, FKC, D], where=moe)
        ewr_sb = sb("ewr_sb", [P, E, KD, D], where=moe)
        cm_mu = sb("cm_mu", [P, 2, E, KD], where=moe)
        logits = sb("logits", [P, G, E], where=moe)
        ld_moe = [sem(f"ld_moe{i}") for i in range(4)]
        ei_out = [sem(f"ei_out{i}") for i in range(2)]
        ys = ExitStack()
        with ys:
            def yb(name, shape, dt=F32):
                return sb(name, shape, dt, ys)
            NY = 2
            def pad(name):
                return yb(name, [P, NY, KD, BG, SP1])

            def flat(name):
                return yb(name, [P, NY, KD * P])
            z_in = yb("z_in", [P, NY, D])
            xn, kp, vp, pp, e1b, e2b, evb, aa, bb = (pad(n) for n in (
                "xn", "kp", "vp", "pp", "e1b", "e2b", "evb", "aa", "bb"))
            d1, d2, qq, d3, d4, e1, e2, e2v, e1a, e1bb, er, r_lim, rw = (flat(n) for n in (
                "d1", "d2", "qq", "d3", "d4", "e1", "e2", "e2v", "e1a", "e1bb", "er", "r_lim", "rw"))
            z3 = yb("z3", [P, NY, D])
            ei = yb("ei", [P, NY, D])
            ei_shift = yb("ei_shift", [P, NY, D])
            eiT = yb("eiT", [P, NY, KD, P])
            st3 = yb("st3", [P, NY, 6])
            mv3 = yb("mv3", [P, NY, 2])
            var3 = yb("var3", [P, NY, 1])
            rs3 = yb("rs3", [P, NY, 1])
            bZ, bKV, bR, bX, bE, bL = banks[0:6]
            y_pad = sem("y_pad")
            rt_consts = sem("rt_consts")
            (pe_z, pe_kv, pe_r, pe_x, pe_e, pe_l,
             ac_zin, ac_z, ac_kv, ac_r, ac_e1b, ac_e2b, ac_e1, ac_e2, ac_ei, ac_sh,
             dv_pp, dv_d1, dv_qq, dv_d3, dv_scan, dv_rw, dv_r, dv_x2, dv_var, dv_z3, dv_lg,
             po_d2, po_d4, po_ev, po_e2v, po_e1b, po_num, po_r3, po_ei) = (sem("y_" + n) for n in (
                 "pe_z pe_kv pe_r pe_x pe_e pe_l "
                 "ac_zin ac_z ac_kv ac_r ac_e1b ac_e2b ac_e1 ac_e2 ac_ei ac_sh "
                 "dv_pp dv_d1 dv_qq dv_d3 dv_scan dv_rw dv_r dv_x2 dv_var dv_z3 dv_lg "
                 "po_d2 po_d4 po_ev po_e2v po_e1b po_num po_r3 po_ei").split())
            YSTEPS = G + 6
            YPEEL = 8
            YTAIL = 7

            def body_of(t, s):
                return t[:, s.slot, :, :, 1:SP1].rearrange("p k j s -> p (k j) s")

            def before(t, s):
                return t[:, s.slot, :, :, 0:S].rearrange("p k j s -> p (k j) s")

            def line(t, s):
                return t[:, s.slot].rearrange("p k j s -> p (k j s)")

            def seqs(t, s):
                return t[:, s.slot].rearrange("p (q s) -> p q s", s=S)

            with nc.Block() as block:
                @block.sync
                def _(sp):
                    sp.dma_start(ewk_sb[:], eWk.rearrange("e (k p) f -> p e k f", p=P)).then_inc(ld_moe[0], 16)
                    sp.dma_start(ewr_sb[:], eWr.rearrange("e (k p) f -> p e k f", p=P)).then_inc(ld_moe[1], 16)
                    sp.dma_start(ewv_sb[:], eWv.rearrange("e (k p) f -> p e k f", p=P)).then_inc(ld_moe[2], 16)
                    sp.dma_start(rows_e[0:1, 0:D], zero_row[:]).then_inc(zero_out, 16)
                    for i, m in enumerate((cm_mu_k, cm_mu_r)):
                        for e in range(E):
                            sp.dma_start(cm_mu[:, i, e], m[e].rearrange("(k p) -> p k", p=P)).then_inc(ld_moe[3], 16)

                    def body(s):
                        d = s.back(5, G)
                        if d:
                            sp.wait_ge(po_ei, d.n + 1)
                            sp.dma_start(rows_e[bass.ds(d.n * P, P), D:2 * D], ei[:, d.slot]).then_inc(ei_out[d.slot], 16)
                            sp.wait_ge(ac_sh, d.n + 1)
                            sp.dma_start(rows_e[bass.ds(d.n * P + 1, P), 0:D], ei_shift[:, d.slot]).then_inc(ei_out[d.slot], 16)
                    sweep(sp, YSTEPS, YPEEL, NY, body, YTAIL)
                    sp.wait_ge(zero_out, 16)
                    for i in range(NY):
                        sp.wait_ge(ei_out[i], 32 * G // NY)

                @block.gpsimd
                def _(pool):
                    for t in (xn, e1b, evb, e2b, vp):
                        nc.gpsimd.memset(t[:, :, :, :, 0:1], 0.0)
                    nc.gpsimd.memset(kp[:, :, :, :, 0:1], NEG).then_inc(y_pad, 1)

                    def iota(t, pattern, channel):
                        nc.gpsimd.iota(t, pattern, base=0, channel_multiplier=channel,
                                       allow_small_or_imprecise_dtypes=True).then_inc(rt_consts, 1)
                    iota(iota_e[:], [[1, E]], 0)
                    iota(iota_bf[:], [[1, P]], 0)
                    iota(tile_bf[:], [[1, NT1]], 0)
                    iota(tile_lo[:], [[P, G]], 0)
                    iota(iota_t[:], [[1, NT1]], 0)
                    iota(chunk_id[:], [[1, G]], 0)
                    iota(part_id[:], [[0, 1]], 1)
                    nc.gpsimd.memset(ones_e[:], 1.0).then_inc(rt_consts, 1)
                    nc.gpsimd.memset(before_m[:], 1.0).then_inc(rt_consts, 1)
                    nc.gpsimd.memset(ones_m[:], 1.0).then_inc(rt_consts, 1)
                    nc.gpsimd.memset(chunk_on[:], 1.0)
                    pool.drain()
                    nc.gpsimd.memset(chunk_on[:, :, 0:1], 0.0).then_inc(rt_consts, 1)
                    nc.gpsimd.affine_select(out=before_m[:], in_=before_m[:], compare_op=ALU.is_gt, fill=0.0, base=0,
                                            pattern=[[1, P]], channel_multiplier=-1).then_inc(rt_consts, 2)

                    def body(s):
                        w, v, x, d = s.back(2, G), s.back(3, G), s.back(4, G), s.back(5, G)
                        if w:
                            need(pool, ac_e2, w.n - NY + 1)
                            pool.wait_ge(dv_pp, w.n + 1)
                            nc.gpsimd.tensor_tensor(seqs(d2, w), body_of(kp, w), body_of(pp, w), ALU.subtract).then_inc(po_d2, 1)
                        if v:
                            pool.wait_ge(dv_scan, v.n + 1)
                            pool.wait_ge(ac_e1, v.n + 1)
                            need(pool, dv_rw, v.n - NY + 1)
                            nc.gpsimd.tensor_tensor(seqs(e1bb, v), seqs(e1, v), before(bb, v), ALU.mult).then_inc(po_e1b, 1)
                            nc.gpsimd.tensor_tensor(seqs(e1a, v), seqs(e1, v), before(aa, v), ALU.mult)
                            pool.drain()
                            nc.gpsimd.tensor_tensor(e1a[:, v.slot], e1a[:, v.slot], e2v[:, v.slot], ALU.add).then_inc(po_num, 1)
                        if d:
                            pool.wait_ge(dv_z3, d.n + 1)
                            need(pool, pe_e, d.n - NY + 1)
                            need(pool, ac_sh, d.n - NY + 1)
                            need(pool, ei_out[d.slot], d.lap * 32)
                            nc.gpsimd.tensor_tensor(ei[:, d.slot], z3[:, d.slot], g2[:], ALU.mult)
                            pool.drain()
                            nc.gpsimd.tensor_tensor(ei[:, d.slot], ei[:, d.slot], b2[:], ALU.add).then_inc(po_ei, 1)
                        if w:
                            pool.wait_ge(dv_qq, w.n + 1)
                            nc.gpsimd.tensor_tensor(seqs(d4, w), body_of(kp, w), seqs(qq, w), ALU.subtract).then_inc(po_d4, 1)
                            pool.wait_ge(ac_e2b, w.n + 1)
                            need(pool, dv_scan, w.n - NY + 1)
                            nc.gpsimd.tensor_tensor(body_of(evb, w), body_of(e2b, w), body_of(vp, w), ALU.mult).then_inc(po_ev, 1)
                            pool.wait_ge(ac_e2, w.n + 1)
                            need(pool, dv_rw, w.n - NY + 1)
                            nc.gpsimd.tensor_tensor(seqs(e2v, w), seqs(e2, w), body_of(vp, w), ALU.mult).then_inc(po_e2v, 1)
                        if x:
                            pool.wait_ge(dv_var, x.n + 1)
                            need(pool, dv_z3, x.n - NY + 1)
                            nc.gpsimd.tensor_tensor(rs3[:, x.slot], var3[:, x.slot], eps_pow[:], ALU.pow).then_inc(po_r3, 1)
                    sweep(pool, YSTEPS, YPEEL, NY, body, YTAIL)

                @block.tensor
                def _(pe):
                    def products(s, i):
                        for m in range(KD):
                            o = (bKV, bKV, bR)[i][:, (i % 2 * KD + m) * P:(i % 2 * KD + m + 1) * P]
                            for k in range(KD):
                                for h in range(2):
                                    last = nc.tensor.matmul(o.rearrange("p (j s) -> p j s", j=BG),
                                                            mixed_w[:, i, k, h, m * P:(m + 1) * P],
                                                            xn[:, s.slot, k, :, 1 - h:1 - h + S],
                                                            start=k == 0 and h == 0, stop=k == KD - 1 and h == 1)
                        return last

                    def body(s):
                        a, b, x, g = s.back(0, G), s.back(1, G), s.back(4, G), s.back(6, G)
                        if b:
                            pe.wait_ge(ac_z, b.n + 1)
                            need(pe, ac_kv, b.n)
                            products(b, 0)
                            products(b, 1).then_inc(pe_kv, 1)
                        if a:
                            pe.wait_ge(ac_zin, a.n + 1)
                            need(pe, ac_z, a.n)
                            for k in range(KD):
                                last = nc.tensor.transpose(bZ[:, k * P:(k + 1) * P], z_in[:, a.slot, k * P:(k + 1) * P], ident[:])
                            last.then_inc(pe_z, 1)
                        if g:
                            pe.wait_ge(po_ei, g.n + 1)
                            need(pe, ac_ei, g.n)
                            for k in range(KD):
                                last = nc.tensor.transpose(bE[:, k * P:(k + 1) * P], ei[:, g.slot, k * P:(k + 1) * P], ident[:])
                            last.then_inc(pe_e, 1)
                        if b:
                            need(pe, dv_r, b.n)
                            products(b, 2).then_inc(pe_r, 1)
                        if g:
                            pe.wait_ge(ac_ei, g.n + 1)
                            need(pe, dv_lg, g.n)
                            for k in range(KD):
                                last = nc.tensor.matmul(bL[:, 0:E], eiT[:, g.slot, k], r_w[:, k], start=k == 0, stop=k == KD - 1)
                            last.then_inc(pe_l, 1)
                        if x:
                            pe.wait_ge(dv_rw, x.n + 1)
                            need(pe, dv_x2, x.n)
                            for k in range(KD):
                                last = nc.tensor.matmul(bX[:, 0:D], rw[:, x.slot, k * P:(k + 1) * P], t_wo[:, k],
                                                        start=k == 0, stop=k == KD - 1)
                            last.then_inc(pe_x, 1)
                    sweep(pe, YSTEPS, YPEEL, NY, body, YTAIL)

                @block.scalar
                def _(act):
                    act.wait_ge(y_pad, 1)

                    def copy_in(s):
                        need(act, pe_z, s.n - NY + 1)
                        nc.scalar.activation(z_in[:, s.slot], xz[:, s.n], ACT.Copy).then_inc(ac_zin, 1)

                    def body(s):
                        a, b, w, d, g = (s.back(k, G) for k in (0, 1, 2, 5, 6))
                        if b:
                            act.wait_ge(pe_kv, b.n + 1)
                            need(act, po_e2v, b.n - NY + 1)
                            need(act, dv_qq, b.n - NY + 1)
                            nc.scalar.activation(body_of(kp, b), bKV[:, 0:KD * P].rearrange("p (q s) -> p q s", s=S), ACT.Copy)
                            nc.scalar.activation(body_of(vp, b), bKV[:, KD * P:].rearrange("p (q s) -> p q s", s=S),
                                                 ACT.Copy).then_inc(ac_kv, 1)
                        if a:
                            act.wait_ge(pe_z, a.n + 1)
                            need(act, pe_r, a.n - NY + 1)
                            for k in range(KD):
                                last = nc.scalar.activation(xn[:, a.slot, k, :, 1:SP1],
                                                            bZ[:, k * P:(k + 1) * P].rearrange("p (j s) -> p j s", s=S),
                                                            ACT.Identity, bias=b1[:, k:k + 1], scale=g1[:, k:k + 1])
                            last.then_inc(ac_z, 1)
                        if g:
                            act.wait_ge(pe_e, g.n + 1)
                            need(act, pe_l, g.n - NY + 1)
                            nc.scalar.activation(eiT[:, g.slot].rearrange("p k t -> p (k t)"), bE[:, 0:KD * P],
                                                 ACT.Copy).then_inc(ac_ei, 1)
                        if w:
                            act.wait_ge(dv_r, w.n + 1)
                            need(act, dv_rw, w.n - NY + 1)
                            nc.scalar.activation(er[:, w.slot], r_lim[:, w.slot], ACT.Exp, scale=-1.0).then_inc(ac_r, 1)
                            need(act, dv_scan, w.n - NY + 1)
                            need(act, po_ev, w.n - NY + 1)
                            act.wait_ge(dv_d1, w.n + 1)
                            for k in range(KD):
                                last = nc.scalar.activation(e1b[:, w.slot, k, :, 1:SP1],
                                                            d1[:, w.slot, k * P:(k + 1) * P].rearrange("p (j s) -> p j s", s=S),
                                                            ACT.Exp, bias=wneg[:, k:k + 1])
                            last.then_inc(ac_e1b, 1)
                            act.wait_ge(po_d2, w.n + 1)
                            nc.scalar.activation(body_of(e2b, w), seqs(d2, w), ACT.Exp).then_inc(ac_e2b, 1)
                            act.wait_ge(dv_d3, w.n + 1)
                            need(act, po_num, w.n - NY + 1)
                            nc.scalar.activation(e1[:, w.slot], d3[:, w.slot], ACT.Exp).then_inc(ac_e1, 1)
                            act.wait_ge(po_d4, w.n + 1)
                            need(act, po_e2v, w.n - NY + 1)
                            for k in range(KD):
                                last = nc.scalar.activation(e2[:, w.slot, k * P:(k + 1) * P], d4[:, w.slot, k * P:(k + 1) * P],
                                                            ACT.Exp, bias=u_c[:, k:k + 1])
                            last.then_inc(ac_e2, 1)
                        if s.back(-1, G):
                            copy_in(s.back(-1, G))
                        if d:
                            act.wait_ge(po_ei, d.n + 1)
                            need(act, ei_out[d.slot], d.lap * 32)
                            nc.scalar.activation(ei_shift[:, d.slot], ei[:, d.slot], ACT.Copy, scale=keep[:]).then_inc(ac_sh, 1)
                    copy_in(Step(0, 0, NY))
                    sweep(act, YSTEPS, YPEEL, NY, body, YTAIL)

                @block.vector
                def _(dve):
                    dve.wait_ge(y_pad, 1)

                    def body(s):
                        b, w, v, x, d, g = (s.back(k, G) for k in range(1, 7))
                        if w:
                            dve.wait_ge(ac_kv, w.n + 1)
                            need(dve, po_d4, w.n - NY + 1)
                            nc.vector.tensor_tensor_scan(line(pp, w), w_pad[:].rearrange("p k j s -> p (k j s)"),
                                                         line(kp, w), NEG, ALU.add, ALU.max).then_inc(dv_pp, 1)
                        if v:
                            dve.wait_ge(ac_e1b, v.n + 1)
                            dve.wait_ge(ac_e2b, v.n + 1)
                            need(dve, po_num, v.n - NY + 1)
                            nc.vector.tensor_tensor_scan(line(bb, v), line(e1b, v), line(e2b, v), 0.0, ALU.mult, ALU.add)
                            dve.wait_ge(po_ev, v.n + 1)
                            nc.vector.tensor_tensor_scan(line(aa, v), line(e1b, v), line(evb, v), 0.0, ALU.mult,
                                                         ALU.add).then_inc(dv_scan, 1)
                        if d:
                            dve.wait_ge(po_r3, d.n + 1)
                            need(dve, po_ei, d.n - NY + 1)
                            nc.vector.tensor_scalar(z3[:, d.slot], a_x2[:, d.n], mv3[:, d.slot, 0:1], rs3[:, d.slot],
                                                    ALU.subtract, ALU.mult).then_inc(dv_z3, 1)
                        if w:
                            dve.drain()
                            need(dve, ac_e1b, w.n - NY + 1)
                            nc.vector.tensor_tensor(seqs(d1, w), before(pp, w), body_of(pp, w), ALU.subtract).then_inc(dv_d1, 1)
                            for k in range(KD):
                                last = nc.vector.scalar_tensor_tensor(
                                    qq[:, w.slot, k * P:(k + 1) * P].rearrange("p (j s) -> p j s", s=S),
                                    kp[:, w.slot, k, :, 1:SP1], u_c[:, k:k + 1], pp[:, w.slot, k, :, 0:S], ALU.add, ALU.max)
                            last.then_inc(dv_qq, 1)
                            dve.drain()
                            need(dve, ac_e1, w.n - NY + 1)
                            nc.vector.tensor_tensor(seqs(d3, w), before(pp, w), seqs(qq, w), ALU.subtract).then_inc(dv_d3, 1)
                        if v:
                            dve.wait_ge(po_e1b, v.n + 1)
                            dve.wait_ge(ac_e2, v.n + 1)
                            nc.vector.tensor_tensor(e1bb[:, v.slot], e1bb[:, v.slot], e2[:, v.slot], ALU.add)
                            dve.drain()
                            dve.wait_ge(ac_r, v.n + 1)
                            nc.vector.scalar_tensor_tensor(e1bb[:, v.slot], er[:, v.slot], 1.0, e1bb[:, v.slot], ALU.add, ALU.mult)
                            dve.drain()
                            nc.vector.reciprocal(e1bb[:, v.slot], e1bb[:, v.slot])
                        if b:
                            dve.wait_ge(pe_r, b.n + 1)
                            need(dve, ac_r, b.n - NY + 1)
                            nc.vector.tensor_scalar(r_lim[:, b.slot], bR[:, 0:KD * P], -R_LOW, None, ALU.max).then_inc(dv_r, 1)
                        if x:
                            dve.wait_ge(pe_x, x.n + 1)
                            nc.vector.tensor_tensor(a_x2[:, x.n], bX[:, 0:D], a_x2[:, x.n], ALU.add).then_inc(dv_x2, 1)
                        if v or x:
                            dve.drain()
                        if v:
                            dve.wait_ge(po_num, v.n + 1)
                            need(dve, pe_x, v.n - NY + 1)
                            nc.vector.tensor_tensor(rw[:, v.slot], e1a[:, v.slot], e1bb[:, v.slot], ALU.mult).then_inc(dv_rw, 1)
                        if x:
                            nc.vector.bn_stats(st3[:, x.slot], a_x2[:, x.n])
                        if g:
                            dve.wait_ge(pe_l, g.n + 1)
                            nc.vector.tensor_copy(logits[:, g.n], bL[:, 0:E]).then_inc(dv_lg, 1)
                        if x:
                            dve.drain()
                            nc.vector.bn_aggr(mv3[:, x.slot], st3[:, x.slot])
                            dve.drain()
                            need(dve, po_r3, x.n - NY + 1)
                            nc.vector.tensor_scalar(var3[:, x.slot], mv3[:, x.slot, 1:2], EPS, None, ALU.add).then_inc(dv_var, 1)
                    sweep(dve, YSTEPS, YPEEL, NY, body, YTAIL)


        def routing(tag, choices, tiles, scores_in, softmax, table, tile_expert, slot_of, weights, pool_work=None, unit=None):
            with ExitStack() as rs:
                def rb(name, shape, dt=F32):
                    return sb(tag + name, shape, dt, rs)
                tile_id = iota_t[:, 0:tiles]
                mx, total = rb("mx", [P, G]), rb("total", [P, G])
                pr = rb("pr", [P, G, E])
                top, at = rb("top", [P, G, 8]), rb("at", [P, G, 8], U32)
                at_f = rb("at_f", [P, choices, G])
                hot = rb("hot", [P, choices, G, E])
                mask = rb("mask", [P, G, E], BF16)
                tot_ec, run_ec, pos = rb("tot_ec", [P, E, G]), rb("run_ec", [P, E, G]), rb("pos", [P, G, E])
                cmp_eg = rb("cmp_eg", [P, E, G])
                n_tiles, t_end, base = rb("n_tiles", [P, E]), rb("t_end", [P, E]), rb("base", [P, E])
                cmp_te = rb("cmp_te", [P, tiles, E])
                te_f = rb("te_f", [P, tiles])
                prod = rb("prod", [P, choices, G, E])
                slot_f, slot_i = rb("slot_f", [P, choices, G]), rb("slot_i", [P, choices, G], I32)
                q_i, r_i = rb("q_i", [P, choices, G], I32), rb("r_i", [P, choices, G], I32)
                q_f, r_f = rb("q_f", [P, choices, G], BF16), rb("r_f", [P, choices, G], BF16)
                hot_r = rb("hot_r", [P, choices, G, P], BF16)
                hot_q = rb("hot_q", [P, choices, G, tiles], BF16)
                hot_cp = rb("hot_cp", [P, choices, G, 2, tiles], BF16)
                table_p = rb("table_p", [P, tiles])
                bC, bTab = banks[0], banks[7]
                s_mask, s_cnt, s_hot, s_tab = (sem(tag + n) for n in ("mask", "cnt", "hot", "tab"))
                if softmax:
                    s_sub, s_exp = sem(tag + "sub"), sem(tag + "exp")
                with nc.Block() as block:
                    if pool_work:
                        @block.gpsimd
                        def _(pool):
                            pool_work()

                    @block.scalar
                    def _(act):
                        if unit:
                            unit.gelus(act, 0)
                        if softmax:
                            act.wait_ge(s_sub, 1)
                            nc.scalar.activation(pr[:], pr[:], ACT.Exp).then_inc(s_exp, 1)

                    @block.tensor
                    def _(pe):
                        pe.wait_ge(s_mask, 1)
                        m = mask[:].rearrange("p c e -> p (c e)")
                        nc.tensor.matmul(bC[:, 0:G * E], before_m[:], m, start=True, stop=True)
                        nc.tensor.matmul(bC[:, G * E:2 * G * E], ones_m[:], m, start=True, stop=True).then_inc(s_cnt, 1)
                        if unit:
                            unit.hidden(pe, 0, zT_c[:, 0], ws12)
                        for k in range(choices):
                            pe.wait_ge(s_hot, k + 1)
                            for c in range(G):
                                last = nc.tensor.matmul(bTab[:, 0:2 * tiles], hot_r[:, k, c],
                                                        hot_cp[:, k, c].rearrange("p a t -> p (a t)"),
                                                        start=k == 0 and c == 0, stop=k == choices - 1 and c == G - 1)
                        last.then_inc(s_tab, 1)
                        if unit:
                            unit.down(pe, 0, 0, ws3)

                    @block.vector
                    def _(dve):
                        def step(ins):
                            dve.drain()
                            return ins

                        def tt(o, a, b, op):
                            return step(nc.vector.tensor_tensor(o, a, b, op))

                        def over_e(v):
                            return v.unsqueeze(2).to_broadcast([P, G, E])

                        def over_g(v):
                            return v.unsqueeze(2).to_broadcast([P, E, G])
                        dve.wait_ge(rt_consts, 13)
                        src = scores_in
                        if softmax:
                            step(nc.vector.reduce_max(mx[:], scores_in[:], AX))
                            nc.vector.tensor_tensor(pr[:], scores_in[:], over_e(mx[:]), ALU.subtract).then_inc(s_sub, 1)
                            dve.wait_ge(s_exp, 1)
                            step(nc.vector.reduce_sum(total[:], pr[:], AX))
                            step(nc.vector.reciprocal(total[:], total[:]))
                            tt(pr[:], pr[:], over_e(total[:]), ALU.mult)
                            src = pr
                        for c in range(G):
                            nc.vector.max(top[:, c], src[:, c])
                        dve.drain()
                        for c in range(G):
                            nc.vector.max_index(at[:, c], top[:, c], src[:, c])
                        dve.drain()
                        if weights is not None:
                            tt(total[:], top[:, :, 0], top[:, :, 1], ALU.add)
                            step(nc.vector.reciprocal(total[:], total[:]))
                            for k in range(choices):
                                nc.vector.tensor_tensor(weights[:, k], top[:, :, k], total[:], ALU.mult)
                        step(nc.vector.tensor_copy(at_f[:], at[:, :, 0:choices].rearrange("p g k -> p k g")))
                        tt(hot[:].rearrange("p k g e -> p (k g) e"),
                           iota_e[:].unsqueeze(1).to_broadcast([P, choices * G, E]),
                           at_f[:].rearrange("p k g -> p (k g)").unsqueeze(2).to_broadcast([P, choices * G, E]), ALU.is_equal)
                        if choices == 2:
                            nc.vector.tensor_tensor(mask[:], hot[:, 0], hot[:, 1], ALU.add).then_inc(s_mask, 1)
                        else:
                            nc.vector.tensor_copy(mask[:], hot[:, 0]).then_inc(s_mask, 1)
                        dve.wait_ge(s_cnt, 1)
                        step(nc.vector.tensor_copy(tot_ec[:], bC[:, G * E:2 * G * E].rearrange("p (c e) -> p e c", e=E)))
                        step(nc.vector.tensor_tensor_scan(run_ec[:].rearrange("p e c -> p (e c)"),
                                                          chunk_on[:].rearrange("p e c -> p (e c)"),
                                                          tot_ec[:].rearrange("p e c -> p (e c)"), 0.0, ALU.mult, ALU.add))
                        tt(cmp_eg[:], over_g(run_ec[:, :, G - 1]), tile_lo[:].unsqueeze(1).to_broadcast([P, E, G]), ALU.is_gt)
                        step(nc.vector.reduce_sum(n_tiles[:], cmp_eg[:], AX))
                        step(nc.vector.tensor_tensor_scan(t_end[:], ones_e[:], n_tiles[:], 0.0, ALU.mult, ALU.add))
                        tt(base[:], t_end[:], n_tiles[:], ALU.subtract)
                        step(nc.vector.tensor_scalar(base[:], base[:], float(P), None, ALU.mult))
                        tt(run_ec[:], run_ec[:], tot_ec[:], ALU.subtract)
                        tt(run_ec[:], run_ec[:], over_g(base[:]), ALU.add)
                        tt(pos[:], bC[:, 0:G * E].rearrange("p (c e) -> p c e", e=E),
                           run_ec[:].rearrange("p e c -> p c e"), ALU.add)
                        tt(cmp_te[:], t_end[:].unsqueeze(1).to_broadcast([P, tiles, E]),
                           tile_id.unsqueeze(2).to_broadcast([P, tiles, E]), ALU.is_le)
                        for k in range(choices):
                            nc.vector.tensor_tensor(prod[:, k], hot[:, k], pos[:], ALU.mult)
                        step(nc.vector.reduce_sum(te_f[:], cmp_te[:], AX))
                        nc.vector.tensor_scalar(tile_expert[:], te_f[:], float(E - 1), None, ALU.min)
                        step(nc.vector.reduce_sum(slot_f[:].rearrange("p k g -> p (k g)"),
                                                  prod[:].rearrange("p k g e -> p (k g) e"), AX))
                        step(nc.vector.tensor_copy(slot_i[:], slot_f[:]))
                        nc.vector.tensor_copy(slot_of[:], slot_f[:])
                        nc.vector.tensor_scalar(q_i[:], slot_i[:], 7, None, ALU.logical_shift_right)
                        step(nc.vector.tensor_scalar(r_i[:], slot_i[:], P - 1, None, ALU.bitwise_and))
                        nc.vector.tensor_copy(q_f[:], q_i[:])
                        step(nc.vector.tensor_copy(r_f[:], r_i[:]))
                        if unit:
                            unit.products(dve, 0, 0)
                        for k in range(choices):
                            nc.vector.tensor_tensor(hot_q[:, k], tile_bf[:, 0:tiles].unsqueeze(1).to_broadcast([P, G, tiles]),
                                                    q_f[:, k].unsqueeze(2).to_broadcast([P, G, tiles]), ALU.is_equal)
                        dve.drain()
                        for k in range(choices):
                            nc.vector.tensor_tensor(hot_r[:, k], iota_bf[:].unsqueeze(1).to_broadcast([P, G, P]),
                                                    r_f[:, k].unsqueeze(2).to_broadcast([P, G, P]), ALU.is_equal)
                            nc.vector.tensor_tensor(hot_cp[:, k, :, 0], hot_q[:, k],
                                                    chunk_id[:].unsqueeze(2).to_broadcast([P, G, tiles]), ALU.mult)
                            nc.vector.tensor_scalar(hot_cp[:, k, :, 1], hot_q[:, k], part_id[:], None,
                                                    ALU.mult).then_inc(s_hot, 1)
                        dve.wait_ge(s_tab, 1)
                        step(nc.vector.tensor_copy(table_p[:], bTab[:, tiles:2 * tiles]))
                        nc.vector.scalar_tensor_tensor(table[:], bTab[:, 0:tiles], float(P), table_p[:], ALU.mult, ALU.add)

        def most_tiles(pairs):
            return (pairs - E) // P + E

        table1 = sb("table1", [P, NT1], U32, moe)
        expert1 = sb("expert1", [P, NT1], I32, moe)
        def add_x2():
            for c in range(0, G, 4):
                nc.gpsimd.tensor_tensor(x1[:, c:c + 4], x1[:, c:c + 4], a_x2[:, c:c + 4], ALU.add)
        routing("r1_", 2, NT1, logits, True, table1, expert1, slot1, gate, add_x2)

        ws3 = mixed_w[:].rearrange("p i k h d -> p (i k h d)")[:, 0:HC * D].rearrange("p (f d) -> p f d", d=D)
        ld_s = sem("ld_s")

        rows_y = nc.dram_tensor("rows_y", [NT1 * P, D], F32).ap()
        with ExitStack() as ms:
            NM = 3

            def mb(name, shape, dt=F32):
                return sb(name, shape, dt, ms)
            pick = mb("pick", [P, NM, 1], U32)
            pair = mb("pair", [P, NM, 2 * D])
            mu_e = mb("mu_e", [P, NM, 2, KD])
            wk_e = mb("wk_e", [P, NM, KD, FK])
            prevT, diffT = mb("prevT", [P, NM, KD, P]), mb("diffT", [P, NM, KD, P])
            xk, xr = mb("xk", [P, NM, KD, P]), mb("xr", [P, NM, KD, P])
            h_relu = mb("h_relu", [P, NM, FK])
            hT = mb("hT", [P, NM, FKC, P])
            sig = mb("sig", [P, NM, D])
            y = mb("y", [P, NM, D])
            bA, bR, bH, bY = banks[0:4]
            (pe_a, pe_r, pe_h, pe_y, ac_p, ac_sig, ac_relu, dv_d, dv_x, dv_sq, dv_y, po_mu, ac_wk) = (
                sem("m_" + n) for n in ("pe_a pe_r pe_h pe_y ac_p ac_sig ac_relu dv_d dv_x dv_sq dv_y "
                                        "po_mu ac_wk").split())
            got = [sem(f"m_got{i}") for i in range(NM)]
            put = [sem(f"m_put{i}") for i in range(NM)]
            MSTEPS = NT1 + 2

            with nc.Block() as block:
                @block.gpsimd
                def _(pool):
                    pool.wait_ge(ld_moe[3], 16 * 2 * E)

                    def body(s):
                        need(pool, pe_a, s.n - NM + 1)
                        nc.gpsimd.tensor_copy(pick[:, s.slot], table1[:, bass.ds(s.n, 1)]).then_inc(picked, 1)
                        wait_picked(pool, 0, s)
                        nc.gpsimd.indirect_dma_start(out=pair[:, s.slot], out_offset=None, in_=rows_e[0:TOK, :],
                                                     in_offset=bass.IndirectOffsetOnAxis(ap=pick[:, s.slot], axis=0)
                                                     ).then_inc(got[s.slot], 16)
                        e = pool.value_load(expert1[0:1, bass.ds(s.n, 1)], min_val=0, max_val=E - 1)
                        need(pool, dv_x, s.n - NM + 1)
                        nc.gpsimd.tensor_copy(mu_e[:, s.slot], cm_mu[:, :, e]).then_inc(po_mu, 1)
                    sweep(pool, NT1, NM, NM, body, 0)

                @block.tensor
                def _(pe):
                    for i in range(3):
                        pe.wait_ge(ld_moe[i], 16)

                    def body(s):
                        a, b, d = (s.back(k, NT1) for k in range(3))
                        if a:
                            pe.wait_ge(got[a.slot], a.lap * 16 + 16)
                            need(pe, dv_d, a.n)
                            for q in range(2 * KD):
                                last = nc.tensor.transpose(bA[:, q * P:(q + 1) * P], pair[:, a.slot, q * P:(q + 1) * P], ident[:])
                            last.then_inc(pe_a, 1)
                        if b:
                            pe.wait_ge(dv_x, b.n + 1)
                            pe.wait_ge(ac_wk, b.n + 1)
                            need(pe, dv_sq, b.n)
                            for f in range(FKC):
                                for k in range(KD):
                                    last = nc.tensor.matmul(bH[:, f * P:(f + 1) * P], wk_e[:, b.slot, k, f * P:(f + 1) * P],
                                                            xk[:, b.slot, k], start=k == 0, stop=k == KD - 1)
                            last.then_inc(pe_h, 1)
                            e = pe.value_load(expert1[0:1, bass.ds(b.n, 1)], min_val=0, max_val=E - 1)
                            need(pe, ac_sig, b.n)
                            for k in range(KD):
                                last = nc.tensor.matmul(bR[:, 0:D], xr[:, b.slot, k], ewr_sb[:, e, k], start=k == 0, stop=k == KD - 1)
                            last.then_inc(pe_r, 1)
                        if d:
                            e = pe.value_load(expert1[0:1, bass.ds(d.n, 1)], min_val=0, max_val=E - 1)
                            pe.wait_ge(dv_sq, d.n + 1)
                            need(pe, dv_y, d.n)
                            for f in range(FKC):
                                last = nc.tensor.matmul(bY[:, 0:D], hT[:, d.slot, f], ewv_sb[:, e, f], start=f == 0, stop=f == FKC - 1)
                            last.then_inc(pe_y, 1)
                    sweep(pe, MSTEPS, 6, NM, body, 2)

                @block.scalar
                def _(act):
                    act.wait_ge(ld_moe[0], 16)

                    def body(s):
                        a, b = s.back(0, NT1), s.back(1, NT1)
                        if a:
                            act.wait_ge(pe_a, a.n + 1)
                            need(act, dv_x, a.n - NM + 1)
                            nc.scalar.activation(prevT[:, a.slot].rearrange("p k t -> p (k t)"), bA[:, 0:KD * P],
                                                 ACT.Copy).then_inc(ac_p, 1)
                            e = act.value_load(expert1[0:1, bass.ds(a.n, 1)], min_val=0, max_val=E - 1)
                            need(act, pe_h, a.n - NM + 1)
                            nc.scalar.activation(wk_e[:, a.slot], ewk_sb[:, e], ACT.Copy).then_inc(ac_wk, 1)
                        if b:
                            act.wait_ge(pe_h, b.n + 1)
                            need(act, dv_sq, b.n - NM + 1)
                            nc.scalar.activation(h_relu[:, b.slot], bH[:], ACT.Relu).then_inc(ac_relu, 1)
                            act.wait_ge(pe_r, b.n + 1)
                            need(act, dv_y, b.n - NM + 1)
                            nc.scalar.activation(sig[:, b.slot], bR[:, 0:D], ACT.Sigmoid).then_inc(ac_sig, 1)
                    sweep(act, MSTEPS, 6, NM, body, 2)

                @block.vector
                def _(dve):
                    def body(s):
                        a, b, d = (s.back(k, NT1) for k in range(3))
                        if a:
                            dve.wait_ge(ac_p, a.n + 1)
                            nc.vector.tensor_tensor(diffT[:, a.slot].rearrange("p k t -> p (k t)"), bA[:, KD * P:],
                                                    prevT[:, a.slot].rearrange("p k t -> p (k t)"), ALU.subtract).then_inc(dv_d, 1)
                            dve.drain()
                            dve.wait_ge(po_mu, a.n + 1)
                            need(dve, pe_r, a.n - NM + 1)
                            for i, o in enumerate((xk, xr)):
                                for k in range(KD):
                                    last = nc.vector.scalar_tensor_tensor(o[:, a.slot, k], diffT[:, a.slot, k],
                                                                          mu_e[:, a.slot, i, k:k + 1], prevT[:, a.slot, k],
                                                                          ALU.mult, ALU.add)
                            last.then_inc(dv_x, 1)
                        if b:
                            dve.wait_ge(ac_relu, b.n + 1)
                            need(dve, pe_y, b.n - NM + 1)
                            nc.vector.tensor_tensor(hT[:, b.slot].rearrange("p f t -> p (f t)"), bH[:], h_relu[:, b.slot], ALU.mult).then_inc(dv_sq, 1)
                        if d:
                            dve.wait_ge(pe_y, d.n + 1)
                            dve.wait_ge(ac_sig, d.n + 1)
                            need(dve, put[d.slot], d.lap * 16)
                            nc.vector.tensor_tensor(y[:, d.slot], bY[:, 0:D], sig[:, d.slot], ALU.mult).then_inc(dv_y, 1)
                    sweep(dve, MSTEPS, 6, NM, body, 2)

                @block.sync
                def _(sp):
                    shared_loads = [(ws12[:, i], w.rearrange("(k p) h -> p k h", p=P)) for i, w in enumerate((w1s, w2s))]
                    shared_loads.append((ws3, w3s.rearrange("(f p) d -> p f d", p=P)))
                    sp.dma_start(r2_w[:], Wg.rearrange("(k p) e -> p k e", p=P)).then_inc(ld_s, 16)

                    def body(s):
                        if isinstance(s.n, int) and s.n < 3:
                            sp.dma_start(*shared_loads[s.n]).then_inc(ld_s, 16)
                        sp.wait_ge(dv_y, s.n + 1)
                        sp.dma_start(rows_y[bass.ds(s.n * P, P), :], y[:, s.slot]).then_inc(put[s.slot], 16)
                    sweep(sp, NT1, NM, NM, body, 0)
                    for i in range(NM):
                        sp.wait_ge(put[i], NT1 // NM * 16)
            assert NT1 % NM == 0

        moe.close()

        KEPT = 4
        SHARED_C = G - KEPT
        NT2 = most_tiles(TOK)
        HH = HC // 2
        rows_z = nc.dram_tensor("rows_z", [TOK, D], F32).ap()
        rows_f = nc.dram_tensor("rows_f", [NT2 * P, D], F32).ap()
        table2 = sb("table2", [P, NT2], U32)
        expert2 = sb("expert2", [P, NT2], I32)
        slot2 = sb("slot2", [P, 1, G], U32)
        zT_c = sb("zT_c", [P, KEPT, KD, P])
        act_g = sb("act_g", [P, 2, HH * P])
        hT = sb("hT_f", [P, 2, HC, P])
        bZ, bU, bG, bY, bL = banks[0], banks[1:3], banks[3:5], banks[5:7], banks[7]

        c_got = [sem(f"c_got{i}") for i in range(KEPT)]

        class Geglu:

            def __init__(self, tag):
                self.pe_u, self.pe_g, self.pe_y, self.ac_g, self.dv_h, self.dv_y = (
                    sem(tag + n) for n in ("pe_u", "pe_g", "pe_y", "ac_g", "dv_h", "dv_y"))

            def hidden(self, pe, u, zT, w12):
                for half in range(2):
                    for i, (bank, done, free) in enumerate(((bU, self.pe_u, self.ac_g), (bG, self.pe_g, self.dv_h))):
                        need(pe, free, u * 2 + half - 1)
                        for f in range(HH):
                            col0 = (half * HH + f) * P
                            for k in range(KD):
                                last = nc.tensor.matmul(bank[half][:, f * P:(f + 1) * P],
                                                        w12[:, i, k, col0:col0 + P], zT[:, k],
                                                        start=k == 0, stop=k == KD - 1)
                        last.then_inc(done, 1)

            def gelus(self, act, u):
                for half in range(2):
                    act.wait_ge(self.pe_u, u * 2 + half + 1)
                    need(act, self.dv_h, u * 2 + half - 1)
                    nc.scalar.activation(act_g[:, half], bU[half][:], ACT.Gelu).then_inc(self.ac_g, 1)

            def products(self, dve, u, parity):
                for half in range(2):
                    dve.wait_ge(self.ac_g, u * 2 + half + 1)
                    dve.wait_ge(self.pe_g, u * 2 + half + 1)
                    if half == 0:
                        need(dve, self.pe_y, u - 1)
                    nc.vector.tensor_tensor(hT[:, parity, half * HH:(half + 1) * HH].rearrange("p f t -> p (f t)"),
                                            bG[half][:], act_g[:, half], ALU.mult).then_inc(self.dv_h, 1)

            def down(self, pe, u, parity, w3):
                pe.wait_ge(self.dv_h, u * 2 + 2)
                need(pe, self.dv_y, u - 1)
                for f in range(HC):
                    last = nc.tensor.matmul(bY[parity][:, 0:D], hT[:, parity, f], w3[:, f], start=f == 0, stop=f == HC - 1)
                last.then_inc(self.pe_y, 1)

            def add_shared(self, dve, u, parity, chunk):
                dve.wait_ge(self.pe_y, u + 1)
                nc.vector.tensor_tensor(xz[:, chunk], bY[parity][:, 0:D], xz[:, chunk], ALU.add).then_inc(self.dv_y, 1)

        with ExitStack() as cs:
            NC = KEPT

            def cb(name, shape, dt=F32):
                return sb(name, shape, dt, cs)
            pick = cb("pick_c", [P, NC, 2], U32)
            ya, yb2 = cb("ya", [P, NC, D]), cb("yb2", [P, NC, D])
            z4 = cb("z4", [P, NC, D])
            st4, mv4, var4, rs4 = (cb(n, [P, NC, w]) for n, w in (("st4", 6), ("mv4", 2), ("var4", 1), ("rs4", 1)))
            pe_z, pe_l, ac_z, dv_x, dv_var, dv_z, dv_l, po_r = (sem("c_" + n) for n in (
                "pe_z pe_l ac_z dv_x dv_var dv_z dv_l po_r").split())
            ge = Geglu("c_")
            got = c_got
            put = [sem(f"c_put{i}") for i in range(NC)]
            CSTEPS, CPEEL, CTAIL = G + 2, 5, 5
            with nc.Block() as block:
                @block.sync
                def _(sp):
                    def body(s):
                        sp.wait_ge(dv_z, s.n + 1)
                        sp.dma_start(rows_z[bass.ds(s.n * P, P), :], z4[:, s.slot]).then_inc(put[s.slot], 16)
                    sweep(sp, G, NC, NC, body, 0)
                    for i in range(NC):
                        sp.wait_ge(put[i], G // NC * 16)

                @block.gpsimd
                def _(pool):
                    def body(s):
                        a, b = s.back(0, G), s.back(1, G)
                        if a:
                            need(pool, dv_x, a.n - NC + 1)
                            nc.gpsimd.tensor_copy(pick[:, a.slot], slot1[:, :, a.n]).then_inc(picked, 1)
                            wait_picked(pool, NT1, a)
                            for k, t in enumerate((ya, yb2)):
                                nc.gpsimd.indirect_dma_start(out=t[:, a.slot], out_offset=None, in_=rows_y[:, :],
                                                             in_offset=bass.IndirectOffsetOnAxis(ap=pick[:, a.slot, k:k + 1], axis=0)
                                                             ).then_inc(got[a.slot], 16)
                        if b:
                            pool.wait_ge(dv_var, b.n + 1)
                            nc.gpsimd.tensor_tensor(rs4[:, b.slot], var4[:, b.slot], eps_pow[:], ALU.pow).then_inc(po_r, 1)
                    sweep(pool, CSTEPS, CPEEL, NC, body, 2)

                @block.tensor
                def _(pe):
                    pe.wait_ge(ld_s, 16 * 4)

                    def body(s):
                        a, u, v = s.back(0, G), s.back(1, SHARED_C), s.back(2, SHARED_C)
                        if u:
                            ge.hidden(pe, u.n, zT_c[:, u.slot], ws12)
                        if a:
                            pe.wait_ge(dv_z, a.n + 1)
                            need(pe, ac_z, a.n)
                            for k in range(KD):
                                last = nc.tensor.transpose(bZ[:, k * P:(k + 1) * P], z4[:, a.slot, k * P:(k + 1) * P], ident[:])
                            last.then_inc(pe_z, 1)
                        if v:
                            ge.down(pe, v.n, v.slot % 2, ws3)
                        if a:
                            pe.wait_ge(ac_z, a.n + 1)
                            need(pe, dv_l, a.n)
                            for k in range(KD):
                                last = nc.tensor.matmul(bL[:, 0:E], zT_c[:, a.slot, k], r2_w[:, k], start=k == 0, stop=k == KD - 1)
                            last.then_inc(pe_l, 1)
                    sweep(pe, CSTEPS, CPEEL, NC, body, CTAIL)

                @block.scalar
                def _(act):
                    def body(s):
                        a, u = s.back(0, G), s.back(1, SHARED_C)
                        if u:
                            ge.gelus(act, u.n)
                        if a:
                            act.wait_ge(pe_z, a.n + 1)
                            need(act, pe_l, a.n - NC + 1)
                            need(act, ge.pe_g, (a.n - NC + 1) * 2)
                            nc.scalar.activation(zT_c[:, a.slot].rearrange("p k t -> p (k t)"), bZ[:, 0:KD * P],
                                                 ACT.Copy).then_inc(ac_z, 1)
                    sweep(act, CSTEPS, CPEEL, NC, body, CTAIL)

                @block.vector
                def _(dve):
                    def body(s):
                        a, b, u, v = s.back(0, G), s.back(1, G), s.back(1, SHARED_C), s.back(3, SHARED_C)
                        if a:
                            dve.wait_ge(got[a.slot], a.lap * 32 + 32)
                            nc.vector.scalar_tensor_tensor(xz[:, a.n], ya[:, a.slot], gate[:, 0, bass.ds(a.n, 1)],
                                                           x1[:, a.n], ALU.mult, ALU.add)
                            dve.drain()
                            nc.vector.scalar_tensor_tensor(xz[:, a.n], yb2[:, a.slot], gate[:, 1, bass.ds(a.n, 1)],
                                                           xz[:, a.n], ALU.mult, ALU.add).then_inc(dv_x, 1)
                            dve.drain()
                            nc.vector.bn_stats(st4[:, a.slot], xz[:, a.n])
                            dve.drain()
                            nc.vector.bn_aggr(mv4[:, a.slot], st4[:, a.slot])
                            dve.drain()
                            need(dve, po_r, a.n - NC + 1)
                            nc.vector.tensor_scalar(var4[:, a.slot], mv4[:, a.slot, 1:2], EPS, None, ALU.add).then_inc(dv_var, 1)
                        if v:
                            ge.add_shared(dve, v.n, v.slot % 2, v.n)
                        if a:
                            dve.wait_ge(po_r, a.n + 1)
                            need(dve, pe_z, a.n - NC + 1)
                            need(dve, put[a.slot], a.lap * 16)
                            nc.vector.tensor_scalar(z4[:, a.slot], xz[:, a.n], mv4[:, a.slot, 0:1], rs4[:, a.slot],
                                                    ALU.subtract, ALU.mult).then_inc(dv_z, 1)
                        if u:
                            ge.products(dve, u.n, u.slot % 2)
                        if b:
                            dve.wait_ge(pe_l, b.n + 1)
                            nc.vector.tensor_copy(logits2[:, b.n], bL[:, 0:E]).then_inc(dv_l, 1)
                    sweep(dve, CSTEPS, CPEEL, NC, body, CTAIL)

        ge = Geglu("f_")
        routing("r2_", 1, NT2, logits2, False, table2, expert2, slot2, None, None, ge)
        with ExitStack() as fs:
            NF = 2
            NG = 4
            NZ = 4
            got_r, GOT0 = c_got, G // KEPT * 32
            assert NZ == KEPT and NZ % NF == 0

            def fb(name, shape, dt=F32):
                return sb(name, shape, dt, fs)
            we12 = fb("we12", [P, NF, 2, KD, H])
            we3 = fb("we3", [P, NF, HC, D])
            pick = fb("pick_f", [P, NZ, 1], U32)
            zr = fb("zr", [P, NZ, D])
            zT = fb("zT_f", [P, NF, KD, P])
            yr = fb("yr", [P, NF, D])
            yg = x1
            pe_z, ac_z, e_sum, e_out = (sem("f_" + n) for n in "pe_z ac_z e_sum e_out".split())
            got_w12 = [sem(f"f_got_w12{i}") for i in range(NF)]
            got_w3 = [sem(f"f_got_w3{i}") for i in range(NF)]
            got_g = [sem(f"f_got_g{i}") for i in range(NG)]
            put = [sem(f"f_put{i}") for i in range(NF)]
            FIRST = G - KEPT
            LAST = FIRST + 2
            FPEEL, FTAIL = 5, 2

            def unit_r(s):
                return s.n + 2, s.offset % 2

            def weights_of(s):
                return s.slot % NF, s.lap * (NZ // NF) + s.slot // NF

            def unit_s(chunk):
                u = chunk - FIRST + (0 if chunk < LAST else NT2)
                return u, u % 2

            with nc.Block() as block:
                @block.sync
                def _(sp):
                    def load_w12(s):
                        e = sp.value_load(expert2[0:1, bass.ds(s.n, 1)], min_val=0, max_val=E - 1)
                        p = s.back(NF, NT2)
                        if p:
                            sp.wait_ge(ge.pe_g, unit_r(p)[0] * 2 + 2)
                        for i, w in enumerate((W1, W2)):
                            sp.dma_start(we12[:, weights_of(s)[0], i],
                                         w[e].rearrange("(k p) h -> p k h", p=P)).then_inc(got_w12[weights_of(s)[0]], 16)

                    def load_w3(s):
                        e = sp.value_load(expert2[0:1, bass.ds(s.n, 1)], min_val=0, max_val=E - 1)
                        p = s.back(NF, NT2)
                        if p:
                            sp.wait_ge(ge.pe_y, unit_r(p)[0] + 1)
                        sp.dma_start(we3[:, weights_of(s)[0]],
                                     W3[e].rearrange("(f p) d -> p f d", p=P)).then_inc(got_w3[weights_of(s)[0]], 16)

                    def body(s):
                        load_w12(s)
                        if s.back(1, NT2):
                            load_w3(s.back(1, NT2))
                    sweep(sp, NT2, FPEEL, NZ, body, FTAIL)
                    load_w3(Step(0, NT2 - 1, NZ))
                    for c in range(G):
                        sp.wait_ge(e_sum, c + 1)
                        sp.dma_start(out_nat[c], xz[:, c]).then_inc(e_out, 16)
                    sp.wait_ge(e_out, 16 * G)

                @block.gpsimd
                def _(pool):
                    def body(s):
                        need(pool, pe_z, s.n - NZ + 1)
                        nc.gpsimd.tensor_copy(pick[:, s.slot], table2[:, bass.ds(s.n, 1)]).then_inc(picked, 1)
                        wait_picked(pool, NT1 + G, s)
                        nc.gpsimd.indirect_dma_start(out=zr[:, s.slot], out_offset=None, in_=rows_z[:, :],
                                                     in_offset=bass.IndirectOffsetOnAxis(ap=pick[:, s.slot], axis=0)
                                                     ).then_inc(got_r[s.slot], 16)
                    sweep(pool, NT2, FPEEL, NZ, body, FTAIL)
                    for i in range(NF):
                        pool.wait_ge(put[i], (NT2 - i + NF - 1) // NF * 16)
                    for c in range(G):
                        need(pool, e_sum, c - NG + 1)
                        nc.gpsimd.indirect_dma_start(out=yg[:, c], out_offset=None, in_=rows_f[:, :],
                                                     in_offset=bass.IndirectOffsetOnAxis(ap=slot2[:, 0, c:c + 1], axis=0)
                                                     ).then_inc(got_g[c % NG], 16)

                @block.tensor
                def _(pe):
                    def transpose_z(s):
                        need(pe, ac_z, s.n)
                        pe.wait_ge(got_r[s.slot], s.lap * 16 + GOT0 + 16)
                        for k in range(KD):
                            last = nc.tensor.transpose(bZ[:, k * P:(k + 1) * P], zr[:, s.slot, k * P:(k + 1) * P], ident[:])
                        last.then_inc(pe_z, 1)

                    def down_routed(s):
                        w, lap = weights_of(s)
                        pe.wait_ge(got_w3[w], lap * 16 + 16)
                        ge.down(pe, *unit_r(s), we3[:, w])

                    def body(s):
                        before, after = s.back(1, NT2), s.back(-1, NT2)
                        pe.wait_ge(ac_z, s.n + 1)
                        w, lap = weights_of(s)
                        pe.wait_ge(got_w12[w], lap * 32 + 32)
                        ge.hidden(pe, unit_r(s)[0], zT[:, s.offset % 2], we12[:, w])
                        if after:
                            transpose_z(after)
                        if before:
                            down_routed(before)
                    ge.hidden(pe, 1, zT_c[:, 1], ws12)
                    transpose_z(Step(0, 0, NZ))
                    ge.down(pe, 1, 1, ws3)
                    sweep(pe, NT2, FPEEL, NZ, body, FTAIL)
                    for c in range(LAST, G):
                        ge.hidden(pe, unit_s(c)[0], zT_c[:, c - FIRST], ws12)
                        if c == LAST:
                            down_routed(Step(0, NT2 - 1, NZ))
                        else:
                            ge.down(pe, *unit_s(c - 1), ws3)
                    ge.down(pe, *unit_s(G - 1), ws3)

                @block.scalar
                def _(act):
                    def copy_z(s):
                        act.wait_ge(pe_z, s.n + 1)
                        p = s.back(NF, NT2)
                        if p:
                            act.wait_ge(ge.pe_g, unit_r(p)[0] * 2 + 2)
                        nc.scalar.activation(zT[:, s.offset % 2].rearrange("p k t -> p (k t)"), bZ[:, 0:KD * P],
                                             ACT.Copy).then_inc(ac_z, 1)

                    def store(s):
                        act.wait_ge(ge.dv_y, unit_r(s)[0] + 1)
                        act.dma_start(rows_f[bass.ds(s.n * P, P), :], yr[:, s.offset % 2]).then_inc(put[s.offset % 2], 16)

                    def body(s):
                        ge.gelus(act, unit_r(s)[0])
                        if s.back(-1, NT2):
                            copy_z(s.back(-1, NT2))
                        if s.back(1, NT2):
                            store(s.back(1, NT2))
                    ge.gelus(act, 1)
                    copy_z(Step(0, 0, NZ))
                    sweep(act, NT2, FPEEL, NZ, body, FTAIL)
                    for c in range(LAST, G):
                        ge.gelus(act, unit_s(c)[0])
                        if c == LAST:
                            store(Step(0, NT2 - 1, NZ))

                @block.vector
                def _(dve):
                    def take_routed(s):
                        u, parity = unit_r(s)
                        dve.wait_ge(ge.pe_y, u + 1)
                        need(dve, put[s.offset % 2], weights_of(s)[1] * 16)
                        nc.vector.tensor_copy(yr[:, s.offset % 2], bY[parity][:, 0:D]).then_inc(ge.dv_y, 1)

                    def body(s):
                        ge.products(dve, *unit_r(s))
                        if s.back(1, NT2):
                            take_routed(s.back(1, NT2))

                    def finish(chunks):
                        dve.drain()
                        for c in chunks:
                            dve.wait_ge(got_g[c % NG], (c // NG + 1) * 16)
                            nc.vector.tensor_tensor(xz[:, c], xz[:, c], yg[:, c], ALU.add).then_inc(e_sum, 1)
                    ge.add_shared(dve, 0, 0, FIRST)
                    ge.products(dve, 1, 1)
                    ge.add_shared(dve, 1, 1, FIRST + 1)
                    sweep(dve, NT2, FPEEL, NZ, body, FTAIL)
                    ge.products(dve, *unit_s(LAST))
                    take_routed(Step(0, NT2 - 1, NZ))
                    finish(range(0, 6))
                    ge.products(dve, *unit_s(LAST + 1))
                    ge.add_shared(dve, *unit_s(LAST), LAST)
                    finish(range(6, G - 2))
                    ge.add_shared(dve, *unit_s(LAST + 1), LAST + 1)
                    finish(range(G - 2, G))


_INS = ['x', 'ctx_1024'] + ['L0_xattn_' + m + n for n in 'qkvo' for m in ('W', 'b', 'A', 'B')] + [
    'L0_attn_' + n for n in ('ln1_g', 'ln1_b', 'ln2_g', 'ln2_b', 'tm_mu_k', 'tm_mu_v', 'tm_mu_r', 'time_decay',
                             'time_first', 'Wk', 'Wv', 'Wr', 'Wo', 'router_w', 'cm_mu_k', 'cm_mu_r', 'eWk', 'eWv',
                             'eWr')] + ['L0_ffn_' + n for n in ('w1s', 'w2s', 'w3s', 'W1', 'W2', 'W3', 'Wg')]


def kernel(**inputs):
    import numpy as _np
    import concourse.bacc as _bacc
    from concourse import mybir as _mybir
    from concourse.bass_utils import run_bass_kernel_spmd as _run

    nc = _bacc.Bacc("TRN2", target_bir_lowering=False, num_devices=1)
    arrays, args = {}, []
    for name in _INS:
        a = _np.ascontiguousarray(inputs[name])
        arrays[f"in_{name}_dram"] = a
        args.append(nc.dram_tensor(f"in_{name}_dram", a.shape, _mybir.dt.from_np(a.dtype), kind="ExternalInput").ap())
    shape = inputs['x'].shape
    args.append(nc.dram_tensor("out_0_dram", shape, _mybir.dt.float32, kind="ExternalOutput").ap())
    perceiver_block(nc, *args)
    r = _run(nc, [arrays], core_ids=[0])
    return r.results[0]["out_0_dram"]
```
